# Optimizing a Trainium2 kernel written in Bass

```python
import numpy as np
import jax
import jax.numpy as jnp

def _softmax(x, axis=-1):
    return jax.nn.softmax(x, axis=axis)

def _gelu(x):
    return jax.nn.gelu(x, approximate=True)

def _silu(x):
    return jax.nn.silu(x)

def _sigmoid(x):
    return jax.nn.sigmoid(x)

def _layernorm(x, axis=-1, eps=1e-05):
    m = jnp.mean(x, axis=axis, keepdims=True)
    v = jnp.var(x, axis=axis, keepdims=True)
    return (x - m) / jnp.sqrt(v + eps)

def _scatter_add(tgt, idx, src, axis=0):
    return tgt.at[idx].add(src)

def _segment_sum(src, seg, n):
    return jax.ops.segment_sum(src, seg, n)
kernel_name = 'mk_flamingo_gated_d2_seqx_r8_61f12f'

def setup_inputs(seed: int=0):
    np.random.seed(seed)
    _w = jnp.asarray

    def _rec_inputs():
        import jax
        import jax.numpy as jnp
        _rk = jax.random.key(seed)
        x = -0.0002928 + 1 * jax.random.normal(jax.random.fold_in(_rk, 1), (32, 64, 256), jnp.float32)
        _lenS = 64 - jax.random.randint(jax.random.fold_in(_rk, 7), (32,), 0, max(1, 64 // 4) + 1, jnp.int32)
        _lenS2 = 64 - jax.random.randint(jax.random.fold_in(_rk, 8), (32,), 0, max(1, 64 // 4) + 1, jnp.int32)
        _ctx_2048P = jax.random.normal(jax.random.fold_in(_rk, 11), (32, 16, 256), jnp.float32)
        _ctx_2048c = jax.random.dirichlet(jax.random.fold_in(_rk, 511), 0.3 * jnp.ones((16,), jnp.float32), (32, 64))
        _ctx_2048t = jnp.einsum('bsk,bkd->bsd', _ctx_2048c, _ctx_2048P)
        _ctx_2048t = _ctx_2048t * jax.lax.rsqrt(jnp.mean(jnp.square(_ctx_2048t)) + 1e-12) * 0.953939
        ctx_2048 = -1.39393e-06 + 0.999914 * (_ctx_2048t + 0.3 * jax.random.normal(jax.random.fold_in(_rk, 611), (32, 64, 256), jnp.float32))
        itok_BxS_0_1023 = jax.random.randint(jax.random.fold_in(_rk, 12), (32, 64), 0, 128, jnp.int32)
        _g = jax.random.normal(jax.random.fold_in(_rk, 9001), (2, 2), jnp.float32)
        _g = jnp.sign(_g) * jnp.maximum(jnp.abs(_g), 1.0) + (_g == 0) * 1.0
        g_xattn = _g[0]
        g_ffn = _g[1]
        return (x, ctx_2048, itok_BxS_0_1023, g_xattn, g_ffn)
    x, ctx_2048, itok_BxS_0_1023, g_xattn, g_ffn = _rec_inputs()

    def _L0_xattn_setup():
        import jax, jax.numpy as jnp
        import numpy as np
        N_HEADS = 8
        ROPE_BASE = 10000.0

        def _rope(x, d):
            t = x.shape[2]
            theta = 1.0 / ROPE_BASE ** (jnp.arange(0, d, 2, dtype=jnp.float32) / d)
            idx = jnp.arange(t, dtype=jnp.float32)[:, None] * theta[None, :]
            idx2 = jnp.concatenate([idx, idx], axis=-1)
            cos = jnp.cos(idx2)[None, None, :, :]
            sin = jnp.sin(idx2)[None, None, :, :]
            x_rope, x_pass = (x[..., :d], x[..., d:])
            d2 = d // 2
            neg_half = jnp.concatenate([-x_rope[..., d2:], x_rope[..., :d2]], axis=-1)
            x_rope = x_rope * cos + neg_half * sin
            return jnp.concatenate([x_rope, x_pass], axis=-1)

        def _proj(W, b, x):
            return jnp.einsum('oc,bct->bot', W, x) + b[None, :, None]
        key = jax.random.key(seed)
        ks = jax.random.split(key, 12)
        B, CH, T = (4, 64, 256)
        s = 1.0 / np.sqrt(CH)
        return {'x': jax.random.normal(ks[0], (B, CH, T), jnp.float32), 'c': jax.random.normal(ks[1], (B, CH, T), jnp.float32), 'Wq': jax.random.normal(ks[2], (CH, CH), jnp.float32) * s, 'bq': jax.random.normal(ks[3], (CH,), jnp.float32) * 0.01, 'Wk': jax.random.normal(ks[4], (CH, CH), jnp.float32) * s, 'bk': jax.random.normal(ks[5], (CH,), jnp.float32) * 0.01, 'Wv': jax.random.normal(ks[6], (CH, CH), jnp.float32) * s, 'bv': jax.random.normal(ks[7], (CH,), jnp.float32) * 0.01, 'Wo': jax.random.normal(ks[8], (CH, CH), jnp.float32) * s, 'bo': jax.random.normal(ks[9], (CH,), jnp.float32) * 0.01}
    _L0_xattn_all = _L0_xattn_setup()
    _L0_xattn_in = {k: v for k, v in _L0_xattn_all.items() if k in ('Wq', 'bq', 'Wk', 'bk', 'Wv', 'bv', 'Wo', 'bo')}
    del _L0_xattn_all

    def _L0_ffn_setup():
        import jax, jax.numpy as jnp
        import numpy as np
        from jax import lax
        E = 64
        H = 256
        I = 88
        G = 8
        TOPK_GROUP = 4
        K = 8
        B, S = (2, 256)
        N = B * S
        CAP = 2 * N * K // E
        SCALE = 2.5

        def _route(x, router_weight, e_bias):
            logits = x.astype(jnp.float32) @ router_weight.astype(jnp.float32).T
            scores = jax.nn.sigmoid(logits)
            sc = scores + e_bias
            n = x.shape[0]
            group_scores = lax.top_k(sc.reshape(n, G, E // G), 2)[0].sum(-1)
            grp_idx = lax.top_k(group_scores, TOPK_GROUP)[1]
            group_mask = jnp.zeros((n, G), jnp.float32).at[jnp.arange(n)[:, None], grp_idx].set(1.0)
            score_mask = jnp.repeat(group_mask, E // G, axis=1)
            masked = jnp.where(score_mask > 0, sc, 0.0)
            topk_idx = lax.top_k(masked, K)[1]
            topk_w = jnp.take_along_axis(scores, topk_idx, axis=1)
            topk_w = topk_w / (topk_w.sum(-1, keepdims=True) + 1e-20)
            return (topk_idx, topk_w * SCALE)

        def _moe_experts(x, topk_idx, topk_w, w_gate, w_up, w_down):
            n = x.shape[0]
            flat_e = topk_idx.reshape(-1)
            rows = jnp.repeat(jnp.arange(n), K)
            oh = jax.nn.one_hot(flat_e, E, dtype=jnp.int32)
            pos = jnp.cumsum(oh, axis=0) - oh
            pos = jnp.take_along_axis(pos, flat_e[:, None], axis=1)[:, 0]
            valid = (pos < CAP).astype(x.dtype)
            p = jnp.minimum(pos, CAP - 1)
            buf = jnp.zeros((E, CAP, H), x.dtype).at[flat_e, p].add(x[rows] * valid[:, None])
            g = jnp.einsum('ech,ehi->eci', buf, w_gate)
            u = jnp.einsum('ech,ehi->eci', buf, w_up)
            y = jnp.einsum('eci,eih->ech', jax.nn.silu(g) * u, w_down)
            y_tok = y[flat_e, p] * (topk_w.reshape(-1) * valid)[:, None]
            return jnp.zeros((n, H), x.dtype).at[rows].add(y_tok)

        def _shared_mlp(x, sh_gate, sh_up, sh_down):
            return jax.nn.silu(x @ sh_gate) * (x @ sh_up) @ sh_down
        key = jax.random.key(seed)
        ks = jax.random.split(key, 9)
        f32 = jnp.float32
        return {'hidden_states': jax.random.normal(ks[0], (B, S, H), f32), 'router_weight': jax.random.normal(ks[1], (E, H), f32) * (2.0 / H) ** 0.5, 'e_bias': jnp.zeros((E,), f32), 'w_gate': jax.random.normal(ks[2], (E, H, I), f32) * (1.0 / H) ** 0.5, 'w_up': jax.random.normal(ks[3], (E, H, I), f32) * (1.0 / H) ** 0.5, 'w_down': jax.random.normal(ks[4], (E, I, H), f32) * (1.0 / I) ** 0.5, 'sh_gate': jax.random.normal(ks[5], (H, I), f32) * (1.0 / H) ** 0.5, 'sh_up': jax.random.normal(ks[6], (H, I), f32) * (1.0 / H) ** 0.5, 'sh_down': jax.random.normal(ks[7], (I, H), f32) * (1.0 / I) ** 0.5}
    _L0_ffn_all = _L0_ffn_setup()
    _L0_ffn_in = {k: v for k, v in _L0_ffn_all.items() if k in ('router_weight', 'e_bias', 'w_gate', 'w_up', 'w_down', 'sh_gate', 'sh_up', 'sh_down')}
    del _L0_ffn_all

    def _L1_xattn_setup():
        import jax, jax.numpy as jnp
        import numpy as np
        B, Lq, Lk = (2, 512, 128)
        Q_DIM, KV_DIM = (256, 256)
        H, HD = (16, 128)
        KVC, QC, R = (64, 96, 64)
        LOOKBACK = 8
        NEG = -1e+30

        def _rope(x, L):
            half = x.shape[-1] // 2
            inv_freq = 1.0 / 10000.0 ** (jnp.arange(half, dtype=jnp.float32) / half)
            ang = jnp.arange(L, dtype=jnp.float32)[:, None] * inv_freq
            cos, sin = (jnp.cos(ang), jnp.sin(ang))
            x1, x2 = (x[..., :half], x[..., half:])
            return jnp.concatenate([x1 * cos - x2 * sin, x1 * sin + x2 * cos], axis=-1)
        key = jax.random.key(seed)
        ks = jax.random.split(key, 11)

        def w(k, shape, fan_in):
            return jax.random.normal(k, shape, jnp.float32) / np.sqrt(fan_in).astype(np.float32)
        return {'q': jax.random.normal(ks[0], (B, Lq, Q_DIM), jnp.float32), 'kv': jax.random.normal(ks[1], (B, Lk, KV_DIM), jnp.float32), 'seg_id': jnp.sort(jax.random.randint(ks[2], (B, Lq), 0, Lk), axis=-1), 'W_kvc': w(ks[3], (KV_DIM, KVC), KV_DIM), 'W_dq': w(ks[4], (Q_DIM, QC), Q_DIM), 'W_uq': w(ks[5], (QC, H * HD), QC), 'W_qr': w(ks[6], (QC, H * R), QC), 'W_uk': w(ks[7], (KVC, H * HD), KVC), 'W_kr': w(ks[8], (KVC, R), KVC), 'W_uv': w(ks[9], (KVC, H * HD), KVC), 'W_o': w(ks[10], (H * HD, Q_DIM), H * HD)}
    _L1_xattn_all = _L1_xattn_setup()
    _L1_xattn_in = {k: v for k, v in _L1_xattn_all.items() if k in ('W_kvc', 'W_dq', 'W_uq', 'W_qr', 'W_uk', 'W_kr', 'W_uv', 'W_o')}
    del _L1_xattn_all

    def _L1_ffn_setup():
        import jax, jax.numpy as jnp
        import numpy as np
        B, S, H = (4, 512, 256)
        I = 176
        E = 8
        K = 2
        INIT = 0.02
        key = jax.random.key(seed)
        k0, k1, k2, k3, k4, k5 = jax.random.split(key, 6)
        return {'x': jax.random.normal(k0, (B, S, H), dtype=jnp.float32), 'w_shared1': jax.random.normal(k1, (H, I), dtype=jnp.float32) * INIT, 'w_shared2': jax.random.normal(k2, (I, H), dtype=jnp.float32) * INIT, 'w1': jax.random.normal(k3, (E, H, I), dtype=jnp.float32) * INIT, 'w2': jax.random.normal(k4, (E, I, H), dtype=jnp.float32) * INIT, 'w_router': jax.random.normal(k5, (H, E), dtype=jnp.float32) * INIT}
    _L1_ffn_all = _L1_ffn_setup()
    _L1_ffn_in = {k: v for k, v in _L1_ffn_all.items() if k in ('w_shared1', 'w_shared2', 'w1', 'w2', 'w_router')}
    del _L1_ffn_all
    return {'x': x, 'ctx_2048': ctx_2048, 'itok_BxS_0_1023': itok_BxS_0_1023, 'g_xattn': g_xattn, 'g_ffn': g_ffn, 'L0_xattn_Wq': _L0_xattn_in['Wq'], 'L0_xattn_bq': _L0_xattn_in['bq'], 'L0_xattn_Wk': _L0_xattn_in['Wk'], 'L0_xattn_bk': _L0_xattn_in['bk'], 'L0_xattn_Wv': _L0_xattn_in['Wv'], 'L0_xattn_bv': _L0_xattn_in['bv'], 'L0_xattn_Wo': _L0_xattn_in['Wo'], 'L0_xattn_bo': _L0_xattn_in['bo'], 'L0_ffn_router_weight': _L0_ffn_in['router_weight'], 'L0_ffn_e_bias': _L0_ffn_in['e_bias'], 'L0_ffn_w_gate': _L0_ffn_in['w_gate'], 'L0_ffn_w_up': _L0_ffn_in['w_up'], 'L0_ffn_w_down': _L0_ffn_in['w_down'], 'L0_ffn_sh_gate': _L0_ffn_in['sh_gate'], 'L0_ffn_sh_up': _L0_ffn_in['sh_up'], 'L0_ffn_sh_down': _L0_ffn_in['sh_down'], 'L1_xattn_W_kvc': _L1_xattn_in['W_kvc'], 'L1_xattn_W_dq': _L1_xattn_in['W_dq'], 'L1_xattn_W_uq': _L1_xattn_in['W_uq'], 'L1_xattn_W_qr': _L1_xattn_in['W_qr'], 'L1_xattn_W_uk': _L1_xattn_in['W_uk'], 'L1_xattn_W_kr': _L1_xattn_in['W_kr'], 'L1_xattn_W_uv': _L1_xattn_in['W_uv'], 'L1_xattn_W_o': _L1_xattn_in['W_o'], 'L1_ffn_w_shared1': _L1_ffn_in['w_shared1'], 'L1_ffn_w_shared2': _L1_ffn_in['w_shared2'], 'L1_ffn_w1': _L1_ffn_in['w1'], 'L1_ffn_w2': _L1_ffn_in['w2'], 'L1_ffn_w_router': _L1_ffn_in['w_router']}

def reference(x, ctx_2048, itok_BxS_0_1023, g_xattn, g_ffn, L0_xattn_Wq, L0_xattn_bq, L0_xattn_Wk, L0_xattn_bk, L0_xattn_Wv, L0_xattn_bv, L0_xattn_Wo, L0_xattn_bo, L0_ffn_router_weight, L0_ffn_e_bias, L0_ffn_w_gate, L0_ffn_w_up, L0_ffn_w_down, L0_ffn_sh_gate, L0_ffn_sh_up, L0_ffn_sh_down, L1_xattn_W_kvc, L1_xattn_W_dq, L1_xattn_W_uq, L1_xattn_W_qr, L1_xattn_W_uk, L1_xattn_W_kr, L1_xattn_W_uv, L1_xattn_W_o, L1_ffn_w_shared1, L1_ffn_w_shared2, L1_ffn_w1, L1_ffn_w2, L1_ffn_w_router):
    import jax
    import jax.numpy as jnp

    def _L0_xattn_ref(x, c, Wq, bq, Wk, bk, Wv, bv, Wo, bo):
        import jax, jax.numpy as jnp
        import numpy as np
        N_HEADS = 8
        ROPE_BASE = 10000.0

        def _rope(x, d):
            t = x.shape[2]
            theta = 1.0 / ROPE_BASE ** (jnp.arange(0, d, 2, dtype=jnp.float32) / d)
            idx = jnp.arange(t, dtype=jnp.float32)[:, None] * theta[None, :]
            idx2 = jnp.concatenate([idx, idx], axis=-1)
            cos = jnp.cos(idx2)[None, None, :, :]
            sin = jnp.sin(idx2)[None, None, :, :]
            x_rope, x_pass = (x[..., :d], x[..., d:])
            d2 = d // 2
            neg_half = jnp.concatenate([-x_rope[..., d2:], x_rope[..., :d2]], axis=-1)
            x_rope = x_rope * cos + neg_half * sin
            return jnp.concatenate([x_rope, x_pass], axis=-1)

        def _proj(W, b, x):
            return jnp.einsum('oc,bct->bot', W, x) + b[None, :, None]
        b, ch, t_t = x.shape
        t_s = c.shape[2]
        h = N_HEADS
        kc = ch // h
        d_rope = int(kc * 0.5)
        q = _proj(Wq, bq, x)
        k = _proj(Wk, bk, c)
        v = _proj(Wv, bv, c)
        q = q.reshape(b, h, kc, t_t).transpose(0, 1, 3, 2)
        k = k.reshape(b, h, kc, t_s).transpose(0, 1, 3, 2)
        v = v.reshape(b, h, kc, t_s).transpose(0, 1, 3, 2)
        q = _rope(q, d_rope)
        k = _rope(k, d_rope)
        scores = jnp.einsum('bhqd,bhkd->bhqk', q, k) / jnp.sqrt(jnp.float32(kc))
        p_attn = jax.nn.softmax(scores, axis=-1)
        out = jnp.einsum('bhqk,bhkd->bhqd', p_attn, v)
        out = out.transpose(0, 1, 3, 2).reshape(b, ch, t_t)
        return _proj(Wo, bo, out)

    def _L0_ffn_ref(hidden_states, router_weight, e_bias, w_gate, w_up, w_down, sh_gate, sh_up, sh_down):
        import jax, jax.numpy as jnp
        import numpy as np
        from jax import lax
        E = 64
        H = 256
        I = 88
        G = 8
        TOPK_GROUP = 4
        K = 8
        B, S = (2, 256)
        N = B * S
        CAP = 2 * N * K // E
        SCALE = 2.5

        def _route(x, router_weight, e_bias):
            logits = x.astype(jnp.float32) @ router_weight.astype(jnp.float32).T
            scores = jax.nn.sigmoid(logits)
            sc = scores + e_bias
            n = x.shape[0]
            group_scores = lax.top_k(sc.reshape(n, G, E // G), 2)[0].sum(-1)
            grp_idx = lax.top_k(group_scores, TOPK_GROUP)[1]
            group_mask = jnp.zeros((n, G), jnp.float32).at[jnp.arange(n)[:, None], grp_idx].set(1.0)
            score_mask = jnp.repeat(group_mask, E // G, axis=1)
            masked = jnp.where(score_mask > 0, sc, 0.0)
            topk_idx = lax.top_k(masked, K)[1]
            topk_w = jnp.take_along_axis(scores, topk_idx, axis=1)
            topk_w = topk_w / (topk_w.sum(-1, keepdims=True) + 1e-20)
            return (topk_idx, topk_w * SCALE)

        def _moe_experts(x, topk_idx, topk_w, w_gate, w_up, w_down):
            n = x.shape[0]
            flat_e = topk_idx.reshape(-1)
            rows = jnp.repeat(jnp.arange(n), K)
            oh = jax.nn.one_hot(flat_e, E, dtype=jnp.int32)
            pos = jnp.cumsum(oh, axis=0) - oh
            pos = jnp.take_along_axis(pos, flat_e[:, None], axis=1)[:, 0]
            valid = (pos < CAP).astype(x.dtype)
            p = jnp.minimum(pos, CAP - 1)
            buf = jnp.zeros((E, CAP, H), x.dtype).at[flat_e, p].add(x[rows] * valid[:, None])
            g = jnp.einsum('ech,ehi->eci', buf, w_gate)
            u = jnp.einsum('ech,ehi->eci', buf, w_up)
            y = jnp.einsum('eci,eih->ech', jax.nn.silu(g) * u, w_down)
            y_tok = y[flat_e, p] * (topk_w.reshape(-1) * valid)[:, None]
            return jnp.zeros((n, H), x.dtype).at[rows].add(y_tok)

        def _shared_mlp(x, sh_gate, sh_up, sh_down):
            return jax.nn.silu(x @ sh_gate) * (x @ sh_up) @ sh_down
        orig_shape = hidden_states.shape
        x = hidden_states.reshape(-1, H)
        topk_idx, topk_w = _route(x, router_weight, e_bias)
        moe_out = _moe_experts(x, topk_idx, topk_w.astype(x.dtype), w_gate, w_up, w_down)
        out = moe_out + _shared_mlp(x, sh_gate, sh_up, sh_down)
        return out.reshape(orig_shape)

    def _L1_xattn_ref(q, kv, seg_id, W_kvc, W_dq, W_uq, W_qr, W_uk, W_kr, W_uv, W_o):
        import jax, jax.numpy as jnp
        import numpy as np
        B, Lq, Lk = (2, 512, 128)
        Q_DIM, KV_DIM = (256, 256)
        H, HD = (16, 128)
        KVC, QC, R = (64, 96, 64)
        LOOKBACK = 8
        NEG = -1e+30

        def _rope(x, L):
            half = x.shape[-1] // 2
            inv_freq = 1.0 / 10000.0 ** (jnp.arange(half, dtype=jnp.float32) / half)
            ang = jnp.arange(L, dtype=jnp.float32)[:, None] * inv_freq
            cos, sin = (jnp.cos(ang), jnp.sin(ang))
            x1, x2 = (x[..., :half], x[..., half:])
            return jnp.concatenate([x1 * cos - x2 * sin, x1 * sin + x2 * cos], axis=-1)
        b, lq, _ = q.shape
        lk = kv.shape[1]
        kv_c = kv @ W_kvc
        q_c = q @ W_dq
        q_nope = (q_c @ W_uq).reshape(b, lq, H, HD).transpose(0, 2, 1, 3)
        q_rope = (q_c @ W_qr).reshape(b, lq, H, R).transpose(0, 2, 1, 3)
        k_nope = (kv_c @ W_uk).reshape(b, lk, H, HD)
        v = (kv_c @ W_uv).reshape(b, lk, H, HD)
        k_rope = kv_c @ W_kr
        q_rope = _rope(q_rope, lq)
        k_rope = _rope(k_rope, lk)
        scale = 1.0 / np.sqrt(HD + R).astype(np.float32)
        scores = (jnp.einsum('bhqd,bkhd->bhqk', q_nope, k_nope) + jnp.einsum('bhqr,bkr->bhqk', q_rope, k_rope)) * scale
        k_ids = jnp.arange(lk)[None, None, :]
        qs = seg_id[:, :, None]
        good = (k_ids <= qs) & (k_ids >= qs - LOOKBACK)
        scores = jnp.where(good[:, None, :, :], scores, NEG)
        attn = jax.nn.softmax(scores, axis=-1)
        out = jnp.einsum('bhqk,bkhd->bqhd', attn, v).reshape(b, lq, H * HD)
        return out @ W_o

    def _L1_ffn_ref(x, w_shared1, w_shared2, w1, w2, w_router):
        import jax, jax.numpy as jnp
        import numpy as np
        B, S, H = (4, 512, 256)
        I = 176
        E = 8
        K = 2
        INIT = 0.02
        bs, seq_len, hidden = x.shape
        xf = x.reshape(-1, hidden)
        T = xf.shape[0]
        shared = jax.nn.silu(xf @ w_shared1) @ w_shared2
        router_logits = xf @ w_router
        routing_probs = jax.nn.softmax(router_logits, axis=-1)
        top_k_probs, top_k_idx = jax.lax.top_k(routing_probs, K)
        top_k_probs = top_k_probs / jnp.sum(top_k_probs, axis=-1, keepdims=True)
        comb = jnp.zeros((T, E), dtype=xf.dtype).at[jnp.arange(T)[:, None], top_k_idx].add(top_k_probs)
        routed = jnp.zeros_like(xf)
        for e in range(E):
            expert_out = jax.nn.silu(xf @ w1[e]) @ w2[e]
            routed = routed + comb[:, e:e + 1] * expert_out
        final = (shared + routed).reshape(bs, seq_len, hidden)
        return final
    x = x + jnp.tanh(g_xattn[0]) * _L0_xattn_ref(_layernorm(x, axis=-1), ctx_2048, L0_xattn_Wq, L0_xattn_bq, L0_xattn_Wk, L0_xattn_bk, L0_xattn_Wv, L0_xattn_bv, L0_xattn_Wo, L0_xattn_bo)
    x = x + jnp.tanh(g_ffn[0]) * _L0_ffn_ref(_layernorm(x, axis=-1), L0_ffn_router_weight, L0_ffn_e_bias, L0_ffn_w_gate, L0_ffn_w_up, L0_ffn_w_down, L0_ffn_sh_gate, L0_ffn_sh_up, L0_ffn_sh_down)
    x = x + jnp.tanh(g_xattn[1]) * _L1_xattn_ref(_layernorm(x, axis=-1), ctx_2048, itok_BxS_0_1023, L1_xattn_W_kvc, L1_xattn_W_dq, L1_xattn_W_uq, L1_xattn_W_qr, L1_xattn_W_uk, L1_xattn_W_kr, L1_xattn_W_uv, L1_xattn_W_o)
    x = x + jnp.tanh(g_ffn[1]) * _L1_ffn_ref(_layernorm(x, axis=-1), L1_ffn_w_shared1, L1_ffn_w_shared2, L1_ffn_w1, L1_ffn_w2, L1_ffn_w_router)
    return x

_drawn_inputs = setup_inputs


def setup_inputs(seed=0):
    import zlib

    import numpy as np

    out = dict(_drawn_inputs(seed))
    spreads = {'g_ffn': (-1.0, 0.6), 'L0_ffn_e_bias': (0.0, 0.1)}
    factors = {'L0_xattn_bq': 4.753,
     'L0_xattn_bk': 5.854,
     'L0_xattn_bv': 8.0,
     'L0_xattn_bo': 8.0,
     'L1_ffn_w1': 2.872,
     'L1_ffn_w2': 2.842,
     'L1_ffn_w_router': 3.207}
    for name, (base, spread) in spreads.items():
        noise = np.random.default_rng([zlib.crc32(name.encode()), seed]).standard_normal(out[name].shape)
        drawn = base * np.exp(spread * noise) if base else spread * noise
        out[name] = jnp.asarray(drawn.astype(out[name].dtype))
    for name, factor in factors.items():
        out[name] = (out[name] * factor).astype(out[name].dtype)
    return out
```

```python
from contextlib import ExitStack, contextmanager

import concourse.bass as bass
from concourse import mybir

F32 = mybir.dt.float32
BF16 = mybir.dt.bfloat16
F16 = mybir.dt.float16
U32 = mybir.dt.uint32
ALU = mybir.AluOpType
ACT = mybir.ActivationFunctionType
AX = mybir.AxisListType

P = 128
B, S, D = 32, 64, 256
T = B * S
NT = T // P
EPS = 1e-5

H0, HD0 = 8, S // 8
BH = 2 * H0
PARTS = 6 * HD0


class Tile:

    def __init__(self, half, par):
        self.half, self.par = half, par
        self.t = 2 * half + par

    def plus(self, n):
        q = self.par + n
        return Tile(self.half + q // 2, q % 2)

    def times(self, n, more):
        return self.t * n + more

    def after(self, n):
        return not isinstance(self.half, int) or self.t >= n


class Chain:

    def __init__(self, eng, sem, tile, per):
        self.eng, self.sem, self.base, self.n, self.per = eng, sem, tile.t * per, 0, per

    def __call__(self, ins):
        self.n += 1
        ins.then_inc(self.sem, 1)
        self.eng.wait_ge(self.sem, self.base + self.n)

    def close(self):
        assert self.n == self.per, (self.n, self.per)


class Held:

    def __init__(self, eng, passed):
        self.eng, self.passed = eng, passed

    def wait_ge(self, sem, value):
        wait = self.eng.wait_ge(sem, value)
        if not isinstance(value, int):
            wait.then_inc(self.passed, 1)


@contextmanager
def stage_semaphores(nc):
    taken = []

    def gs(name):
        taken.append(nc.alloc_semaphore(name=name))
        return taken[-1]

    yield gs
    nc.clear_and_free_semaphores(taken)
    nc.all_engine_barrier()


def tile_steps(eng, step, first, last):
    lo = 2
    for t in range(first, lo):
        step(Tile(t // 2, t % 2))
    hi = (last + 1) // 2 * 2
    with eng.Fori(lo // 2, hi // 2) as half:
        step(Tile(half, 0))
        step(Tile(half, 1))
    for t in range(hi, last + 1):
        step(Tile(t // 2, t % 2))


def normalise_input(nc, gs, x, xn_out):
    with ExitStack() as ctx:
        xa = ctx.enter_context(nc.sbuf_tensor("ln_x", [P, NT, D], F32))
        layer_norm_block(nc, ctx, gs, "ln1", x, xa, xn_out)


def layer_norm_block(nc, ctx, gs, tag, src, xa, dst, xn=None):
    stats = ctx.enter_context(nc.sbuf_tensor(tag + "_stats", [P, NT, 6], F32))
    mv = ctx.enter_context(nc.sbuf_tensor(tag + "_mv", [P, NT, 2], F32))
    rstd = ctx.enter_context(nc.sbuf_tensor(tag + "_rstd", [P, NT], F32))
    eps = ctx.enter_context(nc.sbuf_tensor(tag + "_eps", [P, 1], F32))
    if xn is None:
        xn = ctx.enter_context(nc.sbuf_tensor(tag + "_xn", [P, NT, D], F32))
    Q = 4
    x_in = [gs(f"{tag}_x_in{q}") for q in range(NT // Q)]
    stats_done, mv_done, std_done = gs(tag + "_stats"), gs(tag + "_mv"), gs(tag + "_std")
    rstd_done, xn_done, stored = gs(tag + "_rstd"), gs(tag + "_xn"), gs(tag + "_stored")
    eps_set = gs(tag + "_eps")
    engines = ExitStack()
    block = engines.enter_context(nc.Block())

    @block.sync
    def _(sp):
        for q in range(NT // Q):
            sp.dma_start(xa[:, q * Q:(q + 1) * Q, :], src.rearrange("(t p) d -> p t d", p=P)[:, q * Q:(q + 1) * Q, :]
                         ).then_inc(x_in[q], 16)
        for q in range(NT // Q):
            sp.wait_ge(xn_done, (q + 1) * Q)
            sp.dma_start(dst.rearrange("(t p) d -> p t d", p=P)[:, q * Q:(q + 1) * Q, :], xn[:, q * Q:(q + 1) * Q, :]
                         ).then_inc(stored, 16)
        sp.wait_ge(stored, 16 * (NT // Q))

    @block.vector
    def _(dve):
        dve.memset(eps[:], EPS).then_inc(eps_set, 1)
        for t in range(NT):
            if t % Q == 0:
                dve.wait_ge(x_in[t // Q], 16)
            dve.bn_stats(stats[:, t, :], xa[:, t, :]).then_inc(stats_done, 1)
        for t in range(NT):
            dve.wait_ge(stats_done, t + 1)
            dve.bn_aggr(mv[:, t, :], stats[:, t, :]).then_inc(mv_done, 1)
        dve.wait_ge(std_done, 1)
        dve.reciprocal(rstd[:], rstd[:]).then_inc(rstd_done, 1)
        dve.wait_ge(rstd_done, 1)
        for t in range(NT):
            dve.tensor_scalar(xn[:, t, :], xa[:, t, :], mv[:, t, 0:1], rstd[:, t:t + 1],
                              ALU.subtract, ALU.mult).then_inc(xn_done, 1)

    @block.scalar
    def _(act):
        act.wait_ge(eps_set, 1)
        act.wait_ge(mv_done, NT)
        act.activation(rstd[:], mv[:, :, 1], ACT.Sqrt, bias=eps[:, 0:1]).then_inc(std_done, 1)

    engines.close()


def layer0_attention(nc, gs, x, ctx_in, xn_in, x1_out, w):
    ctx = ExitStack()
    with ctx:
        def sb(name, shape, dt):
            return ctx.enter_context(nc.sbuf_tensor("a0_" + name, shape, dt))

        def ps(name, shape, dt):
            return ctx.enter_context(nc.psum_tensor("a0_" + name, shape, dt))

        ident = sb("ident", [P, P], F32)
        identb = sb("identb", [P, P], BF16)
        wq = sb("wq", [P, P], F32)
        wkv = sb("wkv", [P, 2 * P], F32)
        wo = sb("wo", [P, P], F32)
        bias = sb("bias", [1, 3 * P], F32)
        ones = sb("ones", [1, P], F32)
        bo = sb("bo", [P, 1], F32)
        gate = sb("gate", [P, 1], F32)
        tg = sb("tg", [P, 1], F32)
        cos4 = sb("cos4", [P, 4 * BH, 4], F32)
        sin4 = sb("sin4", [P, 4 * BH, 4], F32)
        pick = sb("pick", [P, BH, P], BF16)
        xn = [sb(f"xn{i}", [P, D], F32) for i in range(2)]
        cx = [sb(f"cx{i}", [P, D], F32) for i in range(2)]
        xres = [sb(f"xres{i}", [P, D], F32) for i in range(2)]
        qkv = sb("qkv", [P, 3, 2, P], F32)
        ra = sb("ra", [P, 4 * BH, 4], F32)
        rb = sb("rb", [P, 4 * BH, 4], F32)
        rest = sb("rest", [P, 2, 2 * BH, HD0], F32)
        parts = sb("parts", [P, 2, 2 * BH, 64], BF16)
        va = [sb(f"va{i}", [P, 2, BH, 32], F32) for i in range(2)]
        qkT = [sb(f"qkT{i}", [P, 2, 2, H0, P], BF16) for i in range(2)]
        top = [sb(f"top{i}", [P, H0, 2, 2], F32) for i in range(2)]
        negm = sb("negm", [P, 2, 2, 64], BF16)
        negT = [sb(f"negT{i}", [P, 2 * P], BF16) for i in range(2)]
        prob = [sb(f"prob{i}", [P, 2, 2 * P], F32) for i in range(4)]
        u = sb("u", [P, 2, 2, P], F32)
        rden = sb("rden", [P, 2, H0], F32)
        att = sb("att", [P, 2, P], F32)
        attT = sb("attT", [P, D], F32)
        res = sb("res", [P, D], F32)
        x1 = [sb(f"x1{i}", [P, D], F32) for i in range(2)]

        mx = [ps(f"mx{i}", [P, 2, 2 * P], F32) for i in range(2)]
        sc = [ps(f"sc{i}", [P, 2, 2 * P], F32) for i in range(2)]
        pv = ps("pv", [P, 2, 2, P], F32)
        ma = [ps(f"ma{i}", [P, 512], F32) for i in range(2)]
        mc = ps("mc", [P, 512], F32)

        const_in = gs("a0_const_in")
        NCONST = 12
        ready = gs("a0_ready")
        tanh_done = gs("a0_tanh")
        xn_in_s = [gs(f"a0_xn_in{i}") for i in range(2)]
        cx_in_s = [gs(f"a0_cx_in{i}") for i in range(2)]
        xres_in = [gs(f"a0_xres_in{i}") for i in range(2)]
        proj = gs("a0_proj")
        proj_out = gs("a0_proj_out")
        rotate = gs("a0_rotate")
        split = gs("a0_split")
        v_staged = gs("a0_v_staged")
        turned = gs("a0_turned")
        turned_out = gs("a0_turned_out")
        score_q = gs("a0_score_q")
        max_done = gs("a0_max")
        neg = gs("a0_neg")
        neg_turned = gs("a0_neg_turned")
        neg_out = gs("a0_neg_out")
        score_k = gs("a0_score_k")
        exp_done = gs("a0_exp")
        pv_done = gs("a0_pv")
        u_out = gs("a0_u_out")
        u_turned = gs("a0_u_turned")
        rden_done = gs("a0_rden")
        att_done = gs("a0_att")
        att_turned = gs("a0_att_turned")
        attT_out = gs("a0_attT_out")
        out_done = gs("a0_out")
        res_done = gs("a0_res")
        x1_done = gs("a0_x1")
        stored = [gs(f"a0_stored{i}") for i in range(2)]

        block = ctx.enter_context(nc.Block())
        consts = [(ident, w["ident"]), (identb, w["identb"]), (wq, w["wq0"]), (wkv, w["wkv0"]), (wo, w["wo0"]),
                  (bias, w["bias0"]), (ones, w["ones0"]), (bo, w["bo0"]), (gate, w["g00"]), (cos4, w["cos4"]),
                  (sin4, w["sin4"]), (pick, w["pick"])]
        assert len(consts) == NCONST

        @block.sync
        def _(sp):
            for dst, src in consts:
                sp.dma_start(dst[:], src).then_inc(const_in, 16)

            def loads(tl):
                row = sp.snap(tl.t * P) if not isinstance(tl.t, int) else tl.t * P
                used = sp.snap(tl.times(2, 0) - 2) if not isinstance(tl.t, int) else tl.times(2, -2)
                got = sp.snap(tl.t - 1) if not isinstance(tl.t, int) else tl.t - 1
                if tl.after(2):
                    sp.wait_ge(proj, used)
                sp.dma_start(xn[tl.par][:], xn_in[bass.ds(row, P), :]).then_inc(xn_in_s[tl.par], 16)
                sp.dma_start(cx[tl.par][:], ctx_in[bass.ds(row, P), :]).then_inc(cx_in_s[tl.par], 16)
                if tl.after(2):
                    sp.wait_ge(x1_done, got)
                sp.dma_start(xres[tl.par][:], x[bass.ds(row, P), :]).then_inc(xres_in[tl.par], 16)

            tile_steps(sp, loads, 0, NT - 1)

        @block.gpsimd
        def _(pool):
            held = Held(pool, gs("a0_pool_passed"))
            pool.wait_ge(const_in, 16 * NCONST)
            pool.wait_ge(ready, 6)
            qkf = qkv[:, 0:2].rearrange("p a c (h d) -> p (a c h) d", d=HD0)

            def rotate_and_split(tl):
                step = Chain(held, rotate, tl, 13)
                held.wait_ge(proj_out, tl.times(2, 2))
                step(pool.tensor_tensor(ra[:], qkf[:, :, 0:4], cos4[:], ALU.mult))
                step(pool.tensor_tensor(rb[:, :, 0:2], qkf[:, :, 2:4], sin4[:, :, 0:2], ALU.mult))
                step(pool.tensor_tensor(rb[:, :, 2:4], qkf[:, :, 0:2], sin4[:, :, 2:4], ALU.mult))
                step(pool.tensor_tensor(qkf[:, :, 0:4], ra[:], rb[:], ALU.add))
                if tl.after(1):
                    held.wait_ge(turned, tl.times(4, 0))
                n = 2 * BH
                q = qkf[:, 0:n, :]
                k = qkf[:, n:2 * n, :]
                pq = parts[:, 0, :, 0:PARTS].rearrange("p h (r d) -> p h r d", d=HD0)
                pk = parts[:, 1, :, 0:PARTS].rearrange("p h (r d) -> p h r d", d=HD0)

                def spread(a, m):
                    return a.unsqueeze(2).to_broadcast([P, n, m, HD0])

                step(pool.tensor_copy(pq[:, :, 0:3, :], spread(q, 3)))
                step(pool.tensor_copy(pk[:, :, 0:4:3, :], spread(k, 2)))
                step(pool.tensor_copy(pk[:, :, 5, :], k))
                step(pool.tensor_tensor(rest[:, 0], q, pq[:, :, 0, :], ALU.subtract))
                step(pool.tensor_tensor(rest[:, 1], k, pk[:, :, 0, :], ALU.subtract))
                step(pool.tensor_copy(pq[:, :, 3:5, :], spread(rest[:, 0], 2)))
                step(pool.tensor_copy(pk[:, :, 1, :], rest[:, 1]))
                step(pool.tensor_copy(pk[:, :, 4, :], rest[:, 1]))
                step(pool.tensor_tensor(pq[:, :, 5, :], rest[:, 0], pq[:, :, 3, :], ALU.subtract))
                step.close()
                pool.tensor_tensor(pk[:, :, 2, :], rest[:, 1], pk[:, :, 1, :], ALU.subtract).then_inc(split, 1)

            def stage_v(tl):
                if tl.after(2):
                    held.wait_ge(pv_done, tl.times(H0, -H0))
                pool.tensor_copy(va[tl.par][:, :, :, 0:HD0], qkv[:, 2].rearrange("p c (h d) -> p c h d", d=HD0)
                                 ).then_inc(v_staged, 1)

            def negate(tl):
                held.wait_ge(max_done, tl.times(BH, BH))
                if tl.after(1):
                    held.wait_ge(neg_turned, tl.times(1, 0))
                m = top[tl.par][:].rearrange("p a r c -> p c (a r)").unsqueeze(2).to_broadcast([P, 2, 2, BH])
                high, low, left = negm[:, :, :, 0:BH], negm[:, :, :, BH:2 * BH], negm[:, :, :, 2 * BH:3 * BH]
                pool.tensor_scalar(high, m, -1.0, None, ALU.mult).then_inc(neg, 1)
                held.wait_ge(neg, tl.times(3, 1))
                pool.tensor_tensor(left, high, m, ALU.add).then_inc(neg, 1)
                held.wait_ge(neg, tl.times(3, 2))
                pool.tensor_scalar(low, left, -1.0, None, ALU.mult).then_inc(neg, 1)

            def residual(tl):
                held.wait_ge(res_done, tl.times(1, 1))
                held.wait_ge(xres_in[tl.par], tl.half * 16 + 16)
                if tl.after(2):
                    held.wait_ge(stored[tl.par], tl.half * 16)
                pool.tensor_tensor(x1[tl.par][:], res[:], xres[tl.par][:], ALU.add).then_inc(x1_done, 1)

            def step(tl, a=True, b=True, c=True):
                if a:
                    rotate_and_split(tl.plus(2))
                if b:
                    negate(tl.plus(1))
                if c:
                    residual(tl)
                if a:
                    stage_v(tl.plus(2))

            rotate_and_split(Tile(0, 0))
            stage_v(Tile(0, 0))
            step(Tile(-1, 1), c=False)

            step(Tile(0, 0))
            step(Tile(0, 1))
            with pool.Fori(1, NT // 2 - 1) as half:
                step(Tile(half, 0))
                step(Tile(half, 1))
            step(Tile(NT // 2 - 1, 0), a=False)
            step(Tile(NT // 2 - 1, 1), a=False, b=False)

        @block.tensor
        def _(pe):
            pe.wait_ge(const_in, 16 * NCONST)
            pe.wait_ge(ready, 6)

            def project(tl):
                pe.wait_ge(xn_in_s[tl.par], tl.half * 16 + 16)
                pe.wait_ge(cx_in_s[tl.par], tl.half * 16 + 16)
                for c in range(2):
                    pos = slice(c * P, (c + 1) * P)
                    pe.matmul(ma[c][:, 0:P], xn[tl.par][:, pos], wq[:], start=True, stop=False)
                    pe.matmul(ma[c][:, 0:P], ones[:], bias[:, 0:P], start=False, stop=True)
                    pe.matmul(ma[c][:, P:3 * P], cx[tl.par][:, pos], wkv[:], start=True, stop=False)
                    pe.matmul(ma[c][:, P:3 * P], ones[:], bias[:, P:3 * P], start=False, stop=True
                              ).then_inc(proj, 1)

            def turn(tl, f):
                if f == 0:
                    pe.wait_ge(split, tl.times(1, 1))
                    if tl.after(1):
                        pe.wait_ge(neg_out, tl.times(1, 0))
                if f >= 2:
                    pe.wait_ge(turned_out, tl.times(4, f - 1))
                out = ma[f % 2][:].bitcast(BF16).rearrange("p (j t) -> p j t", t=P)
                for j in range(H0):
                    g = (f % 2) * BH + 2 * j
                    mm = pe.transpose(out[:, j, :], parts[:, f // 2, g:g + 2, :].rearrange("p h s -> p (h s)"),
                                      identb[:])
                mm.then_inc(turned, 1)

            def score_queries(tl, h):
                if h == 0:
                    pe.wait_ge(turned_out, tl.times(4, 4))
                if h >= 2 or tl.after(1):
                    pe.wait_ge(max_done, tl.times(BH, h - 1))
                rows = slice(64 * (h % 2), 64 * (h % 2) + PARTS)
                t = qkT[tl.par]
                for c in range(2):
                    mm = pe.matmul(mx[h % 2][:, c, :], t[rows, 0, c, h // 2, :], t[rows, 1, :, h // 2, :],
                                   start=True, stop=True)
                mm.then_inc(score_q, 1)

            def turn_neg(tl, a):
                pe.wait_ge(neg, tl.times(3, 3))
                if a:
                    pe.wait_ge(proj_out, tl.plus(1).times(2, 1))
                out = ma[0][:, 0:P].bitcast(BF16).rearrange("p (c t) -> p c t", c=2)
                for c in range(2):
                    mm = pe.transpose(out[:, c, :], negm[:, c].rearrange("p a b -> p (a b)"), identb[:])
                mm.then_inc(neg_turned, 1)

            def score_keys(tl, h):
                if h == 0:
                    pe.wait_ge(neg_out, tl.times(1, 1))
                if h >= 2 or tl.after(1):
                    pe.wait_ge(exp_done, tl.times(BH, h - 1))
                rows = slice(64 * (h % 2), 64 * (h % 2) + PARTS)
                half = slice(64 * (h % 2), 64 * (h % 2) + 64)
                t = qkT[tl.par]
                for c in range(2):
                    pe.matmul(sc[h % 2][:, c, :], t[rows, 1, c, h // 2, :], t[rows, 0, :, h // 2, :],
                              start=True, stop=False)
                    mm = pe.matmul(sc[h % 2][:, c, :], pick[half, h, :], negT[tl.par][half, :], start=False, stop=True)
                mm.then_inc(score_k, 1)

            def weigh(tl, j):
                pe.wait_ge(exp_done, tl.times(BH, 2 * j + 2))
                if j == 0:
                    pe.wait_ge(v_staged, tl.times(1, 1))
                if j == 0 and tl.after(1):
                    pe.wait_ge(u_out, tl.times(2, 0))
                if j == 4:
                    pe.wait_ge(u_out, tl.times(2, 1))
                for c in range(2):
                    for h in (2 * j, 2 * j + 1):
                        col = 32 * (h % 4)
                        mm = pe.matmul(pv[col:col + 32, (h // 4) % 2].rearrange("p a b -> p (a b)"),
                                       va[tl.par][:, c, h, :], prob[h % 4][:, c, :], start=(c == 0), stop=(c == 1),
                                       skip_group_check=True)
                mm.then_inc(pv_done, 1)

            def turn_u(tl, b):
                pe.wait_ge(u_out, tl.times(2, b + 1))
                if b == 1:
                    pe.wait_ge(att_done, tl.times(4, 2))
                elif tl.after(1):
                    pe.wait_ge(res_done, tl.times(1, 0))
                for c in range(2):
                    for g in range(2):
                        mm = pe.transpose(mc[:, (2 * c + g) * P:(2 * c + g + 1) * P], u[:, g, c, :], ident[:])
                mm.then_inc(u_turned, 1)

            def project_out(tl):
                pe.wait_ge(att_done, tl.times(4, 4))
                for c in range(2):
                    mm = pe.transpose(mc[:, c * P:(c + 1) * P], att[:, c, :], ident[:])
                mm.then_inc(att_turned, 1)
                pe.wait_ge(attT_out, tl.times(1, 1))
                pe.matmul(mc[:, 0:D], wo[:], attT[:], start=True, stop=True).then_inc(out_done, 1)

            def step(tl, a=True, b=True, c=True):
                nxt, next2 = tl.plus(1), tl.plus(2)
                for s in range(BH + 4):
                    if b and s < 4:
                        turn(nxt, s)
                    if c and s < BH:
                        score_keys(tl, s)
                        if s % 2 == 0 and s:
                            weigh(tl, s // 2 - 1)
                        if s == 11:
                            turn_u(tl, 0)
                    if b and s >= 4:
                        score_queries(nxt, s - 4)
                    if a and s == 6:
                        project(next2)
                if c:
                    weigh(tl, H0 - 1)
                    turn_u(tl, 1)
                if b:
                    turn_neg(nxt, a)
                if c:
                    project_out(tl)

            project(Tile(0, 0))
            step(Tile(-1, 1), c=False)
            step(Tile(0, 0))
            step(Tile(0, 1))
            with pe.Fori(1, NT // 2 - 1) as half:
                step(Tile(half, 0))
                step(Tile(half, 1))
            step(Tile(NT // 2 - 1, 0), a=False)
            step(Tile(NT // 2 - 1, 1), a=False, b=False)

        @block.scalar
        def _(act):
            act.wait_ge(const_in, 16 * NCONST)
            act.wait_ge(ready, 6)
            act.activation(tg[:], gate[:], ACT.Tanh).then_inc(tanh_done, 1)

            def projections(tl):
                for c in range(2):
                    act.wait_ge(proj, tl.times(2, c + 1))
                    if c == 0 and tl.after(1):
                        act.wait_ge(split, tl.times(1, 0))
                        act.wait_ge(v_staged, tl.times(1, 0))
                    act.copy(qkv[:, :, c, :], ma[c][:, 0:3 * P].rearrange("p (a n) -> p a n", a=3)
                             ).then_inc(proj_out, 1)

            def exponent(tl, h):
                act.wait_ge(score_k, tl.times(BH, h + 1))
                if h >= 4 or tl.after(1):
                    act.wait_ge(pv_done, tl.times(H0, h // 2 - 1))
                act.activation(prob[h % 4][:], sc[h % 2][:], ACT.Exp, scale=float(HD0) ** -0.5).then_inc(exp_done, 1)

            def sums(tl, b):
                act.wait_ge(pv_done, tl.times(H0, 4 * b + 4))
                if b == 1 or tl.after(1):
                    act.wait_ge(u_turned, tl.times(2, b))
                act.copy(u[:], pv[:]).then_inc(u_out, 1)

            def turned_heads(tl):
                act.wait_ge(att_turned, tl.times(1, 1))
                if tl.after(1):
                    act.wait_ge(out_done, tl.times(1, 0))
                act.copy(attT[:], mc[:, 0:D]).then_inc(attT_out, 1)

            def store(tl):
                act.wait_ge(x1_done, tl.times(1, 1))
                act.dma_start(x1_out[bass.ds(tl.t * P, P), :], x1[tl.par][:]).then_inc(stored[tl.par], 16)

            def step(tl, a=True, c=True):
                for s in range(BH):
                    if c:
                        exponent(tl, s)
                        if s == 6 and tl.after(1):
                            store(Tile(tl.half, 0) if tl.par else Tile(tl.half - 1, 1))
                        if s == 10:
                            sums(tl, 0)
                    if a and s == 8:
                        projections(tl.plus(2))
                if c:
                    sums(tl, 1)
                    turned_heads(tl)

            projections(Tile(0, 0))
            step(Tile(-1, 1), c=False)
            step(Tile(0, 0))
            step(Tile(0, 1))
            with act.Fori(1, NT // 2 - 1) as half:
                step(Tile(half, 0))
                step(Tile(half, 1))
            step(Tile(NT // 2 - 1, 0), a=False)
            step(Tile(NT // 2 - 1, 1), a=False)
            store(Tile(NT // 2 - 1, 1))
            for i in range(2):
                act.wait_ge(stored[i], 16 * (NT // 2))

        @block.vector
        def _(dve):
            dve.memset(parts[:, :, :, PARTS:64], 0.0).then_inc(ready, 1)
            dve.memset(negm[:], 0.0).then_inc(ready, 1)
            for i in range(2):
                dve.memset(va[i][:, :, :, HD0:HD0 + 1], 1.0).then_inc(ready, 1)
                dve.memset(va[i][:, :, :, HD0 + 1:32], 0.0).then_inc(ready, 1)
            dve.wait_ge(const_in, 16 * NCONST)
            dve.wait_ge(tanh_done, 1)
            dve.wait_ge(ready, 6)

            def turned_pairs(tl, f):
                dve.wait_ge(turned, tl.times(4, f + 1))
                dve.tensor_copy(qkT[tl.par][:, f // 2, f % 2], ma[f % 2][:].bitcast(BF16)
                                .rearrange("p (j t) -> p j t", t=P)).then_inc(turned_out, 1)

            def maxima(tl, h):
                dve.wait_ge(score_q, tl.times(BH, h + 1))
                if h == 0 and tl.after(2):
                    dve.wait_ge(neg, tl.times(3, -3))
                dve.tensor_reduce(top[tl.par][:, h // 2, h % 2, :], mx[h % 2][:], AX.X, ALU.max).then_inc(max_done, 1)

            def negated(tl):
                dve.wait_ge(neg_turned, tl.times(1, 1))
                dve.tensor_copy(negT[tl.par][:], ma[0][:, 0:P].bitcast(BF16)).then_inc(neg_out, 1)

            def divide(tl, b):
                dve.wait_ge(u_turned, tl.times(2, b + 1))
                if b == 0 and tl.after(1):
                    dve.wait_ge(att_turned, tl.times(1, 0))
                heads = mc[:].rearrange("p (c h w) -> p c h w", c=2, w=32)
                dve.reciprocal(rden[:], heads[:, :, :, HD0]).then_inc(rden_done, 1)
                dve.wait_ge(rden_done, tl.times(2, b + 1))
                for c in range(2):
                    dve.tensor_tensor(att[:, c, b * 64:(b + 1) * 64].rearrange("p (h d) -> p h d", d=HD0),
                                      heads[:, c, :, 0:HD0], rden[:, c, :].unsqueeze(2).to_broadcast([P, H0, HD0]),
                                      ALU.mult).then_inc(att_done, 1)

            def gated(tl):
                dve.wait_ge(out_done, tl.times(1, 1))
                if tl.after(1):
                    dve.wait_ge(x1_done, tl.times(1, 0))
                dve.tensor_scalar(res[:], mc[:, 0:D], bo[:, 0:1], tg[:, 0:1], ALU.add, ALU.mult
                                  ).then_inc(res_done, 1)

            def step(tl, b=True, c=True):
                nxt = tl.plus(1)
                for s in range(BH + 4):
                    if b and s < 4:
                        turned_pairs(nxt, s)
                    if b and s >= 4:
                        maxima(nxt, s - 4)
                    if c and s == 13:
                        divide(tl, 0)
                if b:
                    negated(nxt)
                if c:
                    divide(tl, 1)
                    gated(tl)

            step(Tile(-1, 1), c=False)
            step(Tile(0, 0))
            step(Tile(0, 1))
            with dve.Fori(1, NT // 2 - 1) as half:
                step(Tile(half, 0))
                step(Tile(half, 1))
            step(Tile(NT // 2 - 1, 0))
            step(Tile(NT // 2 - 1, 1), b=False)


E0, K0, I0 = 64, 8, 88
G0, GTOP = 8, 4
CAP = 128
SCALE0 = 2.5
NONE = E0 * CAP
KC = D // P


def turned_tiles(nc, sb, ps, gs, tag, src, dst, block):
    bank = [ps(f"turn{i}", [P, 4, P], F32) for i in range(2)]
    turned, out = gs(tag + "_turned"), gs(tag + "_turned_out")
    fills = NT * KC // 4

    def on_pe(pe, ident):
        for f in range(fills):
            if f >= 2:
                pe.wait_ge(out, f - 1)
            for j in range(4):
                t, c = f * 2 + j // KC, j % KC
                mm = pe.transpose(bank[f % 2][:, j, :], src[:, t, c * P:(c + 1) * P], ident)
            mm.then_inc(turned, 1)

    def on_act(act):
        for f in range(fills):
            act.wait_ge(turned, f + 1)
            act.copy(dst[:, :, f * 2 * P:(f * 2 + 2) * P].rearrange("p c (t n) -> p t c n", t=2),
                     bank[f % 2][:].rearrange("p (t c) n -> p t c n", c=KC)).then_inc(out, 1)

    return on_pe, on_act, out, fills


def routing(nc, gs, xn_all, w, shared_out, idx_out, y_zero, slot_ids, slot_w):
    ctx = ExitStack()
    with ctx:
        def sb(name, shape, dt=F32):
            return ctx.enter_context(nc.sbuf_tensor("r_" + name, shape, dt))

        def ps(name, shape, dt):
            return ctx.enter_context(nc.psum_tensor("r_" + name, shape, dt))

        NE = NT * E0
        ident = sb("ident", [P, P])
        rw = sb("rw", [P, KC, E0])
        ebias = sb("ebias", [P, E0])
        shg, shu = sb("shg", [P, KC, I0]), sb("shu", [P, KC, I0])
        shd = sb("shd", [I0, D])
        earlier = sb("earlier", [P, P], BF16)
        onesb = sb("onesb", [P, P], BF16)
        below = sb("below", [P, G0, G0])
        slot1 = sb("slot1", [P, E0])
        iota = sb("iota", [P, CAP])
        tok = sb("tok", [P, NT])
        xT = sb("xT", [P, KC, T])
        gs_h = sb("silu", [I0, 512])
        hT = sb("hT", [I0, T])
        sh = sb("sh", [P, 2, D])
        zero = sb("zero", [1, D])
        score = sb("score", [P, NT, E0])
        sc = sb("sc", [P, NT, E0])
        hi = [sb(f"hi{n}", [P, NT * G0, 4 >> n]) for n in range(3)]
        lo = [sb(f"lo{n}", [P, NT * G0, 4 >> n]) for n in range(3)]
        tmp = sb("tmp", [P, NT * G0, 2])
        group = sb("group", [P, NT, G0])
        gt = sb("gt", [P, NT, G0, G0])
        eq = sb("eq", [P, NT, G0, G0])
        rank = sb("rank", [P, NT, G0])
        best = sb("best", [P, NT, K0])
        gone = sb("gone", [P, NT, E0])
        sel = sb("sel", [P, NT, E0])
        selb = sb("selb", [P, NT, E0], BF16)
        before = sb("before", [P, NT, E0], BF16)
        wsum = sb("wsum", [P, NT])
        wt = sb("wt", [P, NT, E0])
        slot = sb("slot", [P, NT, E0])
        mine = sb("mine", [P, NT, K0])
        empty = sb("empty", [P, NT, K0])
        idx = sb("idx", [P, NT, K0], U32)
        cidx = sb("cidx", [P, NT, K0], U32)
        cpos = sb("cpos", [P, NT, K0])
        val = sb("val", [P, NT, 3, E0], F16)
        onec = [sb(f"onec{i}", [P, K0, CAP], F16) for i in range(2)]
        onee = sb("onee", [P, K0, E0], F16)
        ev = [sb(f"ev{i}", [P, K0, 3, E0], F16) for i in range(2)]
        stage = sb("stage", [P, 3, E0])

        const_in = gs("r_const_in")
        logits_done = gs("r_logits")
        score_done = gs("r_score")
        up_done = gs("r_up")
        silu_done = gs("r_silu")
        h_done = gs("r_h")
        down_done = gs("r_down")
        sh_out = gs("r_sh_out")
        sh_stored = [gs(f"r_sh_stored{i}") for i in range(2)]
        chain = gs("r_steps")
        sel_done = gs("r_sel")
        pos_done = gs("r_pos")
        val_done = gs("r_val")
        onec_done = gs("r_onec")
        onee_done = gs("r_onee")
        ev_done = gs("r_ev")
        spread_done = gs("r_spread")
        idx_done = gs("r_idx")
        stored = gs("r_stored")
        zeroed = gs("r_zeroed")

        block = ctx.enter_context(nc.Block())
        consts = [(ident, w["ident"]), (rw, w["rw"]), (ebias, w["ebias"]), (shg, w["shg"]), (shu, w["shu"]),
                  (shd, w["shd"]), (earlier, w["earlier"]), (onesb, w["onesb"]), (below, w["below"]),
                  (slot1, w["slot1"]), (iota, w["iota"]), (tok, w["tok"])]
        turn_pe, turn_act, xT_out, xT_fills = turned_tiles(nc, lambda *a: sb(*a), ps, gs, "r", xn_all, xT, block)
        lg = ps("lg", [P, NT, E0], F32)
        up = ps("up", [P, 2, 512], F32)
        down = [ps(f"down{i}", [P, 2, D], F32) for i in range(2)]

        @block.sync
        def _(sp):
            for dst, src in consts:
                sp.dma_start(dst[:], src).then_inc(const_in, 16)
            sp.wait_ge(zeroed, 1)
            sp.dma_start(y_zero, zero[:]).then_inc(stored, 16)
            for p in range(NT // 2):
                sp.wait_ge(sh_out, p + 1)
                sp.dma_start(shared_out.rearrange("(t p) d -> p t d", p=P)[:, 2 * p:2 * p + 2, :], sh[:]
                             ).then_inc(sh_stored[0], 16)
            sp.wait_ge(idx_done, 1)
            sp.dma_start(idx_out.rearrange("(t p) k -> p t k", p=P), idx[:]).then_inc(stored, 16)
            sp.wait_ge(stored, 32)
            sp.wait_ge(sh_stored[0], 16 * (NT // 2))

        @block.tensor
        def _(pe):
            pe.wait_ge(const_in, 16 * len(consts))
            turn_pe(pe, ident[:])
            pe.wait_ge(xT_out, xT_fills)
            for t in range(NT):
                for c in range(KC):
                    mm = pe.matmul(lg[:, t, :], xT[:, c, t * P:(t + 1) * P], rw[:, c, :], start=(c == 0),
                                   stop=(c == KC - 1))
            mm.then_inc(logits_done, 1)
            for b in range(4):
                if b:
                    pe.wait_ge(h_done, b)
                for n, wt_ in enumerate((shg, shu)):
                    for c in range(KC):
                        mm = pe.matmul(up[0:I0, n, :], wt_[:, c, :], xT[:, c, b * 512:(b + 1) * 512],
                                       start=(c == 0), stop=(c == KC - 1))
                mm.then_inc(up_done, 1)
            pe.wait_ge(h_done, 4)
            for p in range(NT // 2):
                if p >= 2:
                    pe.wait_ge(sh_out, p - 1)
                for j in range(2):
                    t = 2 * p + j
                    mm = pe.matmul(down[p % 2][:, j, :], hT[:, t * P:(t + 1) * P], shd[:], start=True, stop=True)
                mm.then_inc(down_done, 1)
            pe.wait_ge(sel_done, 1)
            for n in range(2):
                tiles = slice(n * NT // 2, (n + 1) * NT // 2)
                pe.matmul(lg[:, tiles, :], earlier[:], selb[:, tiles, :], start=True, stop=False)
                mm = pe.matmul(lg[:, tiles, :], onesb[:], before[:, tiles, :], start=False, stop=True)
            mm.then_inc(pos_done, 1)

            def spread(tl):
                pe.wait_ge(onec_done, tl.times(1, 1))
                pe.wait_ge(ev_done, tl.times(1, 1))
                first, last = tl.t == 0, isinstance(tl.t, int) and tl.t == NT - 1
                for k in range(K0):
                    mm = pe.matmul(up[:, 0, 0:3 * E0], onec[tl.par][:, k, :],
                                   ev[tl.par][:, k].rearrange("p v e -> p (v e)"),
                                   start=bool(isinstance(tl.t, int) and first and k == 0),
                                   stop=(last and k == K0 - 1), skip_group_check=True)
                mm.then_inc(spread_done, 1)

            tile_steps(pe, spread, 0, NT - 1)

        @block.scalar
        def _(act):
            act.wait_ge(const_in, 16 * len(consts))
            turn_act(act)
            act.wait_ge(logits_done, 1)
            act.activation(score[:], lg[:], ACT.Sigmoid).then_inc(score_done, 1)
            for b in range(4):
                act.wait_ge(up_done, b + 1)
                if b:
                    act.wait_ge(h_done, b)
                act.activation(gs_h[:], up[0:I0, 0, :], ACT.Silu).then_inc(silu_done, 1)
            for p in range(NT // 2):
                act.wait_ge(down_done, p + 1)
                if p:
                    act.wait_ge(sh_stored[0], 16 * p)
                act.copy(sh[:], down[p % 2][:]).then_inc(sh_out, 1)

        @block.vector
        def _(dve):
            steps = [0]

            def link(ins):
                steps[0] += 1
                ins.then_inc(chain, 1)
                dve.wait_ge(chain, steps[0])

            dve.memset(zero[:], 0.0).then_inc(zeroed, 1)
            dve.wait_ge(const_in, 16 * len(consts))
            for b in range(4):
                dve.wait_ge(silu_done, b + 1)
                dve.tensor_tensor(hT[:, b * 512:(b + 1) * 512], gs_h[:], up[0:I0, 1, :], ALU.mult).then_inc(h_done, 1)
            dve.wait_ge(score_done, 1)
            link(dve.tensor_tensor(sc[:], score[:], ebias[:].unsqueeze(1).to_broadcast([P, NT, E0]), ALU.add))
            eight = sc[:].rearrange("p t (g m) -> p (t g) m", m=8)
            link(dve.tensor_tensor(hi[0][:], eight[:, :, 0:4], eight[:, :, 4:8], ALU.max))
            link(dve.tensor_tensor(lo[0][:], eight[:, :, 0:4], eight[:, :, 4:8], ALU.min))
            for n in range(2):
                m = 2 >> n
                h1, h2 = hi[n][:, :, 0:m], hi[n][:, :, m:2 * m]
                link(dve.tensor_tensor(hi[n + 1][:], h1, h2, ALU.max))
                link(dve.tensor_tensor(lo[n + 1][:], h1, h2, ALU.min))
                link(dve.tensor_tensor(tmp[:, :, 0:m], lo[n][:, :, 0:m], lo[n][:, :, m:2 * m], ALU.max))
                link(dve.tensor_tensor(lo[n + 1][:], lo[n + 1][:], tmp[:, :, 0:m], ALU.max))
            link(dve.tensor_tensor(group[:].rearrange("p t g -> p (t g)"), hi[2][:, :, 0], lo[2][:, :, 0], ALU.add))
            full = [P, NT, G0, G0]
            other, own = group[:].unsqueeze(2).to_broadcast(full), group[:].unsqueeze(3).to_broadcast(full)
            link(dve.tensor_tensor(gt[:], other, own, ALU.is_gt))
            link(dve.tensor_tensor(eq[:], other, own, ALU.is_equal))
            link(dve.tensor_tensor(eq[:], eq[:], below[:].unsqueeze(1).to_broadcast(full), ALU.mult))
            link(dve.tensor_tensor(gt[:], gt[:], eq[:], ALU.add))
            link(dve.tensor_reduce(rank[:], gt[:], AX.X, ALU.add))
            link(dve.tensor_scalar(rank[:], rank[:], float(GTOP) - 0.5, None, ALU.is_lt))
            link(dve.tensor_tensor(sc[:].rearrange("p t (g m) -> p (t g) m", m=8), eight,
                                   rank[:].rearrange("p t g -> p (t g)").unsqueeze(2).to_broadcast([P, NT * G0, 8]),
                                   ALU.mult))
            for t in range(NT):
                ins = dve.max(best[:, t, :], sc[:, t, :])
                if t == NT - 1:
                    link(ins)
            link(dve.memset(before[:, 0, :], 0.0))
            for t in range(NT):
                ins = dve.match_replace(gone[:, t, :], best[:, t, :], sc[:, t, :], -1e30)
                if t == NT - 1:
                    link(ins)
            link(dve.tensor_tensor(sel[:], gone[:], sc[:], ALU.is_lt))
            link(dve.tensor_copy(selb[:], sel[:]))
            for t in range(1, NT):
                link(dve.tensor_tensor(before[:, t, :], before[:, t - 1, :], selb[:, t - 1, :], ALU.add))
            dve.tensor_tensor(wt[:], score[:], sel[:], ALU.mult).then_inc(sel_done, 1)
            dve.wait_ge(sel_done, 1)
            link(dve.tensor_reduce(wsum[:], wt[:], AX.X, ALU.add))
            link(dve.tensor_scalar(wsum[:], wsum[:], 1e-20, None, ALU.add))
            link(dve.reciprocal(wsum[:], wsum[:]))
            link(dve.tensor_tensor(wt[:], wt[:], wsum[:].unsqueeze(2).to_broadcast([P, NT, E0]), ALU.mult))
            link(dve.tensor_scalar(wt[:], wt[:], SCALE0, None, ALU.mult))
            link(dve.tensor_copy(val[:, :, 1, :], wt[:]))
            link(dve.tensor_tensor(val[:, :, 2, :], wt[:], val[:, :, 1, :], ALU.subtract))
            link(dve.tensor_copy(val[:, :, 0, :], tok[:].unsqueeze(2).to_broadcast([P, NT, E0])))
            dve.wait_ge(pos_done, 1)
            link(dve.tensor_scalar(slot[:], lg[:], float(CAP) - 0.5, None, ALU.is_lt))
            link(dve.tensor_tensor(sel[:], sel[:], slot[:], ALU.mult))
            link(dve.tensor_tensor(slot[:], lg[:], slot1[:].unsqueeze(1).to_broadcast([P, NT, E0]), ALU.add))
            link(dve.tensor_tensor(slot[:], slot[:], sel[:], ALU.mult))
            for t in range(NT):
                ins = dve.max(mine[:, t, :], slot[:, t, :])
                if t == NT - 1:
                    link(ins)
            link(dve.tensor_scalar(empty[:], mine[:], 0.0, float(NONE + 1), ALU.is_equal, ALU.mult))
            link(dve.tensor_tensor(cpos[:], mine[:], empty[:], ALU.add))
            dve.tensor_scalar(idx[:], cpos[:], -1.0, None, ALU.add).then_inc(idx_done, 1)
            dve.wait_ge(idx_done, 1)
            link(dve.tensor_scalar(cidx[:], idx[:], CAP - 1, None, ALU.bitwise_and))
            link(dve.tensor_copy(cpos[:], cidx[:]))
            link(dve.tensor_tensor(cpos[:], cpos[:], empty[:], ALU.add))

            def one_hots(tl):
                if tl.after(2):
                    dve.wait_ge(spread_done, tl.times(1, -1))
                here = bass.ds(tl.t, 1)

                def of(a):
                    return a[:, here].rearrange("p o k -> p (o k)")

                dve.tensor_tensor(onec[tl.par][:], iota[:].unsqueeze(1).to_broadcast([P, K0, CAP]),
                                  of(cpos).unsqueeze(2).to_broadcast([P, K0, CAP]), ALU.is_equal
                                  ).then_inc(onec_done, 1)
                if tl.after(1):
                    dve.wait_ge(ev_done, tl.times(1, 0))
                dve.tensor_tensor(onee[:], of(slot).unsqueeze(1).to_broadcast([P, K0, E0]),
                                  of(mine).unsqueeze(2).to_broadcast([P, K0, E0]), ALU.is_equal
                                  ).then_inc(onee_done, 1)
                dve.wait_ge(onee_done, tl.times(1, 1))
                dve.tensor_tensor(ev[tl.par][:], onee[:].unsqueeze(2).to_broadcast([P, K0, 3, E0]),
                                  val[:, here].rearrange("p o v e -> p (o v) e").unsqueeze(1)
                                  .to_broadcast([P, K0, 3, E0]), ALU.mult).then_inc(ev_done, 1)

            tile_steps(dve, one_hots, 0, NT - 1)
            dve.wait_ge(spread_done, NT)
            link(dve.tensor_copy(stage[:].rearrange("p v e -> p (v e)"), up[:, 0, 0:3 * E0]))
            link(dve.tensor_copy(slot_ids[:], stage[:, 0, :]))
            link(dve.tensor_tensor(slot_w[:], stage[:, 1, :], stage[:, 2, :], ALU.add))


def experts(nc, gs, xn2, w, slot_ids, slot_w, y_out):
    ctx = ExitStack()
    with ctx:
        def sb(name, shape, dt=F32):
            return ctx.enter_context(nc.sbuf_tensor("e_" + name, shape, dt))

        def ps(name, shape):
            return ctx.enter_context(nc.psum_tensor("e_" + name, shape, F32))

        ident = sb("ident", [P, P])
        gu = [sb(f"gu{i}", [P, KC, 2, I0]) for i in range(2)]
        dn = [sb(f"dn{i}", [I0, D]) for i in range(2)]
        ids = [sb(f"ids{i}", [P, 1], U32) for i in range(2)]
        x = [sb(f"x{i}", [P, D]) for i in range(2)]
        xT = [sb(f"xT{i}", [P, KC, P]) for i in range(2)]
        sg = [sb(f"sg{i}", [I0, P]) for i in range(2)]
        h = [sb(f"h{i}", [I0, P]) for i in range(2)]
        y = [sb(f"y{i}", [P, D]) for i in range(2)]
        pt = [ps(f"pt{i}", [P, KC, P]) for i in range(2)]
        pg = [ps(f"pg{i}", [P, 2, P]) for i in range(2)]
        py = [ps(f"py{i}", [P, D]) for i in range(2)]

        ident_in = gs("e_ident_in")
        gu_in = [gs(f"e_gu_in{i}") for i in range(2)]
        dn_in = [gs(f"e_dn_in{i}") for i in range(2)]
        ids_done = gs("e_ids")
        x_in = [gs(f"e_x_in{i}") for i in range(2)]
        turned = gs("e_turned")
        xT_done = gs("e_xT")
        up_done = gs("e_up")
        silu_done = gs("e_silu")
        h_done = gs("e_h")
        down_done = gs("e_down")
        y_done = gs("e_y")
        stored = [gs(f"e_stored{i}") for i in range(2)]
        passed = gs("e_pool_passed")
        block = ctx.enter_context(nc.Block())

        @block.sync
        def _(sp):
            sp.dma_start(ident[:], w["ident"]).then_inc(ident_in, 16)

            def load(e):
                at = e.t if isinstance(e.t, int) else sp.snap(e.t)
                used = e.times(1, -1) if isinstance(e.t, int) else sp.snap(e.times(1, -1))
                if e.after(2):
                    sp.wait_ge(up_done, used)
                sp.dma_start(gu[e.par][:], w["gu"][bass.ds(at, 1)].rearrange("o p c g i -> p (o c) g i")
                             ).then_inc(gu_in[e.par], 16)
                if e.after(2):
                    sp.wait_ge(down_done, used)
                sp.dma_start(dn[e.par][:], w["dn"][bass.ds(at, 1)].rearrange("o i d -> i (o d)")
                             ).then_inc(dn_in[e.par], 16)

            tile_steps(sp, load, 0, E0 - 1)

        @block.gpsimd
        def _(pool):
            held = Held(pool, passed)

            def gather(e):
                if e.after(2):
                    held.wait_ge(x_in[e.par], e.half * 16)
                    held.wait_ge(turned, e.times(1, -1))
                pool.tensor_copy(ids[e.par][:], slot_ids[:, bass.ds(e.t, 1)]).then_inc(ids_done, 1)
                held.wait_ge(ids_done, e.times(1, 1))
                pool.indirect_dma_start(x[e.par][:], None, xn2, bass.IndirectOffsetOnAxis(ap=ids[e.par][:, 0:1], axis=0),
                                        bounds_check=T - 1, oob_is_err=False).then_inc(x_in[e.par], 16)

            tile_steps(pool, gather, 0, E0 - 1)

        @block.tensor
        def _(pe):
            pe.wait_ge(ident_in, 16)

            def turn(e):
                pe.wait_ge(x_in[e.par], e.half * 16 + 16)
                if e.after(2):
                    pe.wait_ge(xT_done, e.times(1, -1))
                for c in range(KC):
                    mm = pe.transpose(pt[e.par][:, c, :], x[e.par][:, c * P:(c + 1) * P], ident[:])
                mm.then_inc(turned, 1)

            def up(e):
                pe.wait_ge(gu_in[e.par], e.half * 16 + 16)
                pe.wait_ge(xT_done, e.times(1, 1))
                if e.after(2):
                    pe.wait_ge(h_done, e.times(1, -1))
                for g in range(2):
                    for c in range(KC):
                        mm = pe.matmul(pg[e.par][0:I0, g, :], gu[e.par][:, c, g, :], xT[e.par][:, c, :],
                                       start=(c == 0), stop=(c == KC - 1))
                mm.then_inc(up_done, 1)

            def down(e):
                pe.wait_ge(dn_in[e.par], e.half * 16 + 16)
                pe.wait_ge(h_done, e.times(1, 1))
                if e.after(2):
                    pe.wait_ge(y_done, e.times(1, -1))
                pe.matmul(py[e.par][:], h[e.par][:], dn[e.par][:], start=True, stop=True).then_inc(down_done, 1)

            def step(e, ahead=True):
                if ahead:
                    turn(e.plus(1))
                up(e)
                if e.after(1):
                    down(Tile(e.half, 0) if e.par else Tile(e.half - 1, 1))

            turn(Tile(0, 0))
            tile_steps(pe, step, 0, E0 - 3)
            step(Tile(E0 // 2 - 1, 0))
            step(Tile(E0 // 2 - 1, 1), ahead=False)
            down(Tile(E0 // 2 - 1, 1))

        @block.scalar
        def _(act):
            def rows(e):
                act.wait_ge(turned, e.times(1, 1))
                if e.after(2):
                    act.wait_ge(up_done, e.times(1, -1))
                act.copy(xT[e.par][:], pt[e.par][:]).then_inc(xT_done, 1)

            def silu(e):
                act.wait_ge(up_done, e.times(1, 1))
                if e.after(2):
                    act.wait_ge(h_done, e.times(1, -1))
                act.activation(sg[e.par][:], pg[e.par][0:I0, 0, :], ACT.Silu).then_inc(silu_done, 1)

            def store(e):
                act.wait_ge(y_done, e.times(1, 1))
                act.dma_start(y_out[bass.ds(e.t * CAP, CAP), :], y[e.par][:]).then_inc(stored[e.par], 16)

            def step(e, ahead=True):
                if ahead:
                    rows(e.plus(1))
                silu(e)
                if e.after(2):
                    store(Tile(e.half - 1, e.par))

            rows(Tile(0, 0))
            tile_steps(act, step, 0, E0 - 3)
            step(Tile(E0 // 2 - 1, 0))
            step(Tile(E0 // 2 - 1, 1), ahead=False)
            for par in range(2):
                store(Tile(E0 // 2 - 1, par))
            for par in range(2):
                act.wait_ge(stored[par], 16 * (E0 // 2))

        @block.vector
        def _(dve):
            def inner(e):
                dve.wait_ge(silu_done, e.times(1, 1))
                if e.after(2):
                    dve.wait_ge(down_done, e.times(1, -1))
                dve.tensor_tensor(h[e.par][:], sg[e.par][:], pg[e.par][0:I0, 1, :], ALU.mult).then_inc(h_done, 1)

            def weigh(e):
                dve.wait_ge(down_done, e.times(1, 1))
                if e.after(2):
                    dve.wait_ge(stored[e.par], e.half * 16)
                dve.tensor_scalar(y[e.par][:], py[e.par][:], slot_w[:, bass.ds(e.t, 1)], None, ALU.mult
                                  ).then_inc(y_done, 1)

            def step(e):
                inner(e)
                if e.after(1):
                    weigh(Tile(e.half, 0) if e.par else Tile(e.half - 1, 1))

            tile_steps(dve, step, 0, E0 - 1)
            weigh(Tile(E0 // 2 - 1, 1))


def combine(nc, gs, w, x1, shared, idx, y_in, x2_out):
    ctx = ExitStack()
    with ctx:
        def sb(name, shape, dt=F32):
            return ctx.enter_context(nc.sbuf_tensor("c_" + name, shape, dt))

        gate = sb("gate", [P, 1])
        tg = sb("tg", [P, 1])
        ix = [sb(f"ix{i}", [P, K0], U32) for i in range(2)]
        rows = [sb(f"rows{i}", [P, K0, D]) for i in range(2)]
        x = [sb(f"x{i}", [P, D]) for i in range(2)]
        sh = [sb(f"sh{i}", [P, D]) for i in range(2)]
        total = sb("total", [P, D])
        x2 = [sb(f"x2{i}", [P, D]) for i in range(2)]
        gate_in, tanh_done, passed = gs("c_gate_in"), gs("c_tanh"), gs("c_passed")
        ix_in = [gs(f"c_ix_in{i}") for i in range(2)]
        x_in = [gs(f"c_x_in{i}") for i in range(2)]
        rows_in = [gs(f"c_rows_in{i}") for i in range(2)]
        summed, added, x2_done = gs("c_summed"), gs("c_added"), gs("c_x2")
        stored = [gs(f"c_stored{i}") for i in range(2)]
        block = ctx.enter_context(nc.Block())

        @block.sync
        def _(sp):
            sp.dma_start(gate[:], w["g01"]).then_inc(gate_in, 16)

            def load(tl):
                row = tl.t * P if isinstance(tl.t, int) else sp.snap(tl.t * P)
                used = tl.times(1, -1) if isinstance(tl.t, int) else sp.snap(tl.times(1, -1))
                if tl.after(2):
                    sp.wait_ge(x2_done, used)
                sp.dma_start(ix[tl.par][:], idx[bass.ds(row, P), :]).then_inc(ix_in[tl.par], 16)
                sp.dma_start(x[tl.par][:], x1[bass.ds(row, P), :]).then_inc(x_in[tl.par], 16)
                sp.dma_start(sh[tl.par][:], shared[bass.ds(row, P), :]).then_inc(x_in[tl.par], 16)

            tile_steps(sp, load, 0, NT - 1)

        @block.gpsimd
        def _(pool):
            held = Held(pool, passed)

            def gather(tl):
                held.wait_ge(ix_in[tl.par], tl.half * 16 + 16)
                if tl.after(2):
                    held.wait_ge(summed, tl.times(1, -1))
                for k in range(K0):
                    pool.indirect_dma_start(rows[tl.par][:, k, :], None, y_in,
                                            bass.IndirectOffsetOnAxis(ap=ix[tl.par][:, k:k + 1], axis=0),
                                            bounds_check=NONE, oob_is_err=False).then_inc(rows_in[tl.par], 16)

            tile_steps(pool, gather, 0, NT - 1)

        @block.scalar
        def _(act):
            act.wait_ge(gate_in, 16)
            act.activation(tg[:], gate[:], ACT.Tanh).then_inc(tanh_done, 1)

            def store(tl):
                act.wait_ge(x2_done, tl.times(1, 1))
                act.dma_start(x2_out[bass.ds(tl.t * P, P), :], x2[tl.par][:]).then_inc(stored[tl.par], 16)

            tile_steps(act, store, 0, NT - 1)
            for par in range(2):
                act.wait_ge(stored[par], 16 * (NT // 2))

        @block.vector
        def _(dve):
            dve.wait_ge(tanh_done, 1)

            def step(tl):
                dve.wait_ge(rows_in[tl.par], tl.half * (16 * K0) + 16 * K0)
                if tl.after(1):
                    dve.wait_ge(x2_done, tl.times(1, 0))
                dve.tensor_reduce(total[:], rows[tl.par][:].rearrange("p k d -> p d k"), AX.X, ALU.add
                                  ).then_inc(summed, 1)
                dve.wait_ge(summed, tl.times(1, 1))
                dve.wait_ge(x_in[tl.par], tl.half * 32 + 32)
                dve.tensor_tensor(total[:], total[:], sh[tl.par][:], ALU.add).then_inc(added, 1)
                dve.wait_ge(added, tl.times(1, 1))
                if tl.after(2):
                    dve.wait_ge(stored[tl.par], tl.half * 16)
                dve.scalar_tensor_tensor(x2[tl.par][:], total[:], tg[:, 0:1], x[tl.par][:], ALU.mult, ALU.add
                                         ).then_inc(x2_done, 1)

            tile_steps(dve, step, 0, NT - 1)


H1, HD1, KVC, QC, R1, BACK = 16, 128, 64, 96, 64, 8
HP = H1 // 2
NEG = -1e30


def layer1_keys(nc, gs, w, keysT, ropeT, keysN, aw, bp):
    ctx = ExitStack()
    with ctx:
        def sb(name, shape, dt=F32):
            return ctx.enter_context(nc.sbuf_tensor("k_" + name, shape, dt))

        def ps(name, shape, dt=F32):
            return ctx.enter_context(nc.psum_tensor("k_" + name, shape, dt))

        ident = sb("ident", [P, P])
        ctx_all = sb("ctx", [P, NT, D])
        ctxT = sb("ctxT", [P, KC, T])
        wkvc2 = sb("wkvc2", [P, KC, 2 * KVC])
        wkr = sb("wkr", [KVC, 2, 2 * R1])
        kcos, ksin = sb("kcos", [P, S]), sb("ksin", [P, S])
        wuqT = sb("wuqT", [HD1, H1, QC])
        wukT = sb("wukT", [HD1, H1, KVC])
        wuvT = sb("wuvT", [HD1, H1, KVC])
        wo = sb("wo", [HD1, H1, D])
        kT = sb("kT", [P, T])
        part = sb("part", [P, 512])
        part2 = sb("part2", [P, 512])
        rT = sb("rT", [P, T])
        kN = sb("kN", [P, B, KVC])
        ctx_in = gs("k_ctx_in")
        const_in = gs("k_const_in")
        kT_mm, kT_done = gs("k_kT_mm"), gs("k_kT")
        rope_mm, rope_a, rope_b, rope_done = gs("k_rope_mm"), gs("k_rope_a"), gs("k_rope_b"), gs("k_rope")
        kN_mm, kN_done = gs("k_kN_mm"), gs("k_kN")
        aw_mm, aw_done = gs("k_aw_mm"), gs("k_aw")
        bp_mm, bp_done = gs("k_bp_mm"), gs("k_bp")
        stored = gs("k_stored")
        block = ctx.enter_context(nc.Block())
        turn_pe, turn_act, xT_out, fills = turned_tiles(nc, sb, ps, gs, "k", ctx_all, ctxT, block)
        bank = [ps(f"bank{i}", [P, 512]) for i in range(4)]
        consts = [(ident, w["ident"]), (wkvc2, w["wkvc2"]), (wkr, w["wkr"]), (kcos, w["kcos"]), (ksin, w["ksin"]),
                  (wuqT, w["wuqT"]), (wukT, w["wukT"]), (wuvT, w["wuvT"]), (wo, w["wo1"])]

        @block.sync
        def _(sp):
            for dst, src in consts:
                sp.dma_start(dst[:], src).then_inc(const_in, 16)
            sp.dma_start(ctx_all[:], w["ctx"].rearrange("(t p) d -> p t d", p=P)).then_inc(ctx_in, 16)
            sp.wait_ge(kT_done, 4)
            sp.dma_start(keysT, kT[:]).then_inc(stored, 16)
            sp.wait_ge(rope_done, 4)
            sp.dma_start(ropeT, rT[:]).then_inc(stored, 16)
            sp.wait_ge(kN_done, 4)
            sp.dma_start(keysN, kN[:].rearrange("p b l -> p (b l)")).then_inc(stored, 16)
            sp.wait_ge(stored, 48)

        @block.tensor
        def _(pe):
            pe.wait_ge(const_in, 16 * len(consts))
            pe.wait_ge(ctx_in, 16)
            turn_pe(pe, ident[:])
            pe.wait_ge(xT_out, fills)
            for q in range(4):
                if q >= 2:
                    pe.wait_ge(kT_done, q - 1)
                for c in range(KC):
                    mm = pe.matmul(bank[q % 2][:], wkvc2[:, c, :], ctxT[:, c, q * 512:(q + 1) * 512],
                                   start=(c == 0), stop=(c == KC - 1))
                mm.then_inc(kT_mm, 1)
            for q in range(4):
                pe.wait_ge(kT_done, q + 1)
                if q:
                    pe.wait_ge(rope_b, q)
                for n in range(2):
                    mm = pe.matmul(bank[2 + n][:], wkr[:, n, :], kT[0:KVC, q * 512:(q + 1) * 512],
                                   start=True, stop=True)
                mm.then_inc(rope_mm, 1)
            pe.wait_ge(kT_done, 4)
            for q in range(4):
                if q >= 2:
                    pe.wait_ge(kN_done, q - 1)
                for b in range(8 * q, 8 * q + 8):
                    for r in range(2):
                        rows = slice(64 * r, 64 * r + 64)
                        mm = pe.matmul(bank[q % 2][rows, (b % 8) * KVC:(b % 8 + 1) * KVC], kT[rows, b * S:(b + 1) * S],
                                       ident[rows, 64 * r:64 * r + KVC], start=True, stop=True)
                mm.then_inc(kN_mm, 1)
            for n in range(2):
                pe.wait_ge(kN_done, 3 + n)
                for h in range(8 * n, 8 * n + 8):
                    mm = pe.matmul(bank[n][0:QC, (h % 8) * KVC:(h % 8 + 1) * KVC], wuqT[:, h, :], wukT[:, h, :],
                                   start=True, stop=True)
                mm.then_inc(aw_mm, 1)
            for n in range(HP // 2):
                if n < 2:
                    pe.wait_ge(aw_done, n + 1)
                else:
                    pe.wait_ge(bp_done, n - 1)
                for hp in (2 * n, 2 * n + 1):
                    for r in range(2):
                        mm = pe.matmul(bank[n % 2][64 * r:64 * r + 64, (hp % 2) * D:(hp % 2 + 1) * D],
                                       wuvT[:, 2 * hp + r, :], wo[:, 2 * hp + r, :], start=True, stop=True)
                mm.then_inc(bp_mm, 1)

        @block.scalar
        def _(act):
            turn_act(act)
            for q in range(4):
                act.wait_ge(kT_mm, q + 1)
                act.copy(kT[:, q * 512:(q + 1) * 512], bank[q % 2][:]).then_inc(kT_done, 1)
            for q in range(4):
                act.wait_ge(kN_mm, q + 1)
                act.copy(kN[:, 8 * q:8 * q + 8, :].rearrange("p b l -> p (b l)"), bank[q % 2][:]).then_inc(kN_done, 1)
            for n in range(2):
                act.wait_ge(aw_mm, n + 1)
                act.copy(aw[:, 4 * n:4 * n + 4, :].rearrange("p a b -> p (a b)"), bank[n][0:QC, :]).then_inc(aw_done, 1)
            for n in range(HP // 2):
                act.wait_ge(bp_mm, n + 1)
                act.copy(bp[:, 2 * n:2 * n + 2, :].rearrange("p a b -> p (a b)"), bank[n % 2][:]).then_inc(bp_done, 1)

        @block.vector
        def _(dve):
            dve.wait_ge(const_in, 16 * len(consts))
            for q in range(4):
                dve.wait_ge(rope_mm, q + 1)
                if q:
                    dve.wait_ge(rope_done, q)

                def at_positions(table):
                    return table[:].unsqueeze(1).to_broadcast([P, 8, S])

                dve.tensor_tensor(part[:].rearrange("p (b s) -> p b s", s=S),
                                  bank[2][:].rearrange("p (b s) -> p b s", s=S), at_positions(kcos), ALU.mult
                                  ).then_inc(rope_a, 1)
                dve.tensor_tensor(part2[:].rearrange("p (b s) -> p b s", s=S),
                                  bank[3][:].rearrange("p (b s) -> p b s", s=S), at_positions(ksin), ALU.mult
                                  ).then_inc(rope_b, 1)
                dve.wait_ge(rope_a, q + 1)
                dve.wait_ge(rope_b, q + 1)
                dve.tensor_tensor(rT[:, q * 512:(q + 1) * 512], part[:], part2[:], ALU.add).then_inc(rope_done, 1)


def layer1_attention(nc, gs, w, xn_in, x2, keysT, ropeT, keysN, aw, bp, x3_out):
    ctx = ExitStack()
    with ctx:
        def sb(name, shape, dt=F32):
            return ctx.enter_context(nc.sbuf_tensor("b_" + name, shape, dt))

        def ps(name, shape, dt=F32):
            return ctx.enter_context(nc.psum_tensor("b_" + name, shape, dt))

        ident = sb("ident", [P, P])
        wdq = sb("wdq", [P, KC, QC])
        wqr = sb("wqr", [QC, H1, 2 * R1])
        qtab = sb("qtab", [P, S])
        keyno = sb("keyno", [P, S])
        seg = sb("seg", [P, NT])
        seg_i = sb("seg_i", [P, NT], mybir.dt.int32)
        gate, tg = sb("gate", [P, 1]), sb("tg", [P, 1])
        xn = [sb(f"xn{i}", [P, D]) for i in range(2)]
        x = [sb(f"x{i}", [P, D]) for i in range(2)]
        kT = [sb(f"kT{i}", [P, P]) for i in range(2)]
        rT = [sb(f"rT{i}", [P, P]) for i in range(2)]
        kN = [sb(f"kN{i}", [P, 2, KVC]) for i in range(2)]
        xT = sb("xT", [P, KC, P])
        qc = sb("qc", [QC, P])
        qn = sb("qn", [P, HP, P])
        qr = sb("qr", [P, H1, P])
        mask = sb("mask", [P, S])
        mask2 = sb("mask2", [P, S])
        s = sb("s", [P, 2, HP, S])
        top = sb("top", [P, H1])
        e = sb("e", [P, 2, HP, S])
        total = sb("total", [P, H1])
        p = sb("p", [P, HP, 2, S])
        pT = sb("pT", [P, HP, P])
        u = sb("u", [P, HP, 2, S])
        x3 = [sb(f"x3{i}", [P, D]) for i in range(2)]
        pa = ps("pa", [P, 512])
        pb = [ps(f"pb{i}", [P, 4, P]) for i in range(2)]
        pc = [ps(f"pc{i}", [P, HP, S]) for i in range(2)]
        pd = [ps(f"pd{i}", [P, 4, P]) for i in range(2)]
        pu = ps("pu", [P, HP, S])

        const_in = gs("b_const_in")
        seg_done, tanh_done = gs("b_seg"), gs("b_tanh")
        xn_in_s = [gs(f"b_xn_in{i}") for i in range(2)]
        x_in = [gs(f"b_x_in{i}") for i in range(2)]
        k_in = [gs(f"b_k_in{i}") for i in range(2)]
        xT_mm, xT_done = gs("b_xT_mm"), gs("b_xT")
        qc_mm, qc_done = gs("b_qc_mm"), gs("b_qc")
        qn_mm, qn_done = gs("b_qn_mm"), gs("b_qn")
        qr_mm, qr_done = gs("b_qr_mm"), gs("b_qr")
        s_mm, s_done = gs("b_s_mm"), gs("b_s")
        mask_steps, top_done, less_done = gs("b_mask"), gs("b_top"), gs("b_less")
        exp_done, total_steps, p_done = gs("b_exp"), gs("b_total"), gs("b_p")
        pT_mm, pT_done = gs("b_pT_mm"), gs("b_pT")
        u_mm, u_done = gs("b_u_mm"), gs("b_u")
        o_mm, x3_done = gs("b_o_mm"), gs("b_x3")
        stored = [gs(f"b_stored{i}") for i in range(2)]
        pe_passed, pool_passed = gs("b_pe_passed"), gs("b_pool_passed")
        block = ctx.enter_context(nc.Block())
        consts = [(ident, w["ident"]), (wdq, w["wdq"]), (wqr, w["wqr"]), (qtab, w["qtab"]), (keyno, w["keyno"]),
                  (seg_i, w["seg"]), (gate, w["g10"])]

        @block.sync
        def _(sp):
            for dst, src in consts:
                sp.dma_start(dst[:], src).then_inc(const_in, 16)

            def load(tl):
                fixed = isinstance(tl.t, int)
                row = tl.t * P if fixed else sp.snap(tl.t * P)
                used = tl.times(1, -1) if fixed else sp.snap(tl.times(1, -1))
                if tl.after(2):
                    sp.wait_ge(xT_mm, used)
                sp.dma_start(xn[tl.par][:], xn_in[bass.ds(row, P), :]).then_inc(xn_in_s[tl.par], 16)
                if tl.after(2):
                    sp.wait_ge(x3_done, used)
                sp.dma_start(x[tl.par][:], x2[bass.ds(row, P), :]).then_inc(x_in[tl.par], 16)
                sp.dma_start(kT[tl.par][:], keysT[:, bass.ds(row, P)]).then_inc(k_in[tl.par], 16)
                sp.dma_start(rT[tl.par][:], ropeT[:, bass.ds(row, P)]).then_inc(k_in[tl.par], 16)
                sp.dma_start(kN[tl.par][:].rearrange("p b l -> p (b l)"), keysN[:, bass.ds(row, P)]
                             ).then_inc(k_in[tl.par], 16)

            tile_steps(sp, load, 0, NT - 1)

        @block.tensor
        def _(pe):
            held = Held(pe, pe_passed)
            pe.wait_ge(const_in, 16 * len(consts))

            def front(tl):
                pe.wait_ge(xn_in_s[tl.par], tl.half * 16 + 16)
                if tl.after(1):
                    pe.wait_ge(qc_done, tl.times(1, 0))
                if tl.after(2):
                    pe.wait_ge(x3_done, tl.times(1, -1))
                for c in range(KC):
                    mm = pe.transpose(pa[:, c * P:(c + 1) * P], xn[tl.par][:, c * P:(c + 1) * P], ident[:])
                mm.then_inc(xT_mm, 1)
                pe.wait_ge(xT_done, tl.times(1, 1))
                for c in range(KC):
                    mm = pe.matmul(pa[0:QC, 2 * P:3 * P], wdq[:, c, :], xT[:, c, :], start=(c == 0), stop=(c == KC - 1))
                mm.then_inc(qc_mm, 1)
                pe.wait_ge(qc_done, tl.times(1, 1))
                for f in range(2):
                    if tl.after(1):
                        pe.wait_ge(qr_done, tl.times(4, f - 1))
                    for j in range(4):
                        mm = pe.matmul(pb[f][:, j, :], aw[:, 4 * f + j, :], qc[:], start=True, stop=True)
                    mm.then_inc(qn_mm, 1)
                for f in range(4):
                    if f < 2:
                        pe.wait_ge(qn_done, tl.times(2, f + 1))
                    else:
                        pe.wait_ge(qr_done, tl.times(4, f - 1))
                    for j in range(4):
                        mm = pe.matmul(pb[f % 2][:, j, :], wqr[:, 4 * f + j, :], qc[:], start=True, stop=True)
                    mm.then_inc(qr_mm, 1)
                pe.wait_ge(qr_done, tl.times(4, 4))
                pe.wait_ge(k_in[tl.par], tl.half * 48 + 48)
                if tl.after(1):
                    pe.wait_ge(s_done, tl.times(2, 0))
                for hp in range(HP):
                    for r in range(2):
                        rows = slice(64 * r, 64 * r + 64)
                        for b in range(2):
                            own = slice(64 * b, 64 * b + 64)
                            pe.matmul(pc[r][own, hp, :], qr[:, 2 * hp + r, own], rT[tl.par][:, own],
                                      start=True, stop=False)
                            mm = pe.matmul(pc[r][own, hp, :], qn[rows, hp, own], kT[tl.par][rows, own],
                                           start=False, stop=True)
                mm.then_inc(s_mm, 1)

            def back(tl):
                pe.wait_ge(p_done, tl.times(2, 2))
                for f in range(2):
                    if tl.after(1):
                        pe.wait_ge(pT_done, tl.times(2, f - 1))
                    for j in range(4):
                        hp = 4 * f + j
                        mm = pe.transpose(pd[f][:, j, :], p[:, hp].rearrange("p r k -> p (r k)"), ident[:])
                    mm.then_inc(pT_mm, 1)
                held.wait_ge(pT_done, tl.times(2, 2))
                for b in range(2):
                    if b or tl.after(1):
                        held.wait_ge(u_done, tl.times(2, b))
                    for r in range(2):
                        rows = slice(64 * r, 64 * r + 64)
                        mm = pe.matmul(pu[rows, :, :], kN[tl.par][rows, b, :], pT[rows, :, 64 * b:64 * b + 64],
                                       start=True, stop=True)
                    mm.then_inc(u_mm, 1)
                pe.wait_ge(u_done, tl.times(2, 2))
                for hp in range(HP):
                    mm = pe.matmul(pa[:, 0:D], u[:, hp].rearrange("p b q -> p (b q)"), bp[:, hp, :],
                                   start=(hp == 0), stop=(hp == HP - 1))
                mm.then_inc(o_mm, 1)

            def step(tl, ahead=True):
                if ahead:
                    front(tl.plus(1))
                back(tl)

            front(Tile(0, 0))
            tile_steps(pe, step, 0, NT - 3)
            step(Tile(NT // 2 - 1, 0))
            step(Tile(NT // 2 - 1, 1), ahead=False)

        @block.scalar
        def _(act):
            act.wait_ge(const_in, 16 * len(consts))
            act.activation(tg[:], gate[:], ACT.Tanh).then_inc(tanh_done, 1)

            def front(tl):
                act.wait_ge(xT_mm, tl.times(1, 1))
                if tl.after(1):
                    act.wait_ge(qc_mm, tl.times(1, 0))
                act.copy(xT[:].rearrange("p c t -> p (c t)"), pa[:, 0:2 * P]).then_inc(xT_done, 1)
                act.wait_ge(qc_mm, tl.times(1, 1))
                if tl.after(1):
                    act.wait_ge(qr_mm, tl.times(4, 0))
                act.copy(qc[:], pa[0:QC, 2 * P:3 * P]).then_inc(qc_done, 1)
                for f in range(2):
                    act.wait_ge(qn_mm, tl.times(2, f + 1))
                    if f == 0 and tl.after(1):
                        act.wait_ge(s_mm, tl.times(1, 0))
                    act.copy(qn[:, 4 * f:4 * f + 4, :], pb[f][:]).then_inc(qn_done, 1)

            def exponent(tl):
                act.wait_ge(less_done, tl.times(1, 1))
                if tl.after(1):
                    act.wait_ge(p_done, tl.times(2, 0))
                act.activation(e[:], s[:], ACT.Exp, scale=float(HD1 + R1) ** -0.5).then_inc(exp_done, 1)

            def back(tl):
                for f in range(2):
                    act.wait_ge(pT_mm, tl.times(2, f + 1))
                    if f == 0 and tl.after(1):
                        act.wait_ge(u_mm, tl.times(2, 0))
                    act.copy(pT[:, 4 * f:4 * f + 4, :], pd[f][:]).then_inc(pT_done, 1)
                for b in range(2):
                    act.wait_ge(u_mm, tl.times(2, b + 1))
                    if b == 0 and tl.after(1):
                        act.wait_ge(o_mm, tl.times(1, 0))
                    act.copy(u[:, :, b, :], pu[:]).then_inc(u_done, 1)

            def store(tl):
                act.wait_ge(x3_done, tl.times(1, 1))
                act.dma_start(x3_out[bass.ds(tl.t * P, P), :], x3[tl.par][:]).then_inc(stored[tl.par], 16)

            def step(tl, ahead=True):
                if tl.after(1):
                    store(Tile(tl.half, 0) if tl.par else Tile(tl.half - 1, 1))
                if ahead:
                    front(tl.plus(1))
                back(tl)
                if ahead:
                    exponent(tl.plus(1))

            front(Tile(0, 0))
            exponent(Tile(0, 0))
            tile_steps(act, step, 0, NT - 3)
            step(Tile(NT // 2 - 1, 0))
            step(Tile(NT // 2 - 1, 1), ahead=False)
            store(Tile(NT // 2 - 1, 1))
            for par in range(2):
                act.wait_ge(stored[par], 16 * (NT // 2))

        @block.gpsimd
        def _(pool):
            held = Held(pool, pool_passed)

            def step(tl):
                held.wait_ge(top_done, tl.times(1, 1))
                heads = s[:].rearrange("p r a k -> p (r a) k")
                pool.tensor_tensor(heads, heads, top[:].unsqueeze(2).to_broadcast([P, H1, S]), ALU.subtract
                                   ).then_inc(less_done, 1)
                held.wait_ge(total_steps, tl.times(2, 2))
                if tl.after(1):
                    held.wait_ge(pT_mm, tl.times(2, 0))
                for r in range(2):
                    pool.tensor_tensor(p[:, :, r, :], e[:, r], total[:, r * HP:(r + 1) * HP].unsqueeze(2)
                                       .to_broadcast([P, HP, S]), ALU.mult).then_inc(p_done, 1)

            tile_steps(pool, step, 0, NT - 1)

        @block.vector
        def _(dve):
            dve.wait_ge(const_in, 16 * len(consts))
            dve.wait_ge(tanh_done, 1)
            dve.tensor_copy(seg[:], seg_i[:]).then_inc(seg_done, 1)
            dve.wait_ge(seg_done, 1)

            def front(tl):
                for f in range(4):
                    dve.wait_ge(qr_mm, tl.times(4, f + 1))
                    if f == 0 and tl.after(1):
                        dve.wait_ge(s_mm, tl.times(1, 0))
                    dve.tensor_tensor(qr[:, 4 * f:4 * f + 4, :].rearrange("p h (b q) -> p (h b) q", q=S),
                                      pb[f % 2][:].rearrange("p h (b q) -> p (h b) q", q=S),
                                      qtab[:].unsqueeze(1).to_broadcast([P, 8, S]), ALU.mult).then_inc(qr_done, 1)
                if tl.after(1):
                    dve.wait_ge(s_done, tl.times(2, 0))
                step = Chain(dve, mask_steps, tl, 4)
                mine = seg[:, bass.ds(tl.t, 1)]
                step(dve.tensor_scalar(mask[:], keyno[:], mine, 0.0, ALU.subtract, ALU.is_le))
                step(dve.tensor_scalar(mask2[:], keyno[:], mine, float(-BACK), ALU.subtract, ALU.is_ge))
                step(dve.tensor_tensor(mask[:], mask[:], mask2[:], ALU.mult))
                step(dve.tensor_scalar(mask[:], mask[:], 1.0, -NEG, ALU.subtract, ALU.mult))
                step.close()
                dve.wait_ge(s_mm, tl.times(1, 1))
                if tl.after(1):
                    dve.wait_ge(exp_done, tl.times(1, 0))
                for r in range(2):
                    dve.tensor_tensor(s[:, r], pc[r][:], mask[:].unsqueeze(1).to_broadcast([P, HP, S]), ALU.add
                                      ).then_inc(s_done, 1)
                dve.wait_ge(s_done, tl.times(2, 2))
                dve.tensor_reduce(top[:], s[:].rearrange("p r a k -> p (r a) k"), AX.X, ALU.max).then_inc(top_done, 1)

            def sums(tl):
                dve.wait_ge(exp_done, tl.times(1, 1))
                if tl.after(1):
                    dve.wait_ge(p_done, tl.times(2, 0))
                dve.tensor_reduce(total[:], e[:].rearrange("p r a k -> p (r a) k"), AX.X, ALU.add
                                  ).then_inc(total_steps, 1)
                dve.wait_ge(total_steps, tl.times(2, 1))
                dve.reciprocal(total[:], total[:]).then_inc(total_steps, 1)

            def add(tl):
                dve.wait_ge(o_mm, tl.times(1, 1))
                dve.wait_ge(x_in[tl.par], tl.half * 16 + 16)
                if tl.after(2):
                    dve.wait_ge(stored[tl.par], tl.half * 16)
                dve.scalar_tensor_tensor(x3[tl.par][:], pa[:, 0:D], tg[:, 0:1], x[tl.par][:], ALU.mult, ALU.add
                                         ).then_inc(x3_done, 1)

            def step(tl, ahead=True):
                if ahead:
                    front(tl.plus(1))
                add(tl)
                if ahead:
                    sums(tl.plus(1))

            front(Tile(0, 0))
            sums(Tile(0, 0))
            tile_steps(dve, step, 0, NT - 3)
            step(Tile(NT // 2 - 1, 0))
            step(Tile(NT // 2 - 1, 1), ahead=False)


E1, TOP1, I1 = 8, 2, 176
EW = E1 + 1
MT = -(-EW * I1 // P)


def layer1_experts(nc, gs, w, xn_all, x3, out):
    ctx = ExitStack()
    with ctx:
        def sb(name, shape, dt=F32):
            return ctx.enter_context(nc.sbuf_tensor("f_" + name, shape, dt))

        def ps(name, shape, dt=F32):
            return ctx.enter_context(nc.psum_tensor("f_" + name, shape, dt))

        NB = 4
        TB = NT // NB
        ident = sb("ident", [P, P])
        identb = sb("identb", [P, P], BF16)
        gate, tg = sb("gate", [P, 1]), sb("tg", [P, 1])
        wr = sb("wr", [P, KC, E1])
        below = sb("below", [P, E1, E1])
        w1 = sb("w1", [P, KC, MT * P])
        w2 = sb("w2", [P, MT, D])
        spread = sb("spread", [32, MT, P], BF16)
        xT = sb("xT", [P, KC, T])
        logit = sb("logit", [P, NT, E1])
        top = sb("top", [P, NT])
        gt, eq = sb("gt", [P, NT, E1, E1]), sb("eq", [P, NT, E1, E1])
        rank = sb("rank", [P, NT, E1])
        share = sb("share", [P, NT, EW])
        left = sb("left", [P, NT, EW])
        parts = sb("parts", [P, NT, 32], BF16)
        shareT = sb("shareT", [32, T], BF16)
        hs = [sb(f"hs{i}", [P, 512]) for i in range(2)]
        hT = [sb(f"hT{i}", [P, MT, 512]) for i in range(2)]
        x = [sb(f"x{i}", [P, TB, D]) for i in range(2)]
        y = [sb(f"y{i}", [P, TB, D]) for i in range(2)]

        const_in, w_in = gs("f_const_in"), gs("f_w_in")
        tanh_done, logit_mm, less_done, exp_done = gs("f_tanh"), gs("f_logit_mm"), gs("f_less"), gs("f_exp")
        chain, parts_done = gs("f_steps"), gs("f_parts")
        share_mm, share_done = gs("f_share_mm"), gs("f_share")
        up_mm, silu_done, h_done = gs("f_up_mm"), gs("f_silu"), gs("f_h")
        down_mm, y_done = gs("f_down_mm"), gs("f_y")
        x_in = [gs(f"f_x_in{i}") for i in range(2)]
        stored = [gs(f"f_stored{i}") for i in range(2)]
        block = ctx.enter_context(nc.Block())
        turn_pe, turn_act, xT_out, fills = turned_tiles(nc, sb, ps, gs, "f", xn_all, xT, block)
        ph = [ps(f"ph{i}", [P, 512]) for i in range(2)]
        pw = [ps(f"pw{i}", [P, 512]) for i in range(2)]
        po = [ps(f"po{i}", [P, D]) for i in range(2)]
        consts = [(ident, w["ident"]), (identb, w["identb"]), (gate, w["g11"]), (wr, w["wr1"]), (below, w["below"]),
                  (spread, w["spread1"])]

        @block.sync
        def _(sp):
            for dst, src in consts:
                sp.dma_start(dst[:], src).then_inc(const_in, 16)
            sp.dma_start(w1[:], w["w1"]).then_inc(w_in, 16)
            sp.dma_start(w2[:], w["w2"]).then_inc(w_in, 16)

            def load(b):
                fixed = isinstance(b.t, int)
                row = b.t * 512 if fixed else sp.snap(b.t * 512)
                used = b.times(TB, -TB) if fixed else sp.snap(b.times(TB, -TB))
                if b.after(2):
                    sp.wait_ge(y_done, used)
                sp.dma_start(x[b.par][:], x3[bass.ds(row, 512), :].rearrange("(j p) d -> p j d", p=P)
                             ).then_inc(x_in[b.par], 16)

            tile_steps(sp, load, 0, NB - 1)

        @block.tensor
        def _(pe):
            pe.wait_ge(const_in, 16 * len(consts))
            turn_pe(pe, ident[:])
            pe.wait_ge(xT_out, fills)
            for t in range(NT):
                for c in range(KC):
                    mm = pe.matmul(po[0][:, t * E1:(t + 1) * E1], xT[:, c, t * P:(t + 1) * P], wr[:, c, :],
                                   start=(c == 0), stop=(c == KC - 1))
            mm.then_inc(logit_mm, 1)
            pe.wait_ge(parts_done, 1)
            for n in range(2):
                for j in range(8):
                    mm = pe.transpose(pw[n][0:32, :].bitcast(BF16)[:, j * P:(j + 1) * P], parts[:, 8 * n + j, :],
                                      identb[:])
                mm.then_inc(share_mm, 1)
            pe.wait_ge(share_done, 2)
            pe.wait_ge(w_in, 32)

            def up(b):
                tokens = bass.ds(b.t * 512, 512)
                for m in range(MT):
                    if m >= 2 or b.after(1):
                        pe.wait_ge(h_done, b.times(MT, m - 1))
                    for c in range(KC):
                        pe.matmul(ph[(b.par * MT + m) % 2][:], w1[:, c, m * P:(m + 1) * P], xT[:, c, tokens],
                                  start=(c == 0), stop=(c == KC - 1))
                    pe.matmul(pw[(b.par * MT + m) % 2][:], spread[:, m, :], shareT[:, tokens], start=True, stop=True
                              ).then_inc(up_mm, 1)

            def down(b):
                for j in range(TB):
                    pe.wait_ge(h_done, b.times(MT, MT))
                    if j >= 2 or b.after(1):
                        pe.wait_ge(y_done, b.times(TB, j - 1))
                    for m in range(MT):
                        mm = pe.matmul(po[j % 2][:], hT[b.par][:, m, j * P:(j + 1) * P], w2[:, m, :],
                                       start=(m == 0), stop=(m == MT - 1))
                    mm.then_inc(down_mm, 1)

            def step(b, ahead=True):
                if ahead:
                    up(b.plus(1))
                down(b)

            up(Tile(0, 0))
            step(Tile(0, 0))
            step(Tile(0, 1))
            step(Tile(1, 0))
            step(Tile(1, 1), ahead=False)

        @block.scalar
        def _(act):
            act.wait_ge(const_in, 16 * len(consts))
            act.activation(tg[:], gate[:], ACT.Tanh).then_inc(tanh_done, 1)
            turn_act(act)
            act.wait_ge(less_done, 1)
            act.activation(logit[:], logit[:], ACT.Exp).then_inc(exp_done, 1)

            def silu(b):
                for m in range(MT):
                    act.wait_ge(up_mm, b.times(MT, m + 1))
                    if m >= 2 or b.after(1):
                        act.wait_ge(h_done, b.times(MT, m - 1))
                    act.activation(hs[(b.par * MT + m) % 2][:], ph[(b.par * MT + m) % 2][:], ACT.Silu).then_inc(silu_done, 1)

            def store(b):
                act.wait_ge(y_done, b.times(TB, TB))
                act.dma_start(out[bass.ds(b.t * 512, 512), :].rearrange("(j p) d -> p j d", p=P), y[b.par][:]
                              ).then_inc(stored[b.par], 16)

            silu(Tile(0, 0))
            for t in range(1, NB):
                silu(Tile(t // 2, t % 2))
                store(Tile((t - 1) // 2, (t - 1) % 2))
            store(Tile((NB - 1) // 2, (NB - 1) % 2))
            for par in range(2):
                act.wait_ge(stored[par], 16 * (NB // 2))

        @block.vector
        def _(dve):
            steps = [0]

            def link(ins):
                steps[0] += 1
                ins.then_inc(chain, 1)
                dve.wait_ge(chain, steps[0])

            dve.wait_ge(const_in, 16 * len(consts))
            dve.wait_ge(tanh_done, 1)
            dve.wait_ge(logit_mm, 1)
            link(dve.tensor_copy(logit[:].rearrange("p t e -> p (t e)"), po[0][:, 0:NT * E1]))
            full = [P, NT, E1, E1]
            other, own = logit[:].unsqueeze(2).to_broadcast(full), logit[:].unsqueeze(3).to_broadcast(full)
            link(dve.tensor_tensor(gt[:], other, own, ALU.is_gt))
            link(dve.tensor_tensor(eq[:], other, own, ALU.is_equal))
            link(dve.tensor_tensor(eq[:], eq[:], below[:].unsqueeze(1).to_broadcast(full), ALU.mult))
            link(dve.tensor_tensor(gt[:], gt[:], eq[:], ALU.add))
            link(dve.tensor_reduce(rank[:], gt[:], AX.X, ALU.add))
            link(dve.tensor_scalar(rank[:], rank[:], float(TOP1) - 0.5, None, ALU.is_lt))
            link(dve.tensor_reduce(top[:], logit[:], AX.X, ALU.max))
            dve.tensor_tensor(logit[:], logit[:], top[:].unsqueeze(2).to_broadcast([P, NT, E1]), ALU.subtract
                              ).then_inc(less_done, 1)
            dve.wait_ge(exp_done, 1)
            link(dve.tensor_tensor(rank[:], rank[:], logit[:], ALU.mult))
            link(dve.tensor_reduce(top[:], rank[:], AX.X, ALU.add))
            link(dve.reciprocal(top[:], top[:]))
            link(dve.tensor_tensor(share[:, :, 0:E1], rank[:], top[:].unsqueeze(2).to_broadcast([P, NT, E1]),
                                   ALU.mult))
            link(dve.memset(share[:, :, E1:EW], 1.0))
            link(dve.memset(parts[:, :, 3 * EW:32], 0.0))
            link(dve.tensor_copy(parts[:, :, 0:EW], share[:]))
            link(dve.tensor_tensor(left[:], share[:], parts[:, :, 0:EW], ALU.subtract))
            link(dve.tensor_copy(parts[:, :, EW:2 * EW], left[:]))
            dve.tensor_tensor(parts[:, :, 2 * EW:3 * EW], left[:], parts[:, :, EW:2 * EW], ALU.subtract
                              ).then_inc(parts_done, 1)
            for n in range(2):
                dve.wait_ge(share_mm, n + 1)
                dve.tensor_copy(shareT[:, n * 1024:(n + 1) * 1024], pw[n][0:32, :].bitcast(BF16)
                                ).then_inc(share_done, 1)

            def inner(b):
                for m in range(MT):
                    dve.wait_ge(silu_done, b.times(MT, m + 1))
                    if m == 0 and b.after(2):
                        dve.wait_ge(down_mm, b.times(TB, -TB))
                    dve.tensor_tensor(hT[b.par][:, m, :], hs[(b.par * MT + m) % 2][:], pw[(b.par * MT + m) % 2][:], ALU.mult).then_inc(h_done, 1)

            def add(b):
                dve.wait_ge(x_in[b.par], b.half * 16 + 16)
                if b.after(2):
                    dve.wait_ge(stored[b.par], b.half * 16)
                for j in range(TB):
                    dve.wait_ge(down_mm, b.times(TB, j + 1))
                    dve.scalar_tensor_tensor(y[b.par][:, j, :], po[j % 2][:], tg[:, 0:1], x[b.par][:, j, :],
                                             ALU.mult, ALU.add).then_inc(y_done, 1)

            inner(Tile(0, 0))
            for t in range(1, NB):
                inner(Tile(t // 2, t % 2))
                add(Tile((t - 1) // 2, (t - 1) % 2))
            add(Tile((NB - 1) // 2, (NB - 1) % 2))


def program(nc, w, out):
    def scratch(name, shape, dt=F32):
        return nc.dram_tensor(name, shape, dt, kind="Internal").ap()

    rows = out.rearrange("b s d -> (b s) d")
    with ExitStack() as keep:
        xn1, x1, xn2 = scratch("d_xn1", (T, D)), scratch("d_x1", (T, D)), scratch("d_xn2", (T, D))
        shared, idx, y = scratch("d_shared", (T, D)), scratch("d_idx", (T, K0), U32), scratch("d_y", (NONE + 1, D))
        with stage_semaphores(nc) as gs:
            normalise_input(nc, gs, w["x"], xn1)
        with stage_semaphores(nc) as gs:
            layer0_attention(nc, gs, w["x"], w["ctx"], xn1, x1, w)
        slot_ids = keep.enter_context(nc.sbuf_tensor("slot_ids", [P, E0], U32))
        slot_w = keep.enter_context(nc.sbuf_tensor("slot_w", [P, E0], F32))
        with ExitStack() as mid:
            xn_all = mid.enter_context(nc.sbuf_tensor("xn_all", [P, NT, D], F32))
            with ExitStack() as ctx:
                xa = ctx.enter_context(nc.sbuf_tensor("ln2_x", [P, NT, D], F32))
                with stage_semaphores(nc) as gs:
                    layer_norm_block(nc, ctx, gs, "ln2", x1, xa, xn2, xn_all)
            with stage_semaphores(nc) as gs:
                routing(nc, gs, xn_all, w, shared, idx, y[NONE:NONE + 1, :], slot_ids, slot_w)
        with stage_semaphores(nc) as gs:
            experts(nc, gs, xn2, w, slot_ids, slot_w, y)
        x2, xn3, x3, xn4 = scratch("d_x2", (T, D)), scratch("d_xn3", (T, D)), scratch("d_x3", (T, D)), scratch("d_xn4", (T, D))
        with stage_semaphores(nc) as gs:
            combine(nc, gs, w, x1, shared, idx, y, x2)
        keysT, ropeT, keysN = scratch("d_keysT", (P, T)), scratch("d_ropeT", (P, T)), scratch("d_keysN", (P, T))
        with ExitStack() as mid:
            aw = mid.enter_context(nc.sbuf_tensor("aw", [QC, HP, P], F32))
            bp = mid.enter_context(nc.sbuf_tensor("bp", [P, HP, D], F32))
            with stage_semaphores(nc) as gs:
                layer1_keys(nc, gs, w, keysT, ropeT, keysN, aw, bp)
            with ExitStack() as ctx:
                xa = ctx.enter_context(nc.sbuf_tensor("ln3_x", [P, NT, D], F32))
                with stage_semaphores(nc) as gs:
                    layer_norm_block(nc, ctx, gs, "ln3", x2, xa, xn3)
            with stage_semaphores(nc) as gs:
                layer1_attention(nc, gs, w, xn3, x2, keysT, ropeT, keysN, aw, bp, x3)
        with ExitStack() as mid:
            xn_all = mid.enter_context(nc.sbuf_tensor("xn_all4", [P, NT, D], F32))
            with ExitStack() as ctx:
                xa = ctx.enter_context(nc.sbuf_tensor("ln4_x", [P, NT, D], F32))
                with stage_semaphores(nc) as gs:
                    layer_norm_block(nc, ctx, gs, "ln4", x3, xa, xn4, xn_all)
            with stage_semaphores(nc) as gs:
                layer1_experts(nc, gs, w, xn_all, x3, rows)


def shape_constants():
    import numpy as np

    f, bf = np.float32, mybir.dt.np(BF16)
    w = {"ident": np.eye(P, dtype=f), "identb": np.eye(P).astype(bf), "ones0": np.ones((1, P), f)}
    half = HD0 // 4
    theta = (f(1.0) / f(10000.0) ** (np.arange(0, HD0 // 2, 2, dtype=f) / f(HD0 // 2))).astype(f)
    ang = (np.arange(D, dtype=f)[:, None] * theta[None, :]).astype(f)
    cos = np.concatenate([np.cos(ang)] * 2, 1).reshape(2, P, 1, 2 * half).transpose(1, 0, 2, 3)
    sin = np.concatenate([-np.sin(ang), np.sin(ang)], 1).reshape(2, P, 1, 2 * half).transpose(1, 0, 2, 3)
    for name, a in (("cos4", cos), ("sin4", sin)):
        a = np.broadcast_to(a[:, None], (P, 2, 2, BH, 2 * half))
        w[name] = np.ascontiguousarray(a.reshape(P, 4 * BH, 2 * half), dtype=f)
    pick = np.zeros((P, BH, P), bf)
    for h in range(BH):
        for row in (h, BH + h):
            pick[row, h] = pick[64 + row, h] = 1
    w["pick"] = pick
    j = np.arange(R1 // 2, dtype=f)
    inv = (f(1.0) / f(10000.0) ** (j / f(R1 // 2))).astype(f)
    ang = (np.arange(S, dtype=f)[:, None] * inv).astype(f)
    c, s_ = np.cos(ang).T, np.sin(ang).T
    w["qtab"] = np.concatenate([c, c, -s_, s_]).astype(f)
    w["kcos"] = np.concatenate([c] * 4).astype(f)
    w["ksin"] = np.concatenate([-s_, s_] * 2).astype(f)
    w["keyno"] = np.broadcast_to(np.arange(S, dtype=f), (P, S))
    spread = np.zeros((32, MT * P), bf)
    for e in range(EW):
        for part in range(3):
            spread[part * EW + e, e * I1:(e + 1) * I1] = 1
    w["spread1"] = spread.reshape(32, MT, P)
    w["earlier"] = np.triu(np.ones((P, P)), 1).astype(bf)
    w["onesb"] = np.ones((P, P), bf)
    w["below"] = np.broadcast_to(np.tril(np.ones((G0, G0), f), -1), (P, G0, G0))
    w["slot1"] = np.broadcast_to(np.arange(E0, dtype=f) * CAP + 1, (P, E0))
    w["iota"] = np.broadcast_to(np.arange(CAP, dtype=f), (P, CAP))
    w["tok"] = np.arange(T, dtype=f).reshape(NT, P).T
    return w


def laid_out(i):
    import numpy as np
    f = np.float32

    def twice(a):
        out = np.zeros((P, P), f)
        out[:S, :S] = out[S:, S:] = a
        return out

    w = shape_constants()
    w["x"] = i["x"].reshape(T, D)
    w["ctx"] = i["ctx_2048"].reshape(T, D)
    w["wq0"] = twice(i["L0_xattn_Wq"].T)
    w["wkv0"] = np.concatenate([twice(i["L0_xattn_Wk"].T), twice(i["L0_xattn_Wv"].T)], 1)
    w["wo0"] = twice(i["L0_xattn_Wo"].T)
    w["bias0"] = np.concatenate([i["L0_xattn_" + n] for n in ("bq", "bq", "bk", "bk", "bv", "bv")])[None]
    w["bo0"] = np.tile(i["L0_xattn_bo"], 2)[:, None]
    def chunks(a):
        return a.reshape(KC, P, a.shape[-1]).transpose(1, 0, 2)

    w["rw"] = chunks(i["L0_ffn_router_weight"].T)
    w["ebias"] = np.broadcast_to(i["L0_ffn_e_bias"], (P, E0))
    w["shg"], w["shu"], w["shd"] = chunks(i["L0_ffn_sh_gate"]), chunks(i["L0_ffn_sh_up"]), i["L0_ffn_sh_down"]
    gu = np.stack([i["L0_ffn_w_gate"], i["L0_ffn_w_up"]], 2)
    w["gu"] = gu.reshape(E0, KC, P, 2, I0).transpose(0, 2, 1, 3, 4)
    w["dn"] = i["L0_ffn_w_down"]

    wkvc, wkr = i["L1_xattn_W_kvc"], i["L1_xattn_W_kr"]

    def swapped(a):
        return np.concatenate([a[..., R1 // 2:], a[..., :R1 // 2]], -1)

    w["wkvc2"] = chunks(np.concatenate([wkvc, wkvc], 1))
    w["wkr"] = np.stack([np.concatenate([a, a], 1) for a in (wkr, swapped(wkr))], 1)
    for name, key in (("wuqT", "W_uq"), ("wukT", "W_uk"), ("wuvT", "W_uv")):
        a = i["L1_xattn_" + key]
        w[name] = a.reshape(a.shape[0], H1, HD1).transpose(2, 1, 0)
    w["wo1"] = i["L1_xattn_W_o"].reshape(H1, HD1, D).transpose(1, 0, 2)
    w["wdq"] = chunks(i["L1_xattn_W_dq"])
    wqr = i["L1_xattn_W_qr"].reshape(QC, H1, R1)
    w["wqr"] = np.concatenate([wqr, swapped(wqr)], 2)
    w["seg"] = i["itok_BxS_0_1023"].reshape(NT, P).T
    w["wr1"] = chunks(i["L1_ffn_w_router"])
    w1 = np.zeros((D, MT * P), f)
    w2 = np.zeros((MT * P, D), f)
    w1[:, :EW * I1] = np.concatenate([*i["L1_ffn_w1"], i["L1_ffn_w_shared1"]], 1)
    w2[:EW * I1] = np.concatenate([*i["L1_ffn_w2"], i["L1_ffn_w_shared2"]], 0)
    w["w1"], w["w2"] = chunks(w1), w2.reshape(MT, P, D).transpose(1, 0, 2)
    for l in range(2):
        for n, g in (("0", "g_xattn"), ("1", "g_ffn")):
            w[f"g{l}{n}"] = np.broadcast_to(i[g][l:l + 1, None], (P, 1))
    return {k: np.ascontiguousarray(a) for k, a in w.items()}


def kernel(**inputs):
    import numpy as np
    import concourse.bacc as bacc
    from concourse.bass_utils import run_bass_kernel_spmd as run

    nc = bacc.Bacc("TRN2", target_bir_lowering=False, num_devices=1)
    arrays = laid_out({k: np.asarray(v) for k, v in inputs.items()})
    w = {k: nc.dram_tensor("in_" + k, a.shape, mybir.dt.from_np(a.dtype), kind="ExternalInput").ap()
         for k, a in arrays.items()}
    out = nc.dram_tensor("out", (B, S, D), F32, kind="ExternalOutput").ap()
    program(nc, w, out)
    r = run(nc, [{"in_" + k: a for k, a in arrays.items()}], core_ids=[0])
    return r.results[0]["out"]
```

```python
from contextlib import ExitStack, contextmanager

import concourse.bass as bass
from concourse import mybir

F32 = mybir.dt.float32
BF16 = mybir.dt.bfloat16
F16 = mybir.dt.float16
U32 = mybir.dt.uint32
ALU = mybir.AluOpType
ACT = mybir.ActivationFunctionType
AX = mybir.AxisListType

P = 128
B, S, D = 32, 64, 256
T = B * S
NT = T // P
EPS = 1e-5

H0, HD0 = 8, S // 8
BH = 2 * H0
VW = 32
NPROB = 8
PARTS = 6 * HD0


class Tile:

    def __init__(self, half, par):
        self.half, self.par = half, par
        self.t = 2 * half + par

    def plus(self, n):
        q = self.par + n
        return Tile(self.half + q // 2, q % 2)

    def times(self, n, more):
        return self.t * n + more

    def after(self, n):
        return not isinstance(self.half, int) or self.t >= n


class Chain:

    def __init__(self, eng, sem, tile, per):
        self.eng, self.sem, self.base, self.n, self.per = eng, sem, tile.t * per, 0, per

    def __call__(self, ins):
        self.n += 1
        ins.then_inc(self.sem, 1)
        self.eng.wait_ge(self.sem, self.base + self.n)

    def close(self):
        assert self.n == self.per, (self.n, self.per)


class Held:

    def __init__(self, eng, passed):
        self.eng, self.passed = eng, passed

    def wait_ge(self, sem, value):
        wait = self.eng.wait_ge(sem, value)
        if not isinstance(value, int):
            wait.then_inc(self.passed, 1)


@contextmanager
def stage_semaphores(nc):
    taken = []

    def gs(name):
        taken.append(nc.alloc_semaphore(name=name))
        return taken[-1]

    yield gs
    nc.clear_and_free_semaphores(taken)
    nc.all_engine_barrier()


def tile_steps(eng, step, first, last):
    lo = 2
    for t in range(first, lo):
        step(Tile(t // 2, t % 2))
    hi = (last + 1) // 2 * 2
    with eng.Fori(lo // 2, hi // 2) as half:
        step(Tile(half, 0))
        step(Tile(half, 1))
    for t in range(hi, last + 1):
        step(Tile(t // 2, t % 2))


def normalise_input(nc, gs, x, xn_out):
    with ExitStack() as ctx:
        xa = ctx.enter_context(nc.sbuf_tensor("ln_x", [P, NT, D], F32))
        layer_norm_block(nc, ctx, gs, "ln1", x, xa, xn_out)


def layer_norm_block(nc, ctx, gs, tag, src, xa, dst, xn=None):
    stats = ctx.enter_context(nc.sbuf_tensor(tag + "_stats", [P, NT, 6], F32))
    mv = ctx.enter_context(nc.sbuf_tensor(tag + "_mv", [P, NT, 2], F32))
    rstd = ctx.enter_context(nc.sbuf_tensor(tag + "_rstd", [P, NT], F32))
    eps = ctx.enter_context(nc.sbuf_tensor(tag + "_eps", [P, 1], F32))
    if xn is None:
        xn = ctx.enter_context(nc.sbuf_tensor(tag + "_xn", [P, NT, D], F32))
    Q = 4
    x_in = [gs(f"{tag}_x_in{q}") for q in range(NT // Q)]
    stats_done, mv_done, std_done = gs(tag + "_stats"), gs(tag + "_mv"), gs(tag + "_std")
    rstd_done, xn_done, stored = gs(tag + "_rstd"), gs(tag + "_xn"), gs(tag + "_stored")
    eps_set = gs(tag + "_eps")
    engines = ExitStack()
    block = engines.enter_context(nc.Block())

    @block.sync
    def _(sp):
        for q in range(NT // Q):
            sp.dma_start(xa[:, q * Q:(q + 1) * Q, :], src.rearrange("(t p) d -> p t d", p=P)[:, q * Q:(q + 1) * Q, :]
                         ).then_inc(x_in[q], 16)
        for q in range(NT // Q):
            sp.wait_ge(xn_done, (q + 1) * Q)
            sp.dma_start(dst.rearrange("(t p) d -> p t d", p=P)[:, q * Q:(q + 1) * Q, :], xn[:, q * Q:(q + 1) * Q, :]
                         ).then_inc(stored, 16)
        sp.wait_ge(stored, 16 * (NT // Q))

    @block.vector
    def _(dve):
        dve.memset(eps[:], EPS).then_inc(eps_set, 1)
        for t in range(NT):
            if t % Q == 0:
                dve.wait_ge(x_in[t // Q], 16)
            dve.bn_stats(stats[:, t, :], xa[:, t, :]).then_inc(stats_done, 1)
        for t in range(NT):
            dve.wait_ge(stats_done, t + 1)
            dve.bn_aggr(mv[:, t, :], stats[:, t, :]).then_inc(mv_done, 1)
        dve.wait_ge(std_done, 1)
        dve.reciprocal(rstd[:], rstd[:]).then_inc(rstd_done, 1)
        dve.wait_ge(rstd_done, 1)
        for t in range(NT):
            dve.tensor_scalar(xn[:, t, :], xa[:, t, :], mv[:, t, 0:1], rstd[:, t:t + 1],
                              ALU.subtract, ALU.mult).then_inc(xn_done, 1)

    @block.scalar
    def _(act):
        act.wait_ge(eps_set, 1)
        act.wait_ge(mv_done, NT)
        act.activation(rstd[:], mv[:, :, 1], ACT.Sqrt, bias=eps[:, 0:1]).then_inc(std_done, 1)

    engines.close()


def layer0_attention(nc, gs, x, ctx_in, xn_in, x1_out, w):
    ctx = ExitStack()
    with ctx:
        def sb(name, shape, dt):
            return ctx.enter_context(nc.sbuf_tensor("a0_" + name, shape, dt))

        def ps(name, shape, dt):
            return ctx.enter_context(nc.psum_tensor("a0_" + name, shape, dt))

        ident = sb("ident", [P, P], F32)
        identb = sb("identb", [P, P], BF16)
        wq = sb("wq", [P, P], F32)
        wkv = sb("wkv", [P, 2 * P], F32)
        wo = sb("wo", [P, P], F32)
        bias = sb("bias", [P, 3 * P], F32)
        bo = sb("bo", [P, 1], F32)
        gate = sb("gate", [P, 1], F32)
        tg = sb("tg", [P, 1], F32)
        cos4 = sb("cos4", [P, 4 * BH, 4], F32)
        sin4 = sb("sin4", [P, 4 * BH, 4], F32)
        pick = sb("pick", [P, BH, P], BF16)
        xn = [sb(f"xn{i}", [P, D], F32) for i in range(2)]
        cx = [sb(f"cx{i}", [P, D], F32) for i in range(2)]
        xres = [sb(f"xres{i}", [P, D], F32) for i in range(2)]
        qkv = [sb(f"qkv{i}", [P, 3, 2, P], F32) for i in range(2)]
        ra = sb("ra", [P, 4 * BH, 4], F32)
        rb = sb("rb", [P, 4 * BH, 4], F32)
        rest = sb("rest", [P, 2, 2 * BH, HD0], F32)
        parts = [sb(f"parts{i}", [P, 2, 2 * BH, 64], BF16) for i in range(2)]
        va = [sb(f"va{i}", [P, 2, BH, VW], F32) for i in range(2)]
        qkT = [sb(f"qkT{i}", [P, 2, 2, H0, P], BF16) for i in range(2)]
        top = [sb(f"top{i}", [P, H0, 2, 2], F32) for i in range(2)]
        negm = sb("negm", [P, 2, 2, 64], BF16)
        negT = [sb(f"negT{i}", [P, 2 * P], BF16) for i in range(2)]
        prob = [sb(f"prob{i}", [P, 2, 2 * P], F32) for i in range(NPROB)]
        u = [sb(f"u{i}", [P, 2, P], F32) for i in range(2)]
        rden = [sb(f"rden{i}", [P, 2, 4], F32) for i in range(2)]
        att = sb("att", [P, 2, P], F32)
        attT = sb("attT", [P, D], F32)
        res = sb("res", [P, D], F32)
        x1 = [sb(f"x1{i}", [P, D], F32) for i in range(2)]

        mx = [ps(f"mx{i}", [P, 2, 2 * P], F32) for i in range(2)]
        sc = [ps(f"sc{i}", [P, 2, 2 * P], F32) for i in range(2)]
        ma = [ps(f"ma{i}", [P, 512], F32) for i in range(2)]
        pv = [ps(f"pv{i}", [P, 2, 2 * P], F32) for i in range(2)]

        const_in = gs("a0_const_in")
        NCONST = 11
        ready = gs("a0_ready")
        tanh_done = gs("a0_tanh")
        xn_in_s = [gs(f"a0_xn_in{i}") for i in range(2)]
        cx_in_s = [gs(f"a0_cx_in{i}") for i in range(2)]
        xres_in = [gs(f"a0_xres_in{i}") for i in range(2)]
        proj = gs("a0_proj")
        proj_out = gs("a0_proj_out")
        rotate = gs("a0_rotate")
        split = gs("a0_split")
        v_staged = gs("a0_v_staged")
        turned = gs("a0_turned")
        turned_out = gs("a0_turned_out")
        score_q = gs("a0_score_q")
        max_done = gs("a0_max")
        neg = gs("a0_neg")
        neg_turned = gs("a0_neg_turned")
        neg_out = gs("a0_neg_out")
        score_k = gs("a0_score_k")
        exp_done = gs("a0_exp")
        pv_done = gs("a0_pv")
        u_out = gs("a0_u_out")
        u_turned = gs("a0_u_turned")
        rden_done = gs("a0_rden")
        att_done = gs("a0_att")
        att_turned = gs("a0_att_turned")
        attT_out = gs("a0_attT_out")
        out_done = gs("a0_out")
        res_done = gs("a0_res")
        x1_done = gs("a0_x1")
        stored = [gs(f"a0_stored{i}") for i in range(2)]

        block = ctx.enter_context(nc.Block())
        consts = [(ident, w["ident"]), (identb, w["identb"]), (wq, w["wq0"]), (wkv, w["wkv0"]), (wo, w["wo0"]),
                  (bias, w["bias0"]), (bo, w["bo0"]), (gate, w["g00"]), (cos4, w["cos4"]),
                  (sin4, w["sin4"]), (pick, w["pick"])]
        assert len(consts) == NCONST

        @block.sync
        def _(sp):
            for dst, src in consts:
                sp.dma_start(dst[:], src).then_inc(const_in, 16)

            def loads(tl, ahead=True, late=True):
                fixed = isinstance(tl.t, int)
                row = tl.t * P if fixed else sp.snap(tl.t * P)
                row_late = row - 2 * P if fixed else sp.snap(tl.t * P - 2 * P)
                used = tl.times(2, -2) if fixed else sp.snap(tl.times(2, 0) - 2)
                got = tl.t - 3 if fixed else sp.snap(tl.t - 3)
                if ahead:
                    if tl.after(2):
                        sp.wait_ge(proj, used)
                    sp.dma_start(xn[tl.par][:], xn_in[bass.ds(row, P), :]).then_inc(xn_in_s[tl.par], 16)
                    sp.dma_start(cx[tl.par][:], ctx_in[bass.ds(row, P), :]).then_inc(cx_in_s[tl.par], 16)
                if late:
                    if tl.after(4):
                        sp.wait_ge(x1_done, got)
                    sp.dma_start(xres[tl.par][:], x[bass.ds(row_late, P), :]).then_inc(xres_in[tl.par], 16)

            for t in range(4):
                loads(Tile(t // 2, t % 2), late=t >= 2)
            with sp.Fori(2, NT // 2) as half:
                loads(Tile(half, 0))
                loads(Tile(half, 1))
            for t in range(NT, NT + 2):
                loads(Tile(t // 2, t % 2), ahead=False)

        @block.gpsimd
        def _(pool):
            held = Held(pool, gs("a0_pool_passed"))
            pool.wait_ge(const_in, 16 * NCONST)
            pool.wait_ge(ready, 7)
            def rotate_and_split(tl):
                step = Chain(held, rotate, tl, 13)
                qkf = qkv[tl.par][:, 0:2].rearrange("p a c (h d) -> p (a c h) d", d=HD0)
                to = parts[tl.par]
                held.wait_ge(proj_out, tl.times(2, 2))
                step(pool.tensor_tensor(ra[:], qkf[:, :, 0:4], cos4[:], ALU.mult))
                step(pool.tensor_tensor(rb[:, :, 0:2], qkf[:, :, 2:4], sin4[:, :, 0:2], ALU.mult))
                step(pool.tensor_tensor(rb[:, :, 2:4], qkf[:, :, 0:2], sin4[:, :, 2:4], ALU.mult))
                step(pool.tensor_tensor(qkf[:, :, 0:4], ra[:], rb[:], ALU.add))
                if tl.after(2):
                    held.wait_ge(turned, tl.times(4, -4))
                n = 2 * BH
                q = qkf[:, 0:n, :]
                k = qkf[:, n:2 * n, :]
                pq = to[:, 0, :, 0:PARTS].rearrange("p h (r d) -> p h r d", d=HD0)
                pk = to[:, 1, :, 0:PARTS].rearrange("p h (r d) -> p h r d", d=HD0)

                def spread(a, m):
                    return a.unsqueeze(2).to_broadcast([P, n, m, HD0])

                step(pool.tensor_copy(pq[:, :, 0:3, :], spread(q, 3)))
                step(pool.tensor_copy(pk[:, :, 0:4:3, :], spread(k, 2)))
                step(pool.tensor_copy(pk[:, :, 5, :], k))
                step(pool.tensor_tensor(rest[:, 0], q, pq[:, :, 0, :], ALU.subtract))
                step(pool.tensor_tensor(rest[:, 1], k, pk[:, :, 0, :], ALU.subtract))
                step(pool.tensor_copy(pq[:, :, 3:5, :], spread(rest[:, 0], 2)))
                step(pool.tensor_copy(pk[:, :, 1, :], rest[:, 1]))
                step(pool.tensor_copy(pk[:, :, 4, :], rest[:, 1]))
                step(pool.tensor_tensor(pq[:, :, 5, :], rest[:, 0], pq[:, :, 3, :], ALU.subtract))
                step.close()
                pool.tensor_tensor(pk[:, :, 2, :], rest[:, 1], pk[:, :, 1, :], ALU.subtract).then_inc(split, 1)

            def stage_v(tl):
                if tl.after(2):
                    held.wait_ge(pv_done, tl.times(BH, -BH))
                pool.tensor_copy(va[tl.par][:, :, :, 0:HD0], qkv[tl.par][:, 2].rearrange("p c (h d) -> p c h d", d=HD0)
                                 ).then_inc(v_staged, 1)

            def residual(tl):
                held.wait_ge(res_done, tl.times(1, 1))
                held.wait_ge(xres_in[tl.par], tl.half * 16 + 16)
                if tl.after(2):
                    held.wait_ge(stored[tl.par], tl.half * 16)
                pool.tensor_tensor(x1[tl.par][:], res[:], xres[tl.par][:], ALU.add).then_inc(x1_done, 1)

            def step(tl, a=True):
                if a:
                    rotate_and_split(tl.plus(2))
                if tl.after(1):
                    residual(tl.plus(-1))
                if a:
                    stage_v(tl.plus(2))

            rotate_and_split(Tile(0, 0))
            stage_v(Tile(0, 0))
            rotate_and_split(Tile(0, 1))
            stage_v(Tile(0, 1))
            step(Tile(0, 0))
            step(Tile(0, 1))
            with pool.Fori(1, NT // 2 - 1) as half:
                step(Tile(half, 0))
                step(Tile(half, 1))
            step(Tile(NT // 2 - 1, 0), a=False)
            step(Tile(NT // 2 - 1, 1), a=False)
            residual(Tile(NT // 2 - 1, 1))

        @block.tensor
        def _(pe):
            pe.wait_ge(const_in, 16 * NCONST)
            pe.wait_ge(ready, 7)

            def project(tl):
                pe.wait_ge(xn_in_s[tl.par], tl.half * 16 + 16)
                pe.wait_ge(cx_in_s[tl.par], tl.half * 16 + 16)
                if tl.after(1):
                    pe.wait_ge(turned_out, tl.times(4, 0))
                for c in range(2):
                    pos = slice(c * P, (c + 1) * P)
                    pe.matmul(ma[c][:, 0:P], xn[tl.par][:, pos], wq[:], start=True, stop=True)
                    pe.matmul(ma[c][:, P:3 * P], cx[tl.par][:, pos], wkv[:], start=True, stop=True
                              ).then_inc(proj, 1)

            def turn(tl, f):
                if f == 0:
                    pe.wait_ge(split, tl.times(1, 1))
                if f >= 2:
                    pe.wait_ge(turned_out, tl.times(4, f - 1))
                out = ma[f % 2][:].bitcast(BF16).rearrange("p (j t) -> p j t", t=P)
                for j in range(H0):
                    g = (f % 2) * BH + 2 * j
                    mm = pe.transpose(out[:, j, :], parts[tl.par][:, f // 2, g:g + 2, :].rearrange("p h s -> p (h s)"),
                                      identb[:])
                mm.then_inc(turned, 1)

            def score_queries(tl, h):
                if h == 0:
                    pe.wait_ge(turned_out, tl.times(4, 4))
                if h >= 2 or tl.after(1):
                    pe.wait_ge(max_done, tl.times(BH, h - 1))
                rows = slice(64 * (h % 2), 64 * (h % 2) + PARTS)
                t = qkT[tl.par]
                for c in range(2):
                    mm = pe.matmul(mx[h % 2][:, c, :], t[rows, 0, c, h // 2, :], t[rows, 1, :, h // 2, :],
                                   start=True, stop=True)
                mm.then_inc(score_q, 1)

            def turn_neg(tl):
                pe.wait_ge(neg, tl.times(3, 3))
                if tl.after(1):
                    pe.wait_ge(att_done, tl.times(4, -1))
                out = pv[0][:, 0, 0:P].bitcast(BF16).rearrange("p (c t) -> p c t", c=2)
                for c in range(2):
                    mm = pe.transpose(out[:, c, :], negm[:, c].rearrange("p a b -> p (a b)"), identb[:])
                mm.then_inc(neg_turned, 1)

            def score_keys(tl, h):
                if h == 0:
                    pe.wait_ge(neg_out, tl.times(1, 1))
                if h >= 2 or tl.after(1):
                    pe.wait_ge(exp_done, tl.times(BH, h - 1))
                rows = slice(64 * (h % 2), 64 * (h % 2) + PARTS)
                half = slice(64 * (h % 2), 64 * (h % 2) + 64)
                t = qkT[tl.par]
                for c in range(2):
                    pe.matmul(sc[h % 2][:, c, :], t[rows, 1, c, h // 2, :], t[rows, 0, :, h // 2, :],
                              start=True, stop=False)
                    mm = pe.matmul(sc[h % 2][:, c, :], pick[half, h, :], negT[tl.par][half, :], start=False, stop=True)
                mm.then_inc(score_k, 1)

            def weigh(tl, h):
                pe.wait_ge(exp_done, tl.times(BH, h + 1))
                if h == 0:
                    pe.wait_ge(v_staged, tl.times(1, 1))
                if h == 4 and tl.after(1):
                    pe.wait_ge(res_done, tl.times(1, 0))
                if h >= 8 and h % 4 == 0:
                    pe.wait_ge(att_done, tl.times(4, h // 4 - 1))
                col = 32 * (h % 4)
                for c in range(2):
                    mm = pe.matmul(pv[h // 4 % 2][col:col + 32, 0, :], va[tl.par][:, c, h, :],
                                   prob[h % NPROB][:, c, :], start=(c == 0), stop=(c == 1), skip_group_check=True)
                mm.then_inc(pv_done, 1)

            def turn_quad(tl, g):
                pe.wait_ge(u_out, tl.times(4, g + 1))
                for c in range(2):
                    mm = pe.transpose(pv[g % 2][:, 1, c * P:(c + 1) * P], u[g % 2][:, c, :], ident[:])
                mm.then_inc(u_turned, 1)

            def turn_heads(tl):
                pe.wait_ge(att_done, tl.times(4, 4))
                for c in range(2):
                    mm = pe.transpose(pv[1][:, 0, c * P:(c + 1) * P], att[:, c, :], ident[:])
                mm.then_inc(att_turned, 1)

            def project_out(tl):
                pe.wait_ge(attT_out, tl.times(1, 1))
                pe.matmul(pv[1][:, 1, :], wo[:], attT[:], start=True, stop=True).then_inc(out_done, 1)

            def step(tl, a=True, b=True, c=True):
                last, nxt, next2 = tl.plus(-1), tl.plus(1), tl.plus(2)
                for s in range(BH + 4):
                    if b and s < 4:
                        turn(nxt, s)
                    if c and s == 1:
                        turn_neg(tl)
                    if tl.after(1) and s == 1:
                        turn_quad(last, 3)
                    if tl.after(1) and s == 3:
                        turn_heads(last)
                    if c and 2 <= s < BH + 2:
                        score_keys(tl, s - 2)
                    if b and s >= 4:
                        score_queries(nxt, s - 4)
                    if a and s == 4:
                        project(next2)
                    if tl.after(1) and s == 6:
                        project_out(last)
                    if c and s >= 4:
                        weigh(tl, s - 4)
                    if c and s >= 9 and s % 4 == 1:
                        turn_quad(tl, (s - 9) // 4)

            project(Tile(0, 0))
            step(Tile(-1, 1), c=False)
            step(Tile(0, 0))
            step(Tile(0, 1))
            with pe.Fori(1, NT // 2 - 1) as half:
                step(Tile(half, 0))
                step(Tile(half, 1))
            step(Tile(NT // 2 - 1, 0), a=False)
            step(Tile(NT // 2 - 1, 1), a=False, b=False)
            turn_quad(Tile(NT // 2 - 1, 1), 3)
            turn_heads(Tile(NT // 2 - 1, 1))
            project_out(Tile(NT // 2 - 1, 1))

        @block.scalar
        def _(act):
            act.wait_ge(const_in, 16 * NCONST)
            act.wait_ge(ready, 7)
            act.activation(tg[:], gate[:], ACT.Tanh).then_inc(tanh_done, 1)

            def exponent(tl, h):
                act.wait_ge(score_k, tl.times(BH, h + 1))
                if h >= NPROB or tl.after(1):
                    act.wait_ge(pv_done, tl.times(BH, h - NPROB + 1))
                act.activation(prob[h % NPROB][:], sc[h % 2][:], ACT.Exp, scale=float(HD0) ** -0.5).then_inc(exp_done, 1)

            def sums(tl, g):
                act.wait_ge(pv_done, tl.times(BH, 4 * g + 4))
                if g >= 2 or tl.after(1):
                    act.wait_ge(u_turned, tl.times(4, g - 1))
                act.copy(u[g % 2][:].rearrange("p c n -> p (c n)"), pv[g % 2][:, 0, :]).then_inc(u_out, 1)

            def turned_heads(tl):
                act.wait_ge(att_turned, tl.times(1, 1))
                if tl.after(1):
                    act.wait_ge(out_done, tl.times(1, 0))
                act.copy(attT[:], pv[1][:, 0, :]).then_inc(attT_out, 1)

            def store(tl):
                act.wait_ge(x1_done, tl.times(1, 1))
                act.dma_start(x1_out[bass.ds(tl.t * P, P), :], x1[tl.par][:]).then_inc(stored[tl.par], 16)

            def step(tl):
                if tl.after(1):
                    sums(tl.plus(-1), 3)
                for h in range(BH):
                    exponent(tl, h)
                    if h >= 5 and h % 4 == 1:
                        sums(tl, h // 4 - 1)
                    if h == 2 and tl.after(1):
                        turned_heads(tl.plus(-1))
                    if h == 4 and tl.after(2):
                        store(tl.plus(-2))

            tile_steps(act, step, 0, NT - 1)
            sums(Tile(NT // 2 - 1, 1), 3)
            turned_heads(Tile(NT // 2 - 1, 1))
            store(Tile(NT // 2 - 1, 0))
            store(Tile(NT // 2 - 1, 1))
            for i in range(2):
                act.wait_ge(stored[i], 16 * (NT // 2))

        @block.vector
        def _(dve):
            dve.memset(negm[:], 0.0).then_inc(ready, 1)
            for i in range(2):
                dve.memset(parts[i][:, :, :, PARTS:64], 0.0).then_inc(ready, 1)
                dve.memset(va[i][:, :, :, HD0:HD0 + 1], 1.0).then_inc(ready, 1)
                dve.memset(va[i][:, :, :, HD0 + 1:VW], 0.0).then_inc(ready, 1)
            dve.wait_ge(const_in, 16 * NCONST)
            dve.wait_ge(tanh_done, 1)
            dve.wait_ge(ready, 7)

            def projections(tl):
                for c in range(2):
                    dve.wait_ge(proj, tl.times(2, c + 1))
                    if c == 0 and tl.after(2):
                        dve.wait_ge(split, tl.times(1, -1))
                        dve.wait_ge(v_staged, tl.times(1, -1))
                    dve.tensor_tensor(qkv[tl.par][:, :, c, :], ma[c][:, 0:3 * P].rearrange("p (a n) -> p a n", a=3),
                                      bias[:].rearrange("p (a n) -> p a n", a=3), ALU.add).then_inc(proj_out, 1)

            def turned_pairs(tl, f):
                dve.wait_ge(turned, tl.times(4, f + 1))
                dve.tensor_copy(qkT[tl.par][:, f // 2, f % 2], ma[f % 2][:].bitcast(BF16)
                                .rearrange("p (j t) -> p j t", t=P)).then_inc(turned_out, 1)

            def maxima(tl, h):
                dve.wait_ge(score_q, tl.times(BH, h + 1))
                if h == 0 and tl.after(2):
                    dve.wait_ge(neg, tl.times(3, -3))
                dve.tensor_reduce(top[tl.par][:, h // 2, h % 2, :], mx[h % 2][:], AX.X, ALU.max).then_inc(max_done, 1)

            def negate(tl):
                dve.wait_ge(max_done, tl.times(BH, BH))
                if tl.after(1):
                    dve.wait_ge(neg_turned, tl.times(1, 0))
                m = top[tl.par][:].rearrange("p a r c -> p c (a r)").unsqueeze(2).to_broadcast([P, 2, 2, BH])
                high, low = negm[:, :, :, 0:BH], negm[:, :, :, BH:2 * BH]
                dve.tensor_scalar(high, m, -1.0, None, ALU.mult).then_inc(neg, 1)
                dve.wait_ge(neg, tl.times(3, 1))
                for c in range(2):
                    dve.scalar_tensor_tensor(low[:, c], m[:, c], -1.0, high[:, c], ALU.mult, ALU.subtract
                                             ).then_inc(neg, 1)

            def negated(tl):
                dve.wait_ge(neg_turned, tl.times(1, 1))
                dve.tensor_copy(negT[tl.par][:], pv[0][:, 0, 0:P].bitcast(BF16)).then_inc(neg_out, 1)

            def divide(tl, g):
                dve.wait_ge(u_turned, tl.times(4, g + 1))
                heads = pv[g % 2][:, 1, :].rearrange("p (c h w) -> p c h w", c=2, w=VW)
                dve.reciprocal(rden[g % 2][:], heads[:, :, :, HD0]).then_inc(rden_done, 1)
                dve.wait_ge(rden_done, tl.times(4, g + 1))
                if g == 0 and tl.after(1):
                    dve.wait_ge(att_turned, tl.times(1, 0))
                dve.tensor_tensor(att[:, :, g * 32:(g + 1) * 32].rearrange("p c (h d) -> p c h d", d=HD0),
                                  heads[:, :, :, 0:HD0], rden[g % 2][:].unsqueeze(3).to_broadcast([P, 2, 4, HD0]), ALU.mult
                                  ).then_inc(att_done, 1)

            def gated(tl):
                dve.wait_ge(out_done, tl.times(1, 1))
                if tl.after(1):
                    dve.wait_ge(x1_done, tl.times(1, 0))
                dve.tensor_scalar(res[:], pv[1][:, 1, :], bo[:, 0:1], tg[:, 0:1], ALU.add, ALU.mult
                                  ).then_inc(res_done, 1)

            def step(tl, a=True, b=True, c=True):
                last, nxt, next2 = tl.plus(-1), tl.plus(1), tl.plus(2)
                for s in range(BH + 4):
                    if b and s < 4:
                        turned_pairs(nxt, s)
                    if c and s == 1:
                        negated(tl)
                    if tl.after(1) and s == 2:
                        divide(last, 3)
                    if b and s >= 4:
                        maxima(nxt, s - 4)
                    if a and s == 5:
                        projections(next2)
                    if tl.after(1) and s == 7:
                        gated(last)
                    if c and s >= 11 and s % 4 == 3:
                        divide(tl, (s - 11) // 4)
                if b:
                    negate(nxt)

            projections(Tile(0, 0))
            step(Tile(-1, 1), c=False)
            step(Tile(0, 0))
            step(Tile(0, 1))
            with dve.Fori(1, NT // 2 - 1) as half:
                step(Tile(half, 0))
                step(Tile(half, 1))
            step(Tile(NT // 2 - 1, 0), a=False)
            step(Tile(NT // 2 - 1, 1), a=False, b=False)
            divide(Tile(NT // 2 - 1, 1), 3)
            gated(Tile(NT // 2 - 1, 1))


E0, K0, I0 = 64, 8, 88
G0, GTOP = 8, 4
CAP = 128
SCALE0 = 2.5
NONE = E0 * CAP
KC = D // P


def turned_tiles(nc, sb, ps, gs, tag, src, dst, block):
    bank = [ps(f"turn{i}", [P, 4, P], F32) for i in range(2)]
    turned, out = gs(tag + "_turned"), gs(tag + "_turned_out")
    fills = NT * KC // 4

    def on_pe(pe, ident):
        for f in range(fills):
            if f >= 2:
                pe.wait_ge(out, f - 1)
            for j in range(4):
                t, c = f * 2 + j // KC, j % KC
                mm = pe.transpose(bank[f % 2][:, j, :], src[:, t, c * P:(c + 1) * P], ident)
            mm.then_inc(turned, 1)

    def on_act(act):
        for f in range(fills):
            act.wait_ge(turned, f + 1)
            act.copy(dst[:, :, f * 2 * P:(f * 2 + 2) * P].rearrange("p c (t n) -> p t c n", t=2),
                     bank[f % 2][:].rearrange("p (t c) n -> p t c n", c=KC)).then_inc(out, 1)

    return on_pe, on_act, out, fills


def routing(nc, gs, xn_all, w, shared_out, idx_out, y_zero, slot_ids, slot_w):
    ctx = ExitStack()
    with ctx:
        def sb(name, shape, dt=F32):
            return ctx.enter_context(nc.sbuf_tensor("r_" + name, shape, dt))

        def ps(name, shape, dt):
            return ctx.enter_context(nc.psum_tensor("r_" + name, shape, dt))

        NE = NT * E0
        ident = sb("ident", [P, P])
        rw = sb("rw", [P, KC, E0])
        ebias = sb("ebias", [P, E0])
        shg, shu = sb("shg", [P, KC, I0]), sb("shu", [P, KC, I0])
        shd = sb("shd", [I0, D])
        earlier = sb("earlier", [P, P], BF16)
        onesb = sb("onesb", [P, P], BF16)
        below = sb("below", [P, G0, G0])
        slot1 = sb("slot1", [P, E0])
        iota = sb("iota", [P, CAP])
        tok = sb("tok", [P, NT])
        xT = sb("xT", [P, KC, T])
        gs_h = sb("silu", [I0, 512])
        hT = sb("hT", [I0, T])
        sh = sb("sh", [P, 2, D])
        zero = sb("zero", [1, D])
        score = sb("score", [P, NT, E0])
        sc = sb("sc", [P, NT, E0])
        hi = [sb(f"hi{n}", [P, NT * G0, 4 >> n]) for n in range(3)]
        lo = [sb(f"lo{n}", [P, NT * G0, 4 >> n]) for n in range(3)]
        tmp = sb("tmp", [P, NT * G0, 2])
        group = sb("group", [P, NT, G0])
        gt = sb("gt", [P, NT, G0, G0])
        eq = sb("eq", [P, NT, G0, G0])
        rank = sb("rank", [P, NT, G0])
        best = sb("best", [P, NT, K0])
        gone = sb("gone", [P, NT, E0])
        sel = sb("sel", [P, NT, E0])
        selb = sb("selb", [P, NT, E0], BF16)
        before = sb("before", [P, NT, E0], BF16)
        wsum = sb("wsum", [P, NT])
        wt = sb("wt", [P, NT, E0])
        slot = sb("slot", [P, NT, E0])
        mine = sb("mine", [P, NT, K0])
        empty = sb("empty", [P, NT, K0])
        idx = sb("idx", [P, NT, K0], U32)
        cidx = sb("cidx", [P, NT, K0], U32)
        cpos = sb("cpos", [P, NT, K0])
        val = sb("val", [P, NT, 3, E0], F16)
        onec = [sb(f"onec{i}", [P, K0, CAP], F16) for i in range(2)]
        onee = sb("onee", [P, K0, E0], F16)
        ev = [sb(f"ev{i}", [P, K0, 3, E0], F16) for i in range(2)]
        stage = sb("stage", [P, 3, E0])

        const_in = gs("r_const_in")
        logits_done = gs("r_logits")
        score_done = gs("r_score")
        up_done = gs("r_up")
        silu_done = gs("r_silu")
        h_done = gs("r_h")
        down_done = gs("r_down")
        sh_out = gs("r_sh_out")
        sh_stored = [gs(f"r_sh_stored{i}") for i in range(2)]
        chain = gs("r_steps")
        sel_done = gs("r_sel")
        pos_done = gs("r_pos")
        val_done = gs("r_val")
        onec_done = gs("r_onec")
        onee_done = gs("r_onee")
        ev_done = gs("r_ev")
        spread_done = gs("r_spread")
        idx_done = gs("r_idx")
        stored = gs("r_stored")
        zeroed = gs("r_zeroed")

        block = ctx.enter_context(nc.Block())
        consts = [(ident, w["ident"]), (rw, w["rw"]), (ebias, w["ebias"]), (shg, w["shg"]), (shu, w["shu"]),
                  (shd, w["shd"]), (earlier, w["earlier"]), (onesb, w["onesb"]), (below, w["below"]),
                  (slot1, w["slot1"]), (iota, w["iota"]), (tok, w["tok"])]
        turn_pe, turn_act, xT_out, xT_fills = turned_tiles(nc, lambda *a: sb(*a), ps, gs, "r", xn_all, xT, block)
        lg = ps("lg", [P, NT, E0], F32)
        up = ps("up", [P, 2, 512], F32)
        down = [ps(f"down{i}", [P, 2, D], F32) for i in range(2)]

        @block.sync
        def _(sp):
            for dst, src in consts:
                sp.dma_start(dst[:], src).then_inc(const_in, 16)
            sp.wait_ge(zeroed, 1)
            sp.dma_start(y_zero, zero[:]).then_inc(stored, 16)
            for p in range(NT // 2):
                sp.wait_ge(sh_out, p + 1)
                sp.dma_start(shared_out.rearrange("(t p) d -> p t d", p=P)[:, 2 * p:2 * p + 2, :], sh[:]
                             ).then_inc(sh_stored[0], 16)
            sp.wait_ge(idx_done, 1)
            sp.dma_start(idx_out.rearrange("(t p) k -> p t k", p=P), idx[:]).then_inc(stored, 16)
            sp.wait_ge(stored, 32)
            sp.wait_ge(sh_stored[0], 16 * (NT // 2))

        @block.tensor
        def _(pe):
            pe.wait_ge(const_in, 16 * len(consts))
            turn_pe(pe, ident[:])
            pe.wait_ge(xT_out, xT_fills)
            for t in range(NT):
                for c in range(KC):
                    mm = pe.matmul(lg[:, t, :], xT[:, c, t * P:(t + 1) * P], rw[:, c, :], start=(c == 0),
                                   stop=(c == KC - 1))
            mm.then_inc(logits_done, 1)
            for b in range(4):
                if b:
                    pe.wait_ge(h_done, b)
                for n, wt_ in enumerate((shg, shu)):
                    for c in range(KC):
                        mm = pe.matmul(up[0:I0, n, :], wt_[:, c, :], xT[:, c, b * 512:(b + 1) * 512],
                                       start=(c == 0), stop=(c == KC - 1))
                mm.then_inc(up_done, 1)
            pe.wait_ge(h_done, 4)
            for p in range(NT // 2):
                if p >= 2:
                    pe.wait_ge(sh_out, p - 1)
                for j in range(2):
                    t = 2 * p + j
                    mm = pe.matmul(down[p % 2][:, j, :], hT[:, t * P:(t + 1) * P], shd[:], start=True, stop=True)
                mm.then_inc(down_done, 1)
            pe.wait_ge(sel_done, 1)
            for n in range(2):
                tiles = slice(n * NT // 2, (n + 1) * NT // 2)
                pe.matmul(lg[:, tiles, :], earlier[:], selb[:, tiles, :], start=True, stop=False)
                mm = pe.matmul(lg[:, tiles, :], onesb[:], before[:, tiles, :], start=False, stop=True)
            mm.then_inc(pos_done, 1)

            def spread(tl):
                pe.wait_ge(onec_done, tl.times(1, 1))
                pe.wait_ge(ev_done, tl.times(1, 1))
                first, last = tl.t == 0, isinstance(tl.t, int) and tl.t == NT - 1
                for k in range(K0):
                    mm = pe.matmul(up[:, 0, 0:3 * E0], onec[tl.par][:, k, :],
                                   ev[tl.par][:, k].rearrange("p v e -> p (v e)"),
                                   start=bool(isinstance(tl.t, int) and first and k == 0),
                                   stop=(last and k == K0 - 1), skip_group_check=True)
                mm.then_inc(spread_done, 1)

            tile_steps(pe, spread, 0, NT - 1)

        @block.scalar
        def _(act):
            act.wait_ge(const_in, 16 * len(consts))
            turn_act(act)
            act.wait_ge(logits_done, 1)
            act.activation(score[:], lg[:], ACT.Sigmoid).then_inc(score_done, 1)
            for b in range(4):
                act.wait_ge(up_done, b + 1)
                if b:
                    act.wait_ge(h_done, b)
                act.activation(gs_h[:], up[0:I0, 0, :], ACT.Silu).then_inc(silu_done, 1)
            for p in range(NT // 2):
                act.wait_ge(down_done, p + 1)
                if p:
                    act.wait_ge(sh_stored[0], 16 * p)
                act.copy(sh[:], down[p % 2][:]).then_inc(sh_out, 1)

        @block.vector
        def _(dve):
            steps = [0]

            def link(ins):
                steps[0] += 1
                ins.then_inc(chain, 1)
                dve.wait_ge(chain, steps[0])

            dve.memset(zero[:], 0.0).then_inc(zeroed, 1)
            dve.wait_ge(const_in, 16 * len(consts))
            for b in range(4):
                dve.wait_ge(silu_done, b + 1)
                dve.tensor_tensor(hT[:, b * 512:(b + 1) * 512], gs_h[:], up[0:I0, 1, :], ALU.mult).then_inc(h_done, 1)
            dve.wait_ge(score_done, 1)
            link(dve.tensor_tensor(sc[:], score[:], ebias[:].unsqueeze(1).to_broadcast([P, NT, E0]), ALU.add))
            eight = sc[:].rearrange("p t (g m) -> p (t g) m", m=8)
            link(dve.tensor_tensor(hi[0][:], eight[:, :, 0:4], eight[:, :, 4:8], ALU.max))
            link(dve.tensor_tensor(lo[0][:], eight[:, :, 0:4], eight[:, :, 4:8], ALU.min))
            for n in range(2):
                m = 2 >> n
                h1, h2 = hi[n][:, :, 0:m], hi[n][:, :, m:2 * m]
                link(dve.tensor_tensor(hi[n + 1][:], h1, h2, ALU.max))
                link(dve.tensor_tensor(lo[n + 1][:], h1, h2, ALU.min))
                link(dve.tensor_tensor(tmp[:, :, 0:m], lo[n][:, :, 0:m], lo[n][:, :, m:2 * m], ALU.max))
                link(dve.tensor_tensor(lo[n + 1][:], lo[n + 1][:], tmp[:, :, 0:m], ALU.max))
            link(dve.tensor_tensor(group[:].rearrange("p t g -> p (t g)"), hi[2][:, :, 0], lo[2][:, :, 0], ALU.add))
            full = [P, NT, G0, G0]
            other, own = group[:].unsqueeze(2).to_broadcast(full), group[:].unsqueeze(3).to_broadcast(full)
            link(dve.tensor_tensor(gt[:], other, own, ALU.is_gt))
            link(dve.tensor_tensor(eq[:], other, own, ALU.is_equal))
            link(dve.tensor_tensor(eq[:], eq[:], below[:].unsqueeze(1).to_broadcast(full), ALU.mult))
            link(dve.tensor_tensor(gt[:], gt[:], eq[:], ALU.add))
            link(dve.tensor_reduce(rank[:], gt[:], AX.X, ALU.add))
            link(dve.tensor_scalar(rank[:], rank[:], float(GTOP) - 0.5, None, ALU.is_lt))
            link(dve.tensor_tensor(sc[:].rearrange("p t (g m) -> p (t g) m", m=8), eight,
                                   rank[:].rearrange("p t g -> p (t g)").unsqueeze(2).to_broadcast([P, NT * G0, 8]),
                                   ALU.mult))
            for t in range(NT):
                ins = dve.max(best[:, t, :], sc[:, t, :])
                if t == NT - 1:
                    link(ins)
            link(dve.memset(before[:, 0, :], 0.0))
            for t in range(NT):
                ins = dve.match_replace(gone[:, t, :], best[:, t, :], sc[:, t, :], -1e30)
                if t == NT - 1:
                    link(ins)
            link(dve.tensor_tensor(sel[:], gone[:], sc[:], ALU.is_lt))
            link(dve.tensor_copy(selb[:], sel[:]))
            for t in range(1, NT):
                link(dve.tensor_tensor(before[:, t, :], before[:, t - 1, :], selb[:, t - 1, :], ALU.add))
            dve.tensor_tensor(wt[:], score[:], sel[:], ALU.mult).then_inc(sel_done, 1)
            dve.wait_ge(sel_done, 1)
            link(dve.tensor_reduce(wsum[:], wt[:], AX.X, ALU.add))
            link(dve.tensor_scalar(wsum[:], wsum[:], 1e-20, None, ALU.add))
            link(dve.reciprocal(wsum[:], wsum[:]))
            link(dve.tensor_tensor(wt[:], wt[:], wsum[:].unsqueeze(2).to_broadcast([P, NT, E0]), ALU.mult))
            link(dve.tensor_scalar(wt[:], wt[:], SCALE0, None, ALU.mult))
            link(dve.tensor_copy(val[:, :, 1, :], wt[:]))
            link(dve.tensor_tensor(val[:, :, 2, :], wt[:], val[:, :, 1, :], ALU.subtract))
            link(dve.tensor_copy(val[:, :, 0, :], tok[:].unsqueeze(2).to_broadcast([P, NT, E0])))
            dve.wait_ge(pos_done, 1)
            link(dve.tensor_scalar(slot[:], lg[:], float(CAP) - 0.5, None, ALU.is_lt))
            link(dve.tensor_tensor(sel[:], sel[:], slot[:], ALU.mult))
            link(dve.tensor_tensor(slot[:], lg[:], slot1[:].unsqueeze(1).to_broadcast([P, NT, E0]), ALU.add))
            link(dve.tensor_tensor(slot[:], slot[:], sel[:], ALU.mult))
            for t in range(NT):
                ins = dve.max(mine[:, t, :], slot[:, t, :])
                if t == NT - 1:
                    link(ins)
            link(dve.tensor_scalar(empty[:], mine[:], 0.0, float(NONE + 1), ALU.is_equal, ALU.mult))
            link(dve.tensor_tensor(cpos[:], mine[:], empty[:], ALU.add))
            dve.tensor_scalar(idx[:], cpos[:], -1.0, None, ALU.add).then_inc(idx_done, 1)
            dve.wait_ge(idx_done, 1)
            link(dve.tensor_scalar(cidx[:], idx[:], CAP - 1, None, ALU.bitwise_and))
            link(dve.tensor_copy(cpos[:], cidx[:]))
            link(dve.tensor_tensor(cpos[:], cpos[:], empty[:], ALU.add))

            def one_hots(tl):
                if tl.after(2):
                    dve.wait_ge(spread_done, tl.times(1, -1))
                here = bass.ds(tl.t, 1)

                def of(a):
                    return a[:, here].rearrange("p o k -> p (o k)")

                dve.tensor_tensor(onec[tl.par][:], iota[:].unsqueeze(1).to_broadcast([P, K0, CAP]),
                                  of(cpos).unsqueeze(2).to_broadcast([P, K0, CAP]), ALU.is_equal
                                  ).then_inc(onec_done, 1)
                if tl.after(1):
                    dve.wait_ge(ev_done, tl.times(1, 0))
                dve.tensor_tensor(onee[:], of(slot).unsqueeze(1).to_broadcast([P, K0, E0]),
                                  of(mine).unsqueeze(2).to_broadcast([P, K0, E0]), ALU.is_equal
                                  ).then_inc(onee_done, 1)
                dve.wait_ge(onee_done, tl.times(1, 1))
                dve.tensor_tensor(ev[tl.par][:], onee[:].unsqueeze(2).to_broadcast([P, K0, 3, E0]),
                                  val[:, here].rearrange("p o v e -> p (o v) e").unsqueeze(1)
                                  .to_broadcast([P, K0, 3, E0]), ALU.mult).then_inc(ev_done, 1)

            tile_steps(dve, one_hots, 0, NT - 1)
            dve.wait_ge(spread_done, NT)
            link(dve.tensor_copy(stage[:].rearrange("p v e -> p (v e)"), up[:, 0, 0:3 * E0]))
            link(dve.tensor_copy(slot_ids[:], stage[:, 0, :]))
            link(dve.tensor_tensor(slot_w[:], stage[:, 1, :], stage[:, 2, :], ALU.add))


def experts(nc, gs, xn2, w, slot_ids, slot_w, y_out):
    ctx = ExitStack()
    with ctx:
        def sb(name, shape, dt=F32):
            return ctx.enter_context(nc.sbuf_tensor("e_" + name, shape, dt))

        def ps(name, shape):
            return ctx.enter_context(nc.psum_tensor("e_" + name, shape, F32))

        ident = sb("ident", [P, P])
        gu = [sb(f"gu{i}", [P, KC, 2, I0]) for i in range(2)]
        dn = [sb(f"dn{i}", [I0, D]) for i in range(2)]
        ids = [sb(f"ids{i}", [P, 1], U32) for i in range(2)]
        x = [sb(f"x{i}", [P, D]) for i in range(2)]
        xT = [sb(f"xT{i}", [P, KC, P]) for i in range(2)]
        sg = [sb(f"sg{i}", [I0, P]) for i in range(2)]
        h = [sb(f"h{i}", [I0, P]) for i in range(2)]
        y = [sb(f"y{i}", [P, D]) for i in range(2)]
        pt = [ps(f"pt{i}", [P, KC, P]) for i in range(2)]
        pg = [ps(f"pg{i}", [P, 2, P]) for i in range(2)]
        py = [ps(f"py{i}", [P, D]) for i in range(2)]

        ident_in = gs("e_ident_in")
        gu_in = [gs(f"e_gu_in{i}") for i in range(2)]
        dn_in = [gs(f"e_dn_in{i}") for i in range(2)]
        ids_done = gs("e_ids")
        x_in = [gs(f"e_x_in{i}") for i in range(2)]
        turned = gs("e_turned")
        xT_done = gs("e_xT")
        up_done = gs("e_up")
        silu_done = gs("e_silu")
        h_done = gs("e_h")
        down_done = gs("e_down")
        y_done = gs("e_y")
        stored = [gs(f"e_stored{i}") for i in range(2)]
        passed = gs("e_pool_passed")
        block = ctx.enter_context(nc.Block())

        @block.sync
        def _(sp):
            sp.dma_start(ident[:], w["ident"]).then_inc(ident_in, 16)

            def load(e):
                at = e.t if isinstance(e.t, int) else sp.snap(e.t)
                used = e.times(1, -1) if isinstance(e.t, int) else sp.snap(e.times(1, -1))
                if e.after(2):
                    sp.wait_ge(up_done, used)
                sp.dma_start(gu[e.par][:], w["gu"][bass.ds(at, 1)].rearrange("o p c g i -> p (o c) g i")
                             ).then_inc(gu_in[e.par], 16)
                if e.after(2):
                    sp.wait_ge(down_done, used)
                sp.dma_start(dn[e.par][:], w["dn"][bass.ds(at, 1)].rearrange("o i d -> i (o d)")
                             ).then_inc(dn_in[e.par], 16)

            tile_steps(sp, load, 0, E0 - 1)

        @block.gpsimd
        def _(pool):
            held = Held(pool, passed)

            def gather(e):
                if e.after(2):
                    held.wait_ge(x_in[e.par], e.half * 16)
                    held.wait_ge(turned, e.times(1, -1))
                pool.tensor_copy(ids[e.par][:], slot_ids[:, bass.ds(e.t, 1)]).then_inc(ids_done, 1)
                held.wait_ge(ids_done, e.times(1, 1))
                pool.indirect_dma_start(x[e.par][:], None, xn2, bass.IndirectOffsetOnAxis(ap=ids[e.par][:, 0:1], axis=0),
                                        bounds_check=T - 1, oob_is_err=False).then_inc(x_in[e.par], 16)

            tile_steps(pool, gather, 0, E0 - 1)

        @block.tensor
        def _(pe):
            pe.wait_ge(ident_in, 16)

            def turn(e):
                pe.wait_ge(x_in[e.par], e.half * 16 + 16)
                if e.after(2):
                    pe.wait_ge(xT_done, e.times(1, -1))
                for c in range(KC):
                    mm = pe.transpose(pt[e.par][:, c, :], x[e.par][:, c * P:(c + 1) * P], ident[:])
                mm.then_inc(turned, 1)

            def up(e):
                pe.wait_ge(gu_in[e.par], e.half * 16 + 16)
                pe.wait_ge(xT_done, e.times(1, 1))
                if e.after(2):
                    pe.wait_ge(h_done, e.times(1, -1))
                for g in range(2):
                    for c in range(KC):
                        mm = pe.matmul(pg[e.par][0:I0, g, :], gu[e.par][:, c, g, :], xT[e.par][:, c, :],
                                       start=(c == 0), stop=(c == KC - 1))
                mm.then_inc(up_done, 1)

            def down(e):
                pe.wait_ge(dn_in[e.par], e.half * 16 + 16)
                pe.wait_ge(h_done, e.times(1, 1))
                if e.after(2):
                    pe.wait_ge(y_done, e.times(1, -1))
                pe.matmul(py[e.par][:], h[e.par][:], dn[e.par][:], start=True, stop=True).then_inc(down_done, 1)

            def step(e, ahead=True):
                if ahead:
                    turn(e.plus(1))
                up(e)
                if e.after(1):
                    down(Tile(e.half, 0) if e.par else Tile(e.half - 1, 1))

            turn(Tile(0, 0))
            tile_steps(pe, step, 0, E0 - 3)
            step(Tile(E0 // 2 - 1, 0))
            step(Tile(E0 // 2 - 1, 1), ahead=False)
            down(Tile(E0 // 2 - 1, 1))

        @block.scalar
        def _(act):
            def rows(e):
                act.wait_ge(turned, e.times(1, 1))
                if e.after(2):
                    act.wait_ge(up_done, e.times(1, -1))
                act.copy(xT[e.par][:], pt[e.par][:]).then_inc(xT_done, 1)

            def silu(e):
                act.wait_ge(up_done, e.times(1, 1))
                if e.after(2):
                    act.wait_ge(h_done, e.times(1, -1))
                act.activation(sg[e.par][:], pg[e.par][0:I0, 0, :], ACT.Silu).then_inc(silu_done, 1)

            def store(e):
                act.wait_ge(y_done, e.times(1, 1))
                act.dma_start(y_out[bass.ds(e.t * CAP, CAP), :], y[e.par][:]).then_inc(stored[e.par], 16)

            def step(e, ahead=True):
                if ahead:
                    rows(e.plus(1))
                silu(e)
                if e.after(2):
                    store(Tile(e.half - 1, e.par))

            rows(Tile(0, 0))
            tile_steps(act, step, 0, E0 - 3)
            step(Tile(E0 // 2 - 1, 0))
            step(Tile(E0 // 2 - 1, 1), ahead=False)
            for par in range(2):
                store(Tile(E0 // 2 - 1, par))
            for par in range(2):
                act.wait_ge(stored[par], 16 * (E0 // 2))

        @block.vector
        def _(dve):
            def inner(e):
                dve.wait_ge(silu_done, e.times(1, 1))
                if e.after(2):
                    dve.wait_ge(down_done, e.times(1, -1))
                dve.tensor_tensor(h[e.par][:], sg[e.par][:], pg[e.par][0:I0, 1, :], ALU.mult).then_inc(h_done, 1)

            def weigh(e):
                dve.wait_ge(down_done, e.times(1, 1))
                if e.after(2):
                    dve.wait_ge(stored[e.par], e.half * 16)
                dve.tensor_scalar(y[e.par][:], py[e.par][:], slot_w[:, bass.ds(e.t, 1)], None, ALU.mult
                                  ).then_inc(y_done, 1)

            def step(e):
                inner(e)
                if e.after(1):
                    weigh(Tile(e.half, 0) if e.par else Tile(e.half - 1, 1))

            tile_steps(dve, step, 0, E0 - 1)
            weigh(Tile(E0 // 2 - 1, 1))


def combine(nc, gs, w, x1, shared, idx, y_in, x2_out):
    ctx = ExitStack()
    with ctx:
        def sb(name, shape, dt=F32):
            return ctx.enter_context(nc.sbuf_tensor("c_" + name, shape, dt))

        gate = sb("gate", [P, 1])
        tg = sb("tg", [P, 1])
        ix = [sb(f"ix{i}", [P, K0], U32) for i in range(2)]
        rows = [sb(f"rows{i}", [P, K0, D]) for i in range(2)]
        x = [sb(f"x{i}", [P, D]) for i in range(2)]
        sh = [sb(f"sh{i}", [P, D]) for i in range(2)]
        total = sb("total", [P, D])
        x2 = [sb(f"x2{i}", [P, D]) for i in range(2)]
        gate_in, tanh_done, passed = gs("c_gate_in"), gs("c_tanh"), gs("c_passed")
        ix_in = [gs(f"c_ix_in{i}") for i in range(2)]
        x_in = [gs(f"c_x_in{i}") for i in range(2)]
        rows_in = [gs(f"c_rows_in{i}") for i in range(2)]
        summed, added, x2_done = gs("c_summed"), gs("c_added"), gs("c_x2")
        stored = [gs(f"c_stored{i}") for i in range(2)]
        block = ctx.enter_context(nc.Block())

        @block.sync
        def _(sp):
            sp.dma_start(gate[:], w["g01"]).then_inc(gate_in, 16)

            def load(tl):
                row = tl.t * P if isinstance(tl.t, int) else sp.snap(tl.t * P)
                used = tl.times(1, -1) if isinstance(tl.t, int) else sp.snap(tl.times(1, -1))
                if tl.after(2):
                    sp.wait_ge(x2_done, used)
                sp.dma_start(ix[tl.par][:], idx[bass.ds(row, P), :]).then_inc(ix_in[tl.par], 16)
                sp.dma_start(x[tl.par][:], x1[bass.ds(row, P), :]).then_inc(x_in[tl.par], 16)
                sp.dma_start(sh[tl.par][:], shared[bass.ds(row, P), :]).then_inc(x_in[tl.par], 16)

            tile_steps(sp, load, 0, NT - 1)

        @block.gpsimd
        def _(pool):
            held = Held(pool, passed)

            def gather(tl):
                held.wait_ge(ix_in[tl.par], tl.half * 16 + 16)
                if tl.after(2):
                    held.wait_ge(summed, tl.times(1, -1))
                for k in range(K0):
                    pool.indirect_dma_start(rows[tl.par][:, k, :], None, y_in,
                                            bass.IndirectOffsetOnAxis(ap=ix[tl.par][:, k:k + 1], axis=0),
                                            bounds_check=NONE, oob_is_err=False).then_inc(rows_in[tl.par], 16)

            tile_steps(pool, gather, 0, NT - 1)

        @block.scalar
        def _(act):
            act.wait_ge(gate_in, 16)
            act.activation(tg[:], gate[:], ACT.Tanh).then_inc(tanh_done, 1)

            def store(tl):
                act.wait_ge(x2_done, tl.times(1, 1))
                act.dma_start(x2_out[bass.ds(tl.t * P, P), :], x2[tl.par][:]).then_inc(stored[tl.par], 16)

            tile_steps(act, store, 0, NT - 1)
            for par in range(2):
                act.wait_ge(stored[par], 16 * (NT // 2))

        @block.vector
        def _(dve):
            dve.wait_ge(tanh_done, 1)

            def step(tl):
                dve.wait_ge(rows_in[tl.par], tl.half * (16 * K0) + 16 * K0)
                if tl.after(1):
                    dve.wait_ge(x2_done, tl.times(1, 0))
                dve.tensor_reduce(total[:], rows[tl.par][:].rearrange("p k d -> p d k"), AX.X, ALU.add
                                  ).then_inc(summed, 1)
                dve.wait_ge(summed, tl.times(1, 1))
                dve.wait_ge(x_in[tl.par], tl.half * 32 + 32)
                dve.tensor_tensor(total[:], total[:], sh[tl.par][:], ALU.add).then_inc(added, 1)
                dve.wait_ge(added, tl.times(1, 1))
                if tl.after(2):
                    dve.wait_ge(stored[tl.par], tl.half * 16)
                dve.scalar_tensor_tensor(x2[tl.par][:], total[:], tg[:, 0:1], x[tl.par][:], ALU.mult, ALU.add
                                         ).then_inc(x2_done, 1)

            tile_steps(dve, step, 0, NT - 1)


H1, HD1, KVC, QC, R1, BACK = 16, 128, 64, 96, 64, 8
HP = H1 // 2
NEG = -1e30


def layer1_keys(nc, gs, w, keysT, keysN, aw, bp):
    ctx = ExitStack()
    with ctx:
        def sb(name, shape, dt=F32):
            return ctx.enter_context(nc.sbuf_tensor("k_" + name, shape, dt))

        def ps(name, shape, dt=F32):
            return ctx.enter_context(nc.psum_tensor("k_" + name, shape, dt))

        ident = sb("ident", [P, P])
        ctx_all = sb("ctx", [P, NT, D])
        ctxT = sb("ctxT", [P, KC, T])
        wkvc2 = sb("wkvc2", [P, KC, 2 * KVC])
        wkr = sb("wkr", [KVC, 2, 2 * R1])
        kcos, ksin = sb("kcos", [P, S]), sb("ksin", [P, S])
        wuqT = sb("wuqT", [HD1, H1, QC])
        wukT = sb("wukT", [HD1, H1, KVC])
        wuvT = sb("wuvT", [HD1, H1, KVC])
        wo = sb("wo", [HD1, H1, D])
        kT = sb("kT", [P, T])
        part = sb("part", [P, 512])
        part2 = sb("part2", [P, 512])
        rT = sb("rT", [P, T])
        kN = sb("kN", [P, B, KVC])
        ctx_in = gs("k_ctx_in")
        const_in = gs("k_const_in")
        kT_mm, kT_done = gs("k_kT_mm"), gs("k_kT")
        rope_mm, rope_a, rope_b, rope_done = gs("k_rope_mm"), gs("k_rope_a"), gs("k_rope_b"), gs("k_rope")
        kN_mm, kN_done = gs("k_kN_mm"), gs("k_kN")
        aw_mm, aw_done = gs("k_aw_mm"), gs("k_aw")
        bp_mm, bp_done = gs("k_bp_mm"), gs("k_bp")
        stored = gs("k_stored")
        block = ctx.enter_context(nc.Block())
        turn_pe, turn_act, xT_out, fills = turned_tiles(nc, sb, ps, gs, "k", ctx_all, ctxT, block)
        bank = [ps(f"bank{i}", [P, 512]) for i in range(4)]
        consts = [(ident, w["ident"]), (wkvc2, w["wkvc2"]), (wkr, w["wkr"]), (kcos, w["kcos"]), (ksin, w["ksin"]),
                  (wuqT, w["wuqT"]), (wukT, w["wukT"]), (wuvT, w["wuvT"]), (wo, w["wo1"])]

        @block.sync
        def _(sp):
            for dst, src in consts:
                sp.dma_start(dst[:], src).then_inc(const_in, 16)
            sp.dma_start(ctx_all[:], w["ctx"].rearrange("(t p) d -> p t d", p=P)).then_inc(ctx_in, 16)
            sp.wait_ge(kT_done, 4)
            tiles = keysT.rearrange("(t p) c -> p t c", p=P)
            sp.dma_start(tiles[:, :, 0:P], kT[:].rearrange("p (t c) -> p t c", c=P)).then_inc(stored, 16)
            sp.wait_ge(rope_done, 4)
            sp.dma_start(tiles[:, :, P:2 * P], rT[:].rearrange("p (t c) -> p t c", c=P)).then_inc(stored, 16)
            sp.wait_ge(kN_done, 4)
            sp.dma_start(keysN.rearrange("(t p) c -> p t c", p=P)[:, :, 0:P],
                         kN[:].rearrange("p (t a) l -> p t (a l)", a=2)).then_inc(stored, 16)
            sp.wait_ge(stored, 48)

        @block.tensor
        def _(pe):
            pe.wait_ge(const_in, 16 * len(consts))
            pe.wait_ge(ctx_in, 16)
            turn_pe(pe, ident[:])
            pe.wait_ge(xT_out, fills)
            for q in range(4):
                if q >= 2:
                    pe.wait_ge(kT_done, q - 1)
                for c in range(KC):
                    mm = pe.matmul(bank[q % 2][:], wkvc2[:, c, :], ctxT[:, c, q * 512:(q + 1) * 512],
                                   start=(c == 0), stop=(c == KC - 1))
                mm.then_inc(kT_mm, 1)
            for q in range(4):
                pe.wait_ge(kT_done, q + 1)
                if q:
                    pe.wait_ge(rope_b, q)
                for n in range(2):
                    mm = pe.matmul(bank[2 + n][:], wkr[:, n, :], kT[0:KVC, q * 512:(q + 1) * 512],
                                   start=True, stop=True)
                mm.then_inc(rope_mm, 1)
            pe.wait_ge(kT_done, 4)
            for q in range(4):
                if q >= 2:
                    pe.wait_ge(kN_done, q - 1)
                for b in range(8 * q, 8 * q + 8):
                    for r in range(2):
                        rows = slice(64 * r, 64 * r + 64)
                        mm = pe.matmul(bank[q % 2][rows, (b % 8) * KVC:(b % 8 + 1) * KVC], kT[rows, b * S:(b + 1) * S],
                                       ident[rows, 64 * r:64 * r + KVC], start=True, stop=True)
                mm.then_inc(kN_mm, 1)
            for n in range(2):
                pe.wait_ge(kN_done, 3 + n)
                for h in range(8 * n, 8 * n + 8):
                    mm = pe.matmul(bank[n][0:QC, (h % 8) * KVC:(h % 8 + 1) * KVC], wuqT[:, h, :], wukT[:, h, :],
                                   start=True, stop=True)
                mm.then_inc(aw_mm, 1)
            for n in range(HP // 2):
                if n < 2:
                    pe.wait_ge(aw_done, n + 1)
                else:
                    pe.wait_ge(bp_done, n - 1)
                for hp in (2 * n, 2 * n + 1):
                    for r in range(2):
                        mm = pe.matmul(bank[n % 2][64 * r:64 * r + 64, (hp % 2) * D:(hp % 2 + 1) * D],
                                       wuvT[:, 2 * hp + r, :], wo[:, 2 * hp + r, :], start=True, stop=True)
                mm.then_inc(bp_mm, 1)

        @block.scalar
        def _(act):
            turn_act(act)
            for q in range(4):
                act.wait_ge(kT_mm, q + 1)
                act.copy(kT[:, q * 512:(q + 1) * 512], bank[q % 2][:]).then_inc(kT_done, 1)
            for q in range(4):
                act.wait_ge(kN_mm, q + 1)
                act.copy(kN[:, 8 * q:8 * q + 8, :].rearrange("p b l -> p (b l)"), bank[q % 2][:]).then_inc(kN_done, 1)
            for n in range(2):
                act.wait_ge(aw_mm, n + 1)
                act.copy(aw[:, 4 * n:4 * n + 4, :].rearrange("p a b -> p (a b)"), bank[n][0:QC, :]).then_inc(aw_done, 1)
            for n in range(HP // 2):
                act.wait_ge(bp_mm, n + 1)
                act.copy(bp[:, 2 * n:2 * n + 2, :].rearrange("p a b -> p (a b)"), bank[n % 2][:]).then_inc(bp_done, 1)

        @block.vector
        def _(dve):
            dve.wait_ge(const_in, 16 * len(consts))
            for q in range(4):
                dve.wait_ge(rope_mm, q + 1)
                if q:
                    dve.wait_ge(rope_done, q)

                def at_positions(table):
                    return table[:].unsqueeze(1).to_broadcast([P, 8, S])

                dve.tensor_tensor(part[:].rearrange("p (b s) -> p b s", s=S),
                                  bank[2][:].rearrange("p (b s) -> p b s", s=S), at_positions(kcos), ALU.mult
                                  ).then_inc(rope_a, 1)
                dve.tensor_tensor(part2[:].rearrange("p (b s) -> p b s", s=S),
                                  bank[3][:].rearrange("p (b s) -> p b s", s=S), at_positions(ksin), ALU.mult
                                  ).then_inc(rope_b, 1)
                dve.wait_ge(rope_a, q + 1)
                dve.wait_ge(rope_b, q + 1)
                dve.tensor_tensor(rT[:, q * 512:(q + 1) * 512], part[:], part2[:], ALU.add).then_inc(rope_done, 1)


def layer1_attention(nc, gs, w, xn_in, x2, keysT, keysN, aw, bp, x3_out):
    ctx = ExitStack()
    with ctx:
        def sb(name, shape, dt=F32):
            return ctx.enter_context(nc.sbuf_tensor("b_" + name, shape, dt))

        def ps(name, shape, dt=F32):
            return ctx.enter_context(nc.psum_tensor("b_" + name, shape, dt))

        ident = sb("ident", [P, P])
        wdq = sb("wdq", [P, KC, QC])
        wqr = sb("wqr", [QC, H1, 2 * R1])
        qtab = sb("qtab", [P, S])
        keyno = sb("keyno", [P, S])
        seg = sb("seg", [P, B])
        seg_i = sb("seg_i", [P, B], mybir.dt.int32)
        gate, tg = sb("gate", [P, 1]), sb("tg", [P, 1])
        xn = [sb(f"xn{i}", [P, D]) for i in range(2)]
        x = [sb(f"x{i}", [P, D]) for i in range(2)]
        krT = [sb(f"krT{i}", [P, 2, P]) for i in range(2)]
        kN = [sb(f"kN{i}", [P, 2, KVC]) for i in range(2)]
        xT = sb("xT", [P, KC, P])
        qc = sb("qc", [QC, P])
        qn = sb("qn", [P, HP, P])
        qr = sb("qr", [P, H1, P])
        mask = sb("mask", [P, 2, S])
        mask2 = sb("mask2", [P, 2, S])
        sT = sb("sT", [P, HP, 2, S])
        s = sb("s", [P, HP, 2, S])
        top = sb("top", [P, H1])
        e = sb("e", [P, HP, 2, S])
        total = sb("total", [P, H1])
        p = sb("p", [P, HP, 2, S])
        pT = sb("pT", [P, HP, P])
        u = sb("u", [P, HP, 2, S])
        x3 = [sb(f"x3{i}", [P, D]) for i in range(2)]
        pa = ps("pa", [P, 512])
        pb = [ps(f"pb{i}", [P, 4, P]) for i in range(2)]
        pc = [ps(f"pc{i}", [P, HP, S]) for i in range(2)]
        pd = [ps(f"pd{i}", [P, 4, P]) for i in range(2)]
        pu = ps("pu", [P, HP, S])

        const_in = gs("b_const_in")
        seg_done, tanh_done = gs("b_seg"), gs("b_tanh")
        xn_in_s = [gs(f"b_xn_in{i}") for i in range(2)]
        x_in = [gs(f"b_x_in{i}") for i in range(2)]
        k_in = [gs(f"b_k_in{i}") for i in range(2)]
        xT_mm, xT_done = gs("b_xT_mm"), gs("b_xT")
        qc_mm, qc_done = gs("b_qc_mm"), gs("b_qc")
        qn_mm, qn_done = gs("b_qn_mm"), gs("b_qn")
        qr_mm, qr_done = gs("b_qr_mm"), gs("b_qr")
        sT_mm, sT_done = gs("b_sT_mm"), gs("b_sT")
        s_mm, s_done = gs("b_s_mm"), gs("b_s")
        mask_steps, top_done, less_done = gs("b_mask"), gs("b_top"), gs("b_less")
        exp_done, total_steps, p_done = gs("b_exp"), gs("b_total"), gs("b_p")
        pT_mm, pT_done = gs("b_pT_mm"), gs("b_pT")
        u_mm, u_done = gs("b_u_mm"), gs("b_u")
        o_mm, x3_done = gs("b_o_mm"), gs("b_x3")
        stored = [gs(f"b_stored{i}") for i in range(2)]
        pe_passed, pool_passed = gs("b_pe_passed"), gs("b_pool_passed")
        block = ctx.enter_context(nc.Block())
        consts = [(ident, w["ident"]), (wdq, w["wdq"]), (wqr, w["wqr"]), (qtab, w["qtab"]), (keyno, w["keyno"]),
                  (seg_i, w["seg"]), (gate, w["g10"])]

        @block.sync
        def _(sp):
            for dst, src in consts:
                sp.dma_start(dst[:], src).then_inc(const_in, 16)

            def load(tl):
                fixed = isinstance(tl.t, int)
                row = tl.t * P if fixed else sp.snap(tl.t * P)
                used = tl.times(1, -1) if fixed else sp.snap(tl.times(1, -1))
                weighed = tl.times(2, -2) if fixed else sp.snap(tl.times(2, -2))
                if tl.after(2):
                    sp.wait_ge(xT_mm, used)
                sp.dma_start(xn[tl.par][:], xn_in[bass.ds(row, P), :]).then_inc(xn_in_s[tl.par], 16)
                if tl.after(2):
                    sp.wait_ge(u_mm, weighed)
                sp.dma_start(krT[tl.par][:].rearrange("p a n -> p (a n)"), keysT[bass.ds(row, P), :]
                             ).then_inc(k_in[tl.par], 16)
                sp.dma_start(kN[tl.par][:].rearrange("p b l -> p (b l)"), keysN[bass.ds(row, P), 0:P]
                             ).then_inc(k_in[tl.par], 16)
                if tl.after(2):
                    sp.wait_ge(x3_done, used)
                sp.dma_start(x[tl.par][:], x2[bass.ds(row, P), :]).then_inc(x_in[tl.par], 16)

            tile_steps(sp, load, 0, NT - 1)

        @block.tensor
        def _(pe):
            held = Held(pe, pe_passed)
            pe.wait_ge(const_in, 16 * len(consts))

            def turn_x(tl):
                pe.wait_ge(xn_in_s[tl.par], tl.half * 16 + 16)
                if tl.after(1):
                    pe.wait_ge(qc_done, tl.times(1, 0))
                for c in range(KC):
                    mm = pe.transpose(pa[:, c * P:(c + 1) * P], xn[tl.par][:, c * P:(c + 1) * P], ident[:])
                mm.then_inc(xT_mm, 1)

            def latent(tl):
                pe.wait_ge(xT_done, tl.times(1, 1))
                for c in range(KC):
                    mm = pe.matmul(pa[0:QC, 2 * P:3 * P], wdq[:, c, :], xT[:, c, :], start=(c == 0), stop=(c == KC - 1))
                mm.then_inc(qc_mm, 1)

            def front(tl):
                pe.wait_ge(qc_done, tl.times(1, 1))
                for f in range(2):
                    if tl.after(1):
                        pe.wait_ge(s_done, tl.times(2, f - 1))
                    for j in range(4):
                        mm = pe.matmul(pb[f][:, j, :], aw[:, 4 * f + j, :], qc[:], start=True, stop=True)
                    mm.then_inc(qn_mm, 1)
                for f in range(4):
                    if f < 2:
                        pe.wait_ge(qn_done, tl.times(2, f + 1))
                    else:
                        pe.wait_ge(qr_done, tl.times(4, f - 1))
                    for j in range(4):
                        mm = pe.matmul(pb[f % 2][:, j, :], wqr[:, 4 * f + j, :], qc[:], start=True, stop=True)
                    mm.then_inc(qr_mm, 1)
                held.wait_ge(k_in[tl.par], tl.half * 32 + 32)
                if tl.after(1):
                    held.wait_ge(sT_done, tl.times(2, 0))
                for r in range(2):
                    rows = slice(64 * r, 64 * r + 64)
                    for b in range(2):
                        own = slice(64 * b, 64 * b + 64)
                        pe.matmul(pc[r][own], krT[tl.par][rows, 0, own], qn[rows, :, own], start=True, stop=False)
                for r in range(2):
                    for b in range(2):
                        own = slice(64 * b, 64 * b + 64)
                        if r == b == 0:
                            pe.wait_ge(qr_done, tl.times(4, 4))
                        mm = pe.matmul(pc[r][own], krT[tl.par][:, 1, own], qr[:, r:H1:2, own], start=False, stop=True)
                    mm.then_inc(sT_mm, 1)

            def turn_scores(tl):
                pe.wait_ge(sT_done, tl.times(2, 2))
                for f in range(2):
                    for j in range(4):
                        mm = pe.transpose(pb[f][:, j, :], sT[:, 4 * f + j].rearrange("p r q -> p (r q)"), ident[:])
                    mm.then_inc(s_mm, 1)

            def turn_probs(tl):
                pe.wait_ge(p_done, tl.times(2, 2))
                if tl.after(1):
                    pe.wait_ge(u_done, tl.times(2, 0))
                    pe.wait_ge(x3_done, tl.times(1, 0))
                for f in range(2):
                    for j in range(4):
                        mm = pe.transpose(pd[f][:, j, :], p[:, 4 * f + j].rearrange("p b k -> p (b k)"), ident[:])
                    mm.then_inc(pT_mm, 1)

            def weigh(tl):
                held.wait_ge(pT_done, tl.times(2, 2))
                for b in range(2):
                    rows = slice(64 * b, 64 * b + 64)
                    to = pu[:] if b == 0 else pd[0][:].rearrange("p a n -> p (a n)").rearrange("p (h q) -> p h q", q=S)
                    for r in range(2):
                        half = slice(64 * r, 64 * r + 64)
                        mm = pe.matmul(to[half], kN[tl.par][rows, b, :], pT[rows, :, half], start=True, stop=True)
                    mm.then_inc(u_mm, 1)

            def project_out(tl, pairs):
                if pairs[0] == 0:
                    pe.wait_ge(u_done, tl.times(2, 2))
                out = pd[1][:].rearrange("p a n -> p (a n)")[:, 0:D]
                for hp in pairs:
                    mm = pe.matmul(out, u[:, hp].rearrange("p b q -> p (b q)"), bp[:, hp, :],
                                   start=(hp == 0), stop=(hp == HP - 1))
                if pairs[-1] == HP - 1:
                    mm.then_inc(o_mm, 1)

            def step(tl, ahead=True, ahead2=True):
                if ahead:
                    front(tl.plus(1))
                turn_probs(tl)
                if ahead:
                    turn_scores(tl.plus(1))
                weigh(tl)
                if ahead2:
                    turn_x(tl.plus(2))
                project_out(tl, range(0, HP // 2))
                if ahead2:
                    latent(tl.plus(2))
                project_out(tl, range(HP // 2, HP))

            turn_x(Tile(0, 0))
            latent(Tile(0, 0))
            front(Tile(0, 0))
            turn_scores(Tile(0, 0))
            turn_x(Tile(0, 1))
            latent(Tile(0, 1))
            tile_steps(pe, step, 0, NT - 3)
            step(Tile(NT // 2 - 1, 0), ahead2=False)
            step(Tile(NT // 2 - 1, 1), ahead=False, ahead2=False)

        @block.scalar
        def _(act):
            act.wait_ge(const_in, 16 * len(consts))
            act.activation(tg[:], gate[:], ACT.Tanh).then_inc(tanh_done, 1)

            def turned_x(tl):
                act.wait_ge(xT_mm, tl.times(1, 1))
                act.copy(xT[:].rearrange("p c t -> p (c t)"), pa[:, 0:2 * P]).then_inc(xT_done, 1)

            def latent(tl):
                act.wait_ge(qc_mm, tl.times(1, 1))
                if tl.after(1):
                    act.wait_ge(qr_mm, tl.times(4, 0))
                act.copy(qc[:], pa[0:QC, 2 * P:3 * P]).then_inc(qc_done, 1)

            def front(tl):
                for f in range(2):
                    act.wait_ge(qn_mm, tl.times(2, f + 1))
                    if f == 0 and tl.after(1):
                        act.wait_ge(sT_mm, tl.times(2, 0))
                    act.copy(qn[:, 4 * f:4 * f + 4, :], pb[f][:]).then_inc(qn_done, 1)
                for r in range(2):
                    act.wait_ge(sT_mm, tl.times(2, r + 1))
                    if r == 0 and tl.after(1):
                        act.wait_ge(s_mm, tl.times(2, 0))
                    act.copy(sT[:, :, r, :], pc[r][:]).then_inc(sT_done, 1)

            def exponent(tl):
                act.wait_ge(less_done, tl.times(1, 1))
                if tl.after(1):
                    act.wait_ge(p_done, tl.times(2, 0))
                act.activation(e[:], s[:], ACT.Exp, scale=float(HD1 + R1) ** -0.5).then_inc(exp_done, 1)

            def back(tl):
                for f in range(2):
                    act.wait_ge(pT_mm, tl.times(2, f + 1))
                    if f == 0 and tl.after(1):
                        act.wait_ge(u_mm, tl.times(2, 0))
                    act.copy(pT[:, 4 * f:4 * f + 4, :], pd[f][:]).then_inc(pT_done, 1)
                for b in range(2):
                    act.wait_ge(u_mm, tl.times(2, b + 1))
                    if b == 0 and tl.after(1):
                        act.wait_ge(o_mm, tl.times(1, 0))
                    src = pu[:] if b == 0 else pd[0][:].rearrange("p a n -> p (a n)").rearrange("p (h q) -> p h q", q=S)
                    act.copy(u[:, :, b, :], src).then_inc(u_done, 1)

            def store(tl):
                act.wait_ge(x3_done, tl.times(1, 1))
                act.dma_start(x3_out[bass.ds(tl.t * P, P), :], x3[tl.par][:]).then_inc(stored[tl.par], 16)

            def step(tl, ahead=True, ahead2=True):
                if ahead:
                    front(tl.plus(1))
                if tl.after(1):
                    store(tl.plus(-1))
                back(tl)
                if ahead2:
                    turned_x(tl.plus(2))
                if ahead:
                    exponent(tl.plus(1))
                if ahead2:
                    latent(tl.plus(2))

            turned_x(Tile(0, 0))
            latent(Tile(0, 0))
            front(Tile(0, 0))
            turned_x(Tile(0, 1))
            exponent(Tile(0, 0))
            latent(Tile(0, 1))
            tile_steps(act, step, 0, NT - 3)
            step(Tile(NT // 2 - 1, 0), ahead2=False)
            step(Tile(NT // 2 - 1, 1), ahead=False, ahead2=False)
            store(Tile(NT // 2 - 1, 1))
            for par in range(2):
                act.wait_ge(stored[par], 16 * (NT // 2))

        @block.gpsimd
        def _(pool):
            held = Held(pool, pool_passed)

            def step(tl):
                held.wait_ge(top_done, tl.times(1, 1))
                heads = s[:].rearrange("p a b k -> p (a b) k")
                pool.tensor_tensor(heads, heads, top[:].unsqueeze(2).to_broadcast([P, H1, S]), ALU.subtract
                                   ).then_inc(less_done, 1)
                held.wait_ge(total_steps, tl.times(2, 2))
                if tl.after(1):
                    held.wait_ge(pT_mm, tl.times(2, 0))
                for f in range(2):
                    pairs = slice(4 * f, 4 * f + 4)
                    pool.tensor_tensor(p[:, pairs].rearrange("p a b k -> p (a b) k"),
                                       e[:, pairs].rearrange("p a b k -> p (a b) k"),
                                       total[:, 8 * f:8 * f + 8].unsqueeze(2).to_broadcast([P, 8, S]), ALU.mult
                                       ).then_inc(p_done, 1)

            tile_steps(pool, step, 0, NT - 1)

        @block.vector
        def _(dve):
            dve.wait_ge(const_in, 16 * len(consts))
            dve.wait_ge(tanh_done, 1)
            dve.tensor_copy(seg[:], seg_i[:]).then_inc(seg_done, 1)
            dve.wait_ge(seg_done, 1)

            def front(tl):
                for f in range(4):
                    dve.wait_ge(qr_mm, tl.times(4, f + 1))
                    if f == 0 and tl.after(1):
                        dve.wait_ge(sT_mm, tl.times(2, 0))
                    dve.tensor_tensor(qr[:, 4 * f:4 * f + 4, :].rearrange("p h (b q) -> p (h b) q", q=S),
                                      pb[f % 2][:].rearrange("p h (b q) -> p (h b) q", q=S),
                                      qtab[:].unsqueeze(1).to_broadcast([P, 8, S]), ALU.mult).then_inc(qr_done, 1)
                if tl.after(1):
                    dve.wait_ge(s_done, tl.times(2, 0))
                step = Chain(dve, mask_steps, tl, 6)
                for b in range(2):
                    mine = seg[:, bass.ds(tl.t * 2 + b, 1)]
                    step(dve.tensor_scalar(mask[:, b], keyno[:], mine, 0.0, ALU.subtract, ALU.is_le))
                    step(dve.tensor_scalar(mask2[:, b], keyno[:], mine, float(-BACK), ALU.subtract, ALU.is_ge))
                step(dve.tensor_tensor(mask[:], mask[:], mask2[:], ALU.mult))
                step(dve.tensor_scalar(mask[:], mask[:], 1.0, -NEG, ALU.subtract, ALU.mult))
                step.close()
                if tl.after(1):
                    dve.wait_ge(exp_done, tl.times(1, 0))
                for f in range(2):
                    dve.wait_ge(s_mm, tl.times(2, f + 1))
                    dve.tensor_tensor(s[:, 4 * f:4 * f + 4].rearrange("p a b k -> p a (b k)"), pb[f][:],
                                      mask[:].rearrange("p b k -> p (b k)").unsqueeze(1).to_broadcast([P, 4, P]),
                                      ALU.add).then_inc(s_done, 1)
                dve.wait_ge(s_done, tl.times(2, 2))
                dve.tensor_reduce(top[:], s[:].rearrange("p a b k -> p (a b) k"), AX.X, ALU.max).then_inc(top_done, 1)

            def sums(tl):
                dve.wait_ge(exp_done, tl.times(1, 1))
                if tl.after(1):
                    dve.wait_ge(p_done, tl.times(2, 0))
                dve.tensor_reduce(total[:], e[:].rearrange("p a b k -> p (a b) k"), AX.X, ALU.add
                                  ).then_inc(total_steps, 1)
                dve.wait_ge(total_steps, tl.times(2, 1))
                dve.reciprocal(total[:], total[:]).then_inc(total_steps, 1)

            def add(tl):
                dve.wait_ge(o_mm, tl.times(1, 1))
                dve.wait_ge(x_in[tl.par], tl.half * 16 + 16)
                if tl.after(2):
                    dve.wait_ge(stored[tl.par], tl.half * 16)
                dve.scalar_tensor_tensor(x3[tl.par][:], pd[1][:].rearrange("p a n -> p (a n)")[:, 0:D], tg[:, 0:1], x[tl.par][:], ALU.mult, ALU.add
                                         ).then_inc(x3_done, 1)

            def step(tl, ahead=True):
                if ahead:
                    front(tl.plus(1))
                if ahead:
                    sums(tl.plus(1))
                add(tl)

            front(Tile(0, 0))
            sums(Tile(0, 0))
            tile_steps(dve, step, 0, NT - 3)
            step(Tile(NT // 2 - 1, 0))
            step(Tile(NT // 2 - 1, 1), ahead=False)


E1, TOP1, I1 = 8, 2, 176
EW = E1 + 1
MT = -(-EW * I1 // P)


def layer1_experts(nc, gs, w, xn_all, x3, out):
    ctx = ExitStack()
    with ctx:
        def sb(name, shape, dt=F32):
            return ctx.enter_context(nc.sbuf_tensor("f_" + name, shape, dt))

        def ps(name, shape, dt=F32):
            return ctx.enter_context(nc.psum_tensor("f_" + name, shape, dt))

        NB = 4
        TB = NT // NB
        ident = sb("ident", [P, P])
        identb = sb("identb", [P, P], BF16)
        gate, tg = sb("gate", [P, 1]), sb("tg", [P, 1])
        wr = sb("wr", [P, KC, E1])
        below = sb("below", [P, E1, E1])
        w1 = sb("w1", [P, KC, MT * P])
        w2 = sb("w2", [P, MT, D])
        spread = sb("spread", [32, MT, P], BF16)
        xT = sb("xT", [P, KC, T])
        logit = sb("logit", [P, NT, E1])
        top = sb("top", [P, NT])
        gt, eq = sb("gt", [P, NT, E1, E1]), sb("eq", [P, NT, E1, E1])
        rank = sb("rank", [P, NT, E1])
        share = sb("share", [P, NT, EW])
        left = sb("left", [P, NT, EW])
        parts = sb("parts", [P, NT, 32], BF16)
        shareT = sb("shareT", [32, T], BF16)
        hs = [sb(f"hs{i}", [P, 512]) for i in range(2)]
        hT = [sb(f"hT{i}", [P, MT, 512]) for i in range(2)]
        x = [sb(f"x{i}", [P, TB, D]) for i in range(2)]
        y = [sb(f"y{i}", [P, TB, D]) for i in range(2)]

        const_in, w_in = gs("f_const_in"), gs("f_w_in")
        tanh_done, logit_mm, less_done, exp_done = gs("f_tanh"), gs("f_logit_mm"), gs("f_less"), gs("f_exp")
        chain, parts_done = gs("f_steps"), gs("f_parts")
        share_mm, share_done = gs("f_share_mm"), gs("f_share")
        up_mm, silu_done, h_done = gs("f_up_mm"), gs("f_silu"), gs("f_h")
        down_mm, y_done = gs("f_down_mm"), gs("f_y")
        x_in = [gs(f"f_x_in{i}") for i in range(2)]
        stored = [gs(f"f_stored{i}") for i in range(2)]
        block = ctx.enter_context(nc.Block())
        turn_pe, turn_act, xT_out, fills = turned_tiles(nc, sb, ps, gs, "f", xn_all, xT, block)
        ph = [ps(f"ph{i}", [P, 512]) for i in range(2)]
        pw = [ps(f"pw{i}", [P, 512]) for i in range(2)]
        po = [ps(f"po{i}", [P, D]) for i in range(2)]
        consts = [(ident, w["ident"]), (identb, w["identb"]), (gate, w["g11"]), (wr, w["wr1"]), (below, w["below"]),
                  (spread, w["spread1"])]

        @block.sync
        def _(sp):
            for dst, src in consts:
                sp.dma_start(dst[:], src).then_inc(const_in, 16)
            sp.dma_start(w1[:], w["w1"]).then_inc(w_in, 16)
            sp.dma_start(w2[:], w["w2"]).then_inc(w_in, 16)

            def load(b):
                fixed = isinstance(b.t, int)
                row = b.t * 512 if fixed else sp.snap(b.t * 512)
                used = b.times(TB, -TB) if fixed else sp.snap(b.times(TB, -TB))
                if b.after(2):
                    sp.wait_ge(y_done, used)
                sp.dma_start(x[b.par][:], x3[bass.ds(row, 512), :].rearrange("(j p) d -> p j d", p=P)
                             ).then_inc(x_in[b.par], 16)

            tile_steps(sp, load, 0, NB - 1)

        @block.tensor
        def _(pe):
            pe.wait_ge(const_in, 16 * len(consts))
            turn_pe(pe, ident[:])
            pe.wait_ge(xT_out, fills)
            for t in range(NT):
                for c in range(KC):
                    mm = pe.matmul(po[0][:, t * E1:(t + 1) * E1], xT[:, c, t * P:(t + 1) * P], wr[:, c, :],
                                   start=(c == 0), stop=(c == KC - 1))
            mm.then_inc(logit_mm, 1)
            pe.wait_ge(parts_done, 1)
            for n in range(2):
                for j in range(8):
                    mm = pe.transpose(pw[n][0:32, :].bitcast(BF16)[:, j * P:(j + 1) * P], parts[:, 8 * n + j, :],
                                      identb[:])
                mm.then_inc(share_mm, 1)
            pe.wait_ge(share_done, 2)
            pe.wait_ge(w_in, 32)

            def up(b):
                tokens = bass.ds(b.t * 512, 512)
                for m in range(MT):
                    if m >= 2 or b.after(1):
                        pe.wait_ge(h_done, b.times(MT, m - 1))
                    for c in range(KC):
                        pe.matmul(ph[(b.par * MT + m) % 2][:], w1[:, c, m * P:(m + 1) * P], xT[:, c, tokens],
                                  start=(c == 0), stop=(c == KC - 1))
                    pe.matmul(pw[(b.par * MT + m) % 2][:], spread[:, m, :], shareT[:, tokens], start=True, stop=True
                              ).then_inc(up_mm, 1)

            def down(b):
                for j in range(TB):
                    pe.wait_ge(h_done, b.times(MT, MT))
                    if j >= 2 or b.after(1):
                        pe.wait_ge(y_done, b.times(TB, j - 1))
                    for m in range(MT):
                        mm = pe.matmul(po[j % 2][:], hT[b.par][:, m, j * P:(j + 1) * P], w2[:, m, :],
                                       start=(m == 0), stop=(m == MT - 1))
                    mm.then_inc(down_mm, 1)

            def step(b, ahead=True):
                if ahead:
                    up(b.plus(1))
                down(b)

            up(Tile(0, 0))
            step(Tile(0, 0))
            step(Tile(0, 1))
            step(Tile(1, 0))
            step(Tile(1, 1), ahead=False)

        @block.scalar
        def _(act):
            act.wait_ge(const_in, 16 * len(consts))
            act.activation(tg[:], gate[:], ACT.Tanh).then_inc(tanh_done, 1)
            turn_act(act)
            act.wait_ge(less_done, 1)
            act.activation(logit[:], logit[:], ACT.Exp).then_inc(exp_done, 1)

            def silu(b):
                for m in range(MT):
                    act.wait_ge(up_mm, b.times(MT, m + 1))
                    if m >= 2 or b.after(1):
                        act.wait_ge(h_done, b.times(MT, m - 1))
                    act.activation(hs[(b.par * MT + m) % 2][:], ph[(b.par * MT + m) % 2][:], ACT.Silu).then_inc(silu_done, 1)

            def store(b):
                act.wait_ge(y_done, b.times(TB, TB))
                act.dma_start(out[bass.ds(b.t * 512, 512), :].rearrange("(j p) d -> p j d", p=P), y[b.par][:]
                              ).then_inc(stored[b.par], 16)

            silu(Tile(0, 0))
            for t in range(1, NB):
                silu(Tile(t // 2, t % 2))
                store(Tile((t - 1) // 2, (t - 1) % 2))
            store(Tile((NB - 1) // 2, (NB - 1) % 2))
            for par in range(2):
                act.wait_ge(stored[par], 16 * (NB // 2))

        @block.vector
        def _(dve):
            steps = [0]

            def link(ins):
                steps[0] += 1
                ins.then_inc(chain, 1)
                dve.wait_ge(chain, steps[0])

            dve.wait_ge(const_in, 16 * len(consts))
            dve.wait_ge(tanh_done, 1)
            dve.wait_ge(logit_mm, 1)
            link(dve.tensor_copy(logit[:].rearrange("p t e -> p (t e)"), po[0][:, 0:NT * E1]))
            full = [P, NT, E1, E1]
            other, own = logit[:].unsqueeze(2).to_broadcast(full), logit[:].unsqueeze(3).to_broadcast(full)
            link(dve.tensor_tensor(gt[:], other, own, ALU.is_gt))
            link(dve.tensor_tensor(eq[:], other, own, ALU.is_equal))
            link(dve.tensor_tensor(eq[:], eq[:], below[:].unsqueeze(1).to_broadcast(full), ALU.mult))
            link(dve.tensor_tensor(gt[:], gt[:], eq[:], ALU.add))
            link(dve.tensor_reduce(rank[:], gt[:], AX.X, ALU.add))
            link(dve.tensor_scalar(rank[:], rank[:], float(TOP1) - 0.5, None, ALU.is_lt))
            link(dve.tensor_reduce(top[:], logit[:], AX.X, ALU.max))
            dve.tensor_tensor(logit[:], logit[:], top[:].unsqueeze(2).to_broadcast([P, NT, E1]), ALU.subtract
                              ).then_inc(less_done, 1)
            dve.wait_ge(exp_done, 1)
            link(dve.tensor_tensor(rank[:], rank[:], logit[:], ALU.mult))
            link(dve.tensor_reduce(top[:], rank[:], AX.X, ALU.add))
            link(dve.reciprocal(top[:], top[:]))
            link(dve.tensor_tensor(share[:, :, 0:E1], rank[:], top[:].unsqueeze(2).to_broadcast([P, NT, E1]),
                                   ALU.mult))
            link(dve.memset(share[:, :, E1:EW], 1.0))
            link(dve.memset(parts[:, :, 3 * EW:32], 0.0))
            link(dve.tensor_copy(parts[:, :, 0:EW], share[:]))
            link(dve.tensor_tensor(left[:], share[:], parts[:, :, 0:EW], ALU.subtract))
            link(dve.tensor_copy(parts[:, :, EW:2 * EW], left[:]))
            dve.tensor_tensor(parts[:, :, 2 * EW:3 * EW], left[:], parts[:, :, EW:2 * EW], ALU.subtract
                              ).then_inc(parts_done, 1)
            for n in range(2):
                dve.wait_ge(share_mm, n + 1)
                dve.tensor_copy(shareT[:, n * 1024:(n + 1) * 1024], pw[n][0:32, :].bitcast(BF16)
                                ).then_inc(share_done, 1)

            def inner(b):
                for m in range(MT):
                    dve.wait_ge(silu_done, b.times(MT, m + 1))
                    if m == 0 and b.after(2):
                        dve.wait_ge(down_mm, b.times(TB, -TB))
                    dve.tensor_tensor(hT[b.par][:, m, :], hs[(b.par * MT + m) % 2][:], pw[(b.par * MT + m) % 2][:], ALU.mult).then_inc(h_done, 1)

            def add(b):
                dve.wait_ge(x_in[b.par], b.half * 16 + 16)
                if b.after(2):
                    dve.wait_ge(stored[b.par], b.half * 16)
                for j in range(TB):
                    dve.wait_ge(down_mm, b.times(TB, j + 1))
                    dve.scalar_tensor_tensor(y[b.par][:, j, :], po[j % 2][:], tg[:, 0:1], x[b.par][:, j, :],
                                             ALU.mult, ALU.add).then_inc(y_done, 1)

            inner(Tile(0, 0))
            for t in range(1, NB):
                inner(Tile(t // 2, t % 2))
                add(Tile((t - 1) // 2, (t - 1) % 2))
            add(Tile((NB - 1) // 2, (NB - 1) % 2))


def program(nc, w, out):
    def scratch(name, shape, dt=F32):
        return nc.dram_tensor(name, shape, dt, kind="Internal").ap()

    rows = out.rearrange("b s d -> (b s) d")
    with ExitStack() as keep:
        xn1, x1, xn2 = scratch("d_xn1", (T, D)), scratch("d_x1", (T, D)), scratch("d_xn2", (T, D))
        shared, idx, y = scratch("d_shared", (T, D)), scratch("d_idx", (T, K0), U32), scratch("d_y", (NONE + 1, D))
        with stage_semaphores(nc) as gs:
            normalise_input(nc, gs, w["x"], xn1)
        with stage_semaphores(nc) as gs:
            layer0_attention(nc, gs, w["x"], w["ctx"], xn1, x1, w)
        slot_ids = keep.enter_context(nc.sbuf_tensor("slot_ids", [P, E0], U32))
        slot_w = keep.enter_context(nc.sbuf_tensor("slot_w", [P, E0], F32))
        with ExitStack() as mid:
            xn_all = mid.enter_context(nc.sbuf_tensor("xn_all", [P, NT, D], F32))
            with ExitStack() as ctx:
                xa = ctx.enter_context(nc.sbuf_tensor("ln2_x", [P, NT, D], F32))
                with stage_semaphores(nc) as gs:
                    layer_norm_block(nc, ctx, gs, "ln2", x1, xa, xn2, xn_all)
            with stage_semaphores(nc) as gs:
                routing(nc, gs, xn_all, w, shared, idx, y[NONE:NONE + 1, :], slot_ids, slot_w)
        with stage_semaphores(nc) as gs:
            experts(nc, gs, xn2, w, slot_ids, slot_w, y)
        x2, xn3, x3, xn4 = scratch("d_x2", (T, D)), scratch("d_xn3", (T, D)), scratch("d_x3", (T, D)), scratch("d_xn4", (T, D))
        with stage_semaphores(nc) as gs:
            combine(nc, gs, w, x1, shared, idx, y, x2)
        keysT, keysN = scratch("d_keysT", (T, 2 * P)), scratch("d_keysN", (T, 2 * P))
        with ExitStack() as mid:
            aw = mid.enter_context(nc.sbuf_tensor("aw", [QC, HP, P], F32))
            bp = mid.enter_context(nc.sbuf_tensor("bp", [P, HP, D], F32))
            with stage_semaphores(nc) as gs:
                layer1_keys(nc, gs, w, keysT, keysN, aw, bp)
            with ExitStack() as ctx:
                xa = ctx.enter_context(nc.sbuf_tensor("ln3_x", [P, NT, D], F32))
                with stage_semaphores(nc) as gs:
                    layer_norm_block(nc, ctx, gs, "ln3", x2, xa, xn3)
            with stage_semaphores(nc) as gs:
                layer1_attention(nc, gs, w, xn3, x2, keysT, keysN, aw, bp, x3)
        with ExitStack() as mid:
            xn_all = mid.enter_context(nc.sbuf_tensor("xn_all4", [P, NT, D], F32))
            with ExitStack() as ctx:
                xa = ctx.enter_context(nc.sbuf_tensor("ln4_x", [P, NT, D], F32))
                with stage_semaphores(nc) as gs:
                    layer_norm_block(nc, ctx, gs, "ln4", x3, xa, xn4, xn_all)
            with stage_semaphores(nc) as gs:
                layer1_experts(nc, gs, w, xn_all, x3, rows)


def shape_constants():
    import numpy as np

    f, bf = np.float32, mybir.dt.np(BF16)
    w = {"ident": np.eye(P, dtype=f), "identb": np.eye(P).astype(bf)}
    half = HD0 // 4
    theta = (f(1.0) / f(10000.0) ** (np.arange(0, HD0 // 2, 2, dtype=f) / f(HD0 // 2))).astype(f)
    ang = (np.arange(D, dtype=f)[:, None] * theta[None, :]).astype(f)
    cos = np.concatenate([np.cos(ang)] * 2, 1).reshape(2, P, 1, 2 * half).transpose(1, 0, 2, 3)
    sin = np.concatenate([-np.sin(ang), np.sin(ang)], 1).reshape(2, P, 1, 2 * half).transpose(1, 0, 2, 3)
    for name, a in (("cos4", cos), ("sin4", sin)):
        a = np.broadcast_to(a[:, None], (P, 2, 2, BH, 2 * half))
        w[name] = np.ascontiguousarray(a.reshape(P, 4 * BH, 2 * half), dtype=f)
    pick = np.zeros((P, BH, P), bf)
    for h in range(BH):
        for row in (h, BH + h):
            pick[row, h] = pick[64 + row, h] = 1
    w["pick"] = pick
    j = np.arange(R1 // 2, dtype=f)
    inv = (f(1.0) / f(10000.0) ** (j / f(R1 // 2))).astype(f)
    ang = (np.arange(S, dtype=f)[:, None] * inv).astype(f)
    c, s_ = np.cos(ang).T, np.sin(ang).T
    w["qtab"] = np.concatenate([c, c, -s_, s_]).astype(f)
    w["kcos"] = np.concatenate([c] * 4).astype(f)
    w["ksin"] = np.concatenate([-s_, s_] * 2).astype(f)
    w["keyno"] = np.broadcast_to(np.arange(S, dtype=f), (P, S))
    spread = np.zeros((32, MT * P), bf)
    for e in range(EW):
        for part in range(3):
            spread[part * EW + e, e * I1:(e + 1) * I1] = 1
    w["spread1"] = spread.reshape(32, MT, P)
    w["earlier"] = np.triu(np.ones((P, P)), 1).astype(bf)
    w["onesb"] = np.ones((P, P), bf)
    w["below"] = np.broadcast_to(np.tril(np.ones((G0, G0), f), -1), (P, G0, G0))
    w["slot1"] = np.broadcast_to(np.arange(E0, dtype=f) * CAP + 1, (P, E0))
    w["iota"] = np.broadcast_to(np.arange(CAP, dtype=f), (P, CAP))
    w["tok"] = np.arange(T, dtype=f).reshape(NT, P).T
    return w


def laid_out(i):
    import numpy as np
    f = np.float32

    def twice(a):
        out = np.zeros((P, P), f)
        out[:S, :S] = out[S:, S:] = a
        return out

    w = shape_constants()
    w["x"] = i["x"].reshape(T, D)
    w["ctx"] = i["ctx_2048"].reshape(T, D)
    w["wq0"] = twice(i["L0_xattn_Wq"].T)
    w["wkv0"] = np.concatenate([twice(i["L0_xattn_Wk"].T), twice(i["L0_xattn_Wv"].T)], 1)
    w["wo0"] = twice(i["L0_xattn_Wo"].T)
    w["bias0"] = np.broadcast_to(np.concatenate([i["L0_xattn_" + n] for n in ("bq", "bq", "bk", "bk", "bv", "bv")]),
                                 (P, 3 * P))
    w["bo0"] = np.tile(i["L0_xattn_bo"], 2)[:, None]
    def chunks(a):
        return a.reshape(KC, P, a.shape[-1]).transpose(1, 0, 2)

    w["rw"] = chunks(i["L0_ffn_router_weight"].T)
    w["ebias"] = np.broadcast_to(i["L0_ffn_e_bias"], (P, E0))
    w["shg"], w["shu"], w["shd"] = chunks(i["L0_ffn_sh_gate"]), chunks(i["L0_ffn_sh_up"]), i["L0_ffn_sh_down"]
    gu = np.stack([i["L0_ffn_w_gate"], i["L0_ffn_w_up"]], 2)
    w["gu"] = gu.reshape(E0, KC, P, 2, I0).transpose(0, 2, 1, 3, 4)
    w["dn"] = i["L0_ffn_w_down"]

    wkvc, wkr = i["L1_xattn_W_kvc"], i["L1_xattn_W_kr"]

    def swapped(a):
        return np.concatenate([a[..., R1 // 2:], a[..., :R1 // 2]], -1)

    w["wkvc2"] = chunks(np.concatenate([wkvc, wkvc], 1))
    w["wkr"] = np.stack([np.concatenate([a, a], 1) for a in (wkr, swapped(wkr))], 1)
    for name, key in (("wuqT", "W_uq"), ("wukT", "W_uk"), ("wuvT", "W_uv")):
        a = i["L1_xattn_" + key]
        w[name] = a.reshape(a.shape[0], H1, HD1).transpose(2, 1, 0)
    w["wo1"] = i["L1_xattn_W_o"].reshape(H1, HD1, D).transpose(1, 0, 2)
    w["wdq"] = chunks(i["L1_xattn_W_dq"])
    wqr = i["L1_xattn_W_qr"].reshape(QC, H1, R1)
    w["wqr"] = np.concatenate([wqr, swapped(wqr)], 2)
    w["seg"] = np.tile(i["itok_BxS_0_1023"].reshape(B, S).T, (2, 1))
    w["wr1"] = chunks(i["L1_ffn_w_router"])
    w1 = np.zeros((D, MT * P), f)
    w2 = np.zeros((MT * P, D), f)
    w1[:, :EW * I1] = np.concatenate([*i["L1_ffn_w1"], i["L1_ffn_w_shared1"]], 1)
    w2[:EW * I1] = np.concatenate([*i["L1_ffn_w2"], i["L1_ffn_w_shared2"]], 0)
    w["w1"], w["w2"] = chunks(w1), w2.reshape(MT, P, D).transpose(1, 0, 2)
    for l in range(2):
        for n, g in (("0", "g_xattn"), ("1", "g_ffn")):
            w[f"g{l}{n}"] = np.broadcast_to(i[g][l:l + 1, None], (P, 1))
    return {k: np.ascontiguousarray(a) for k, a in w.items()}


def kernel(**inputs):
    import numpy as np
    import concourse.bacc as bacc
    from concourse.bass_utils import run_bass_kernel_spmd as run

    nc = bacc.Bacc("TRN2", target_bir_lowering=False, num_devices=1)
    arrays = laid_out({k: np.asarray(v) for k, v in inputs.items()})
    w = {k: nc.dram_tensor("in_" + k, a.shape, mybir.dt.from_np(a.dtype), kind="ExternalInput").ap()
         for k, a in arrays.items()}
    out = nc.dram_tensor("out", (B, S, D), F32, kind="ExternalOutput").ap()
    program(nc, w, out)
    r = run(nc, [{"in_" + k: a for k, a in arrays.items()}], core_ids=[0])
    return r.results[0]["out"]
```

```python
from contextlib import ExitStack, contextmanager

import concourse.bass as bass
from concourse import mybir

F32 = mybir.dt.float32
BF16 = mybir.dt.bfloat16
F16 = mybir.dt.float16
U32 = mybir.dt.uint32
ALU = mybir.AluOpType
ACT = mybir.ActivationFunctionType
AX = mybir.AxisListType

P = 128
B, S, D = 32, 64, 256
T = B * S
NT = T // P
EPS = 1e-5

H0, HD0 = 8, S // 8
BH = 2 * H0
VW = 32
NPROB = 8
PARTS = 6 * HD0
LESS = 2


class Tile:

    def __init__(self, half, par, mod=2, count=NT):
        self.half, self.par, self.mod, self.count = half, par, mod, count
        self.t = mod * half + par

    def plus(self, n):
        q = self.par + n
        return Tile(self.half + q // self.mod, q % self.mod, self.mod, self.count)

    def times(self, n, more):
        return self.t * n + more

    def before(self, n):
        return not isinstance(self.half, int) or self.t + n < self.count

    def after(self, n):
        return not isinstance(self.half, int) or self.t >= n


class Chain:

    def __init__(self, eng, sem, tile, per):
        self.eng, self.sem, self.base, self.n, self.per = eng, sem, tile.t * per, 0, per

    def __call__(self, ins):
        self.n += 1
        ins.then_inc(self.sem, 1)
        self.eng.wait_ge(self.sem, self.base + self.n)

    def close(self):
        assert self.n == self.per, (self.n, self.per)


class Held:

    def __init__(self, eng, passed):
        self.eng, self.passed = eng, passed

    def wait_ge(self, sem, value):
        wait = self.eng.wait_ge(sem, value)
        if not isinstance(value, int):
            wait.then_inc(self.passed, 1)


@contextmanager
def stage_semaphores(nc):
    taken = []

    def gs(name):
        taken.append(nc.alloc_semaphore(name=name))
        return taken[-1]

    yield gs
    nc.clear_and_free_semaphores(taken)
    nc.all_engine_barrier()


def tile_steps(eng, step, first, last):
    lo = 2
    for t in range(first, lo):
        step(Tile(t // 2, t % 2))
    hi = (last + 1) // 2 * 2
    with eng.Fori(lo // 2, hi // 2) as half:
        step(Tile(half, 0))
        step(Tile(half, 1))
    for t in range(hi, last + 1):
        step(Tile(t // 2, t % 2))


class Arena:

    def __init__(self, tensor):
        self.tensor, self.at = tensor, 0

    def take(self, shape, dt):
        per = 1
        for n in shape[1:]:
            per *= n
        words = per // (2 if dt in (BF16, F16) else 1)
        view = self.tensor[0:shape[0], self.at:self.at + words]
        self.at += words
        if dt != F32:
            view = view.bitcast(dt)
        if len(shape) == 3:
            view = view.rearrange("p (a b) -> p a b", a=shape[1])
        return view


def constants(take, w, table):
    c = {name: take(name, shape, dt) for name, (shape, dt, key) in table.items()}
    return c, [(c[name][:], w[key]) for name, (shape, dt, key) in table.items()]


def preload(sp, early, landed):
    for dst, src in early:
        sp.dma_start(dst, src).then_inc(landed, 16)


IDENTITIES = {"ident": ([P, P], F32, "ident"), "identb": ([P, P], BF16, "identb")}
LAYER0_ATTENTION = {
    "wq": ([P, P], F32, "wq0"),
    "wkv": ([P, 2 * P], F32, "wkv0"), "wo": ([P, P], F32, "wo0"), "bias": ([P, 3 * P], F32, "bias0"),
    "bo": ([P, 1], F32, "bo0"), "gate": ([P, 1], F32, "g00"), "cos4": ([P, 4 * BH, 4], F32, "cos4"),
    "sin4": ([P, 4 * BH, 4], F32, "sin4")}


def normalise_input(nc, gs, src, xn, early):
    ctx = ExitStack()
    tag = "ln1"
    xa = ctx.enter_context(nc.sbuf_tensor(tag + "_x", [P, NT, D], F32))
    stats = ctx.enter_context(nc.sbuf_tensor(tag + "_stats", [P, NT, 6], F32))
    mv = ctx.enter_context(nc.sbuf_tensor(tag + "_mv", [P, NT, 2], F32))
    rstd = ctx.enter_context(nc.sbuf_tensor(tag + "_rstd", [P, NT], F32))
    eps = ctx.enter_context(nc.sbuf_tensor(tag + "_eps", [P, 1], F32))
    Q = 4
    x_in = [gs(f"{tag}_x_in{q}") for q in range(NT // Q)]
    stats_done, mv_done, std_done = gs(tag + "_stats"), gs(tag + "_mv"), gs(tag + "_std")
    rstd_done, xn_done = gs(tag + "_rstd"), gs(tag + "_xn")
    eps_set, landed = gs(tag + "_eps"), gs(tag + "_landed")
    engines = ExitStack()
    block = engines.enter_context(nc.Block())

    @block.sync
    def _(sp):
        for q in range(NT // Q):
            sp.dma_start(xa[:, q * Q:(q + 1) * Q, :], src.rearrange("(t p) d -> p t d", p=P)[:, q * Q:(q + 1) * Q, :]
                         ).then_inc(x_in[q], 16)
        preload(sp, early, landed)
        sp.wait_ge(landed, 16 * len(early))

    @block.vector
    def _(dve):
        dve.memset(eps[:], EPS).then_inc(eps_set, 1)
        for t in range(NT):
            if t % Q == 0:
                dve.wait_ge(x_in[t // Q], 16)
            dve.bn_stats(stats[:, t, :], xa[:, t, :]).then_inc(stats_done, 1)
        for t in range(NT):
            dve.wait_ge(stats_done, t + 1)
            dve.bn_aggr(mv[:, t, :], stats[:, t, :]).then_inc(mv_done, 1)
        dve.wait_ge(std_done, 1)
        dve.reciprocal(rstd[:], rstd[:]).then_inc(rstd_done, 1)
        dve.wait_ge(rstd_done, 1)
        for t in range(NT):
            dve.tensor_scalar(xn[:, t, :], xa[:, t, :], mv[:, t, 0:1], rstd[:, t:t + 1],
                              ALU.subtract, ALU.mult).then_inc(xn_done, 1)

    @block.scalar
    def _(act):
        act.wait_ge(eps_set, 1)
        act.wait_ge(mv_done, NT)
        act.activation(rstd[:], mv[:, :, 1], ACT.Sqrt, bias=eps[:, 0:1]).then_inc(std_done, 1)

    engines.close()
    ctx.close()


def layer0_attention(nc, gs, x, ctx_in, x1_out, x1_all, c0, c1, early):
    ctx = ExitStack()
    with ctx:
        def sb(name, shape, dt):
            return ctx.enter_context(nc.sbuf_tensor("a0_" + name, shape, dt))

        def ps(name, shape, dt):
            return ctx.enter_context(nc.psum_tensor("a0_" + name, shape, dt))

        ident, identb = c0["ident"], c0["identb"]
        wq, wkv, wo, bias, bo, gate, cos4, sin4 = (c1[n] for n in LAYER0_ATTENTION)
        tg = sb("tg", [P, 1], F32)
        xn = [sb(f"xn{i}", [P, D], F32) for i in range(2)]
        cx = [sb(f"cx{i}", [P, D], F32) for i in range(2)]
        xres = [sb(f"xres{i}", [P, D], F32) for i in range(2)]
        qkv = [sb(f"qkv{i}", [P, 3, 2, P], F32) for i in range(2)]
        ra = sb("ra", [P, 4 * BH, 4], F32)
        rb = sb("rb", [P, 4 * BH, 4], F32)
        rest = sb("rest", [P, 2, 2 * BH, HD0], F32)
        parts = [sb(f"parts{i}", [P, 2, 2 * BH, 64], BF16) for i in range(2)]
        va = [sb(f"va{i}", [P, 2, BH, VW], F32) for i in range(2)]
        qkT = [sb(f"qkT{i}", [P, 2, H0, 2, P], BF16) for i in range(2)]
        top = [sb(f"top{i}", [P, H0, 2, 2], F32) for i in range(2)]
        negm = sb("negm", [P, 2, 2, BH], BF16)
        negT = [sb(f"negT{i}", [2 * BH, 2, P], BF16) for i in range(2)]
        prob = [sb(f"prob{i}", [P, 2, 2 * P], F32) for i in range(NPROB)]
        u = [sb(f"u{i}", [P, 2, P], F32) for i in range(2)]
        rden = [sb(f"rden{i}", [P, 2, 4], F32) for i in range(2)]
        att = sb("att", [P, 2, P], F32)
        attT = sb("attT", [P, D], F32)
        res = sb("res", [P, D], F32)

        mx = [ps(f"mx{i}", [P, 2, 2 * P], F32) for i in range(2)]
        sc = [ps(f"sc{i}", [P, 2, 2 * P], F32) for i in range(2)]
        ma = [ps(f"ma{i}", [P, 512], F32) for i in range(2)]
        pv = [ps(f"pv{i}", [P, 2, 2 * P], F32) for i in range(2)]

        landed = gs("a0_landed")
        ready = gs("a0_ready")
        tanh_done = gs("a0_tanh")
        xn_in_s = [gs(f"a0_xn_in{i}") for i in range(2)]
        cx_in_s = [gs(f"a0_cx_in{i}") for i in range(2)]
        xres_in = [gs(f"a0_xres_in{i}") for i in range(2)]
        proj = gs("a0_proj")
        proj_out = gs("a0_proj_out")
        rotate = gs("a0_rotate")
        split = gs("a0_split")
        v_staged = gs("a0_v_staged")
        turned = gs("a0_turned")
        turned_out = gs("a0_turned_out")
        score_q = gs("a0_score_q")
        max_done = gs("a0_max")
        neg = gs("a0_neg")
        neg_turned = gs("a0_neg_turned")
        neg_out = gs("a0_neg_out")
        neg_in = [gs(f"a0_neg_in{i}") for i in range(2)]
        score_k = gs("a0_score_k")
        exp_done = gs("a0_exp")
        pv_done = gs("a0_pv")
        u_out = gs("a0_u_out")
        u_turned = gs("a0_u_turned")
        rden_done = gs("a0_rden")
        att_done = gs("a0_att")
        att_turned = gs("a0_att_turned")
        attT_out = gs("a0_attT_out")
        out_done = gs("a0_out")
        res_done = gs("a0_res")
        x1_done = gs("a0_x1")
        stored = [gs(f"a0_stored{i}") for i in range(2)]

        block = ctx.enter_context(nc.Block())
        @block.sync
        def _(sp):
            def loads(tl, ahead=True, late=True):
                fixed = isinstance(tl.t, int)
                row = tl.t * P if fixed else sp.snap(tl.t * P)
                row_late = row - 2 * P if fixed else sp.snap(tl.t * P - 2 * P)
                used = tl.times(2, -2) if fixed else sp.snap(tl.times(2, 0) - 2)
                got = tl.t - 3 if fixed else sp.snap(tl.t - 3)
                if ahead:
                    if tl.after(2):
                        sp.wait_ge(proj, used)
                    sp.dma_start(xn[tl.par][:], x1_all[:, bass.ds(tl.t, 1), :].rearrange("p o d -> p (o d)")).then_inc(xn_in_s[tl.par], 16)
                    sp.dma_start(cx[tl.par][:], ctx_in[bass.ds(row, P), :]).then_inc(cx_in_s[tl.par], 16)
                if late:
                    if tl.after(4):
                        sp.wait_ge(x1_done, got)
                    sp.dma_start(xres[tl.par][:], x[bass.ds(row_late, P), :]).then_inc(xres_in[tl.par], 16)

            for t in range(4):
                loads(Tile(t // 2, t % 2), late=t >= 2)
                if t == 1:
                    preload(sp, early, landed)
            with sp.Fori(2, NT // 2) as half:
                loads(Tile(half, 0))
                loads(Tile(half, 1))
            for t in range(NT, NT + 2):
                loads(Tile(t // 2, t % 2), ahead=False)
            sp.wait_ge(landed, 16 * len(early))

        @block.gpsimd
        def _(pool):
            held = Held(pool, gs("a0_pool_passed"))
            pool.wait_ge(ready, 10)
            def rotate_and_split(tl):
                step = Chain(held, rotate, tl, 13)
                qkf = qkv[tl.par][:, 0:2].rearrange("p a c (h d) -> p (a c h) d", d=HD0)
                to = parts[tl.par]
                held.wait_ge(proj_out, tl.times(2, 2))
                step(pool.tensor_tensor(ra[:], qkf[:, :, 0:4], cos4[:], ALU.mult))
                step(pool.tensor_tensor(rb[:, :, 0:2], qkf[:, :, 2:4], sin4[:, :, 0:2], ALU.mult))
                step(pool.tensor_tensor(rb[:, :, 2:4], qkf[:, :, 0:2], sin4[:, :, 2:4], ALU.mult))
                step(pool.tensor_tensor(qkf[:, :, 0:4], ra[:], rb[:], ALU.add))
                if tl.after(2):
                    held.wait_ge(turned, tl.times(4, -4))
                n = 2 * BH
                q = qkf[:, 0:n, :]
                k = qkf[:, n:2 * n, :]
                pq = to[:, 0, :, 0:PARTS].rearrange("p h (r d) -> p h r d", d=HD0)
                pk = to[:, 1, :, 0:PARTS].rearrange("p h (r d) -> p h r d", d=HD0)

                def spread(a, m):
                    return a.unsqueeze(2).to_broadcast([P, n, m, HD0])

                step(pool.tensor_copy(pq[:, :, 0:3, :], spread(q, 3)))
                step(pool.tensor_copy(pk[:, :, 0:4:3, :], spread(k, 2)))
                step(pool.tensor_copy(pk[:, :, 5, :], k))
                step(pool.tensor_tensor(rest[:, 0], q, pq[:, :, 0, :], ALU.subtract))
                step(pool.tensor_tensor(rest[:, 1], k, pk[:, :, 0, :], ALU.subtract))
                step(pool.tensor_copy(pq[:, :, 3:5, :], spread(rest[:, 0], 2)))
                step(pool.tensor_copy(pk[:, :, 1, :], rest[:, 1]))
                step(pool.tensor_copy(pk[:, :, 4, :], rest[:, 1]))
                step(pool.tensor_tensor(pq[:, :, 5, :], rest[:, 0], pq[:, :, 3, :], ALU.subtract))
                step.close()
                pool.tensor_tensor(pk[:, :, 2, :], rest[:, 1], pk[:, :, 1, :], ALU.subtract).then_inc(split, 1)

            def stage_v(tl):
                if tl.after(2):
                    held.wait_ge(pv_done, tl.times(BH, -BH))
                pool.tensor_copy(va[tl.par][:, :, :, 0:HD0], qkv[tl.par][:, 2].rearrange("p c (h d) -> p c h d", d=HD0)
                                 ).then_inc(v_staged, 1)

            def residual(tl):
                held.wait_ge(res_done, tl.times(1, 1))
                held.wait_ge(xres_in[tl.par], tl.half * 16 + 16)
                pool.tensor_tensor(x1_all[:, bass.ds(tl.t, 1), :].rearrange("p o d -> p (o d)"), res[:],
                                   xres[tl.par][:], ALU.add).then_inc(x1_done, 1)

            def step(tl, a=True):
                if a:
                    rotate_and_split(tl.plus(2))
                if tl.after(1):
                    residual(tl.plus(-1))
                if a:
                    stage_v(tl.plus(2))

            rotate_and_split(Tile(0, 0))
            stage_v(Tile(0, 0))
            rotate_and_split(Tile(0, 1))
            stage_v(Tile(0, 1))
            step(Tile(0, 0))
            step(Tile(0, 1))
            with pool.Fori(1, NT // 2 - 1) as half:
                step(Tile(half, 0))
                step(Tile(half, 1))
            step(Tile(NT // 2 - 1, 0), a=False)
            step(Tile(NT // 2 - 1, 1), a=False)
            residual(Tile(NT // 2 - 1, 1))

        @block.tensor
        def _(pe):
            pe.wait_ge(ready, 10)

            def project(tl):
                pe.wait_ge(xn_in_s[tl.par], tl.half * 16 + 16)
                pe.wait_ge(cx_in_s[tl.par], tl.half * 16 + 16)
                if tl.after(1):
                    pe.wait_ge(turned_out, tl.times(4, 0))
                for c in range(2):
                    pos = slice(c * P, (c + 1) * P)
                    pe.matmul(ma[c][:, 0:P], xn[tl.par][:, pos], wq[:], start=True, stop=True)
                    pe.matmul(ma[c][:, P:3 * P], cx[tl.par][:, pos], wkv[:], start=True, stop=True
                              ).then_inc(proj, 1)

            def turn(tl, f):
                if f == 0:
                    pe.wait_ge(split, tl.times(1, 1))
                    if tl.after(1):
                        pe.wait_ge(neg_out, tl.times(1, 0))
                if f >= 2:
                    pe.wait_ge(turned_out, tl.times(4, f - 1))
                out = ma[f % 2][:].bitcast(BF16).rearrange("p (j t) -> p j t", t=P)
                for j in range(H0):
                    g = (f % 2) * BH + 2 * j
                    mm = pe.transpose(out[:, j, :], parts[tl.par][:, f // 2, g:g + 2, :].rearrange("p h s -> p (h s)"),
                                      identb[:])
                mm.then_inc(turned, 1)

            def score_queries(tl, h):
                if h == 0:
                    pe.wait_ge(turned_out, tl.times(4, 4))
                if h >= 2 or tl.after(1):
                    pe.wait_ge(max_done, tl.times(BH, h - 1))
                rows = slice(64 * (h % 2), 64 * (h % 2) + PARTS)
                t = qkT[tl.par]
                for c in range(2):
                    mm = pe.matmul(mx[h % 2][:, c, :], t[rows, 0, h // 2, c, :], t[rows, 1, h // 2, :, :],
                                   start=True, stop=True)
                mm.then_inc(score_q, 1)

            def turn_neg(tl, a):
                pe.wait_ge(neg, tl.times(2, 2))
                if a:
                    pe.wait_ge(proj_out, tl.plus(1).times(2, 1))
                out = ma[0][0:2 * BH, 0:P].bitcast(BF16).rearrange("p (c t) -> p c t", c=2)
                for c in range(2):
                    mm = pe.transpose(out[:, c, :], negm[:, c].rearrange("p a b -> p (a b)"), identb[:])
                mm.then_inc(neg_turned, 1)

            def score_keys(tl, h):
                if h == 0:
                    pe.wait_ge(neg_in[tl.par], tl.half * 64 + 64)
                if h >= 2 or tl.after(1):
                    pe.wait_ge(exp_done, tl.times(BH, h - 1))
                rows = slice(64 * (h % 2), 64 * (h % 2) + PARTS + LESS)
                t = qkT[tl.par]
                for c in range(2):
                    mm = pe.matmul(sc[h % 2][:, c, :], t[rows, 1, h // 2, c, :], t[rows, 0, h // 2, :, :],
                                   start=True, stop=True)
                mm.then_inc(score_k, 1)

            def weigh(tl, h):
                pe.wait_ge(exp_done, tl.times(BH, h + 1))
                if h == 0:
                    pe.wait_ge(v_staged, tl.times(1, 1))
                if h == 4 and tl.after(1):
                    pe.wait_ge(res_done, tl.times(1, 0))
                if h >= 8 and h % 4 == 0:
                    pe.wait_ge(att_done, tl.times(4, h // 4 - 1))
                col = 32 * (h % 4)
                for c in range(2):
                    mm = pe.matmul(pv[h // 4 % 2][col:col + 32, 0, :], va[tl.par][:, c, h, :],
                                   prob[h % NPROB][:, c, :], start=(c == 0), stop=(c == 1), skip_group_check=True)
                mm.then_inc(pv_done, 1)

            def turn_quad(tl, g):
                pe.wait_ge(u_out, tl.times(4, g + 1))
                for c in range(2):
                    mm = pe.transpose(pv[g % 2][:, 1, c * P:(c + 1) * P], u[g % 2][:, c, :], ident[:])
                mm.then_inc(u_turned, 1)

            def turn_heads(tl):
                pe.wait_ge(att_done, tl.times(4, 4))
                for c in range(2):
                    mm = pe.transpose(pv[1][:, 0, c * P:(c + 1) * P], att[:, c, :], ident[:])
                mm.then_inc(att_turned, 1)

            def project_out(tl):
                pe.wait_ge(attT_out, tl.times(1, 1))
                pe.matmul(pv[1][:, 1, :], wo[:], attT[:], start=True, stop=True).then_inc(out_done, 1)

            def step(tl, a=True, b=True, c=True):
                last, nxt, next2 = tl.plus(-1), tl.plus(1), tl.plus(2)
                for s in range(BH + 7):
                    if b and s < 4:
                        turn(nxt, s)
                    if tl.after(1) and s == 1:
                        turn_quad(last, 3)
                    if tl.after(1) and s == 3:
                        turn_heads(last)
                    if c and 4 <= s < BH + 4:
                        score_keys(tl, s - 4)
                    if b and 4 <= s < BH + 4:
                        score_queries(nxt, s - 4)
                    if a and s == 4:
                        project(next2)
                    if tl.after(1) and s == 6:
                        project_out(last)
                    if c and 7 <= s < BH + 7:
                        weigh(tl, s - 7)
                    if c and s >= 12 and s % 4 == 0 and s < 24:
                        turn_quad(tl, (s - 12) // 4)
                if b:
                    turn_neg(nxt, a)

            project(Tile(0, 0))
            step(Tile(-1, 1), c=False)
            step(Tile(0, 0))
            step(Tile(0, 1))
            with pe.Fori(1, NT // 2 - 1) as half:
                step(Tile(half, 0))
                step(Tile(half, 1))
            step(Tile(NT // 2 - 1, 0), a=False)
            step(Tile(NT // 2 - 1, 1), a=False, b=False)
            turn_quad(Tile(NT // 2 - 1, 1), 3)
            turn_heads(Tile(NT // 2 - 1, 1))
            project_out(Tile(NT // 2 - 1, 1))

        @block.scalar
        def _(act):
            act.wait_ge(ready, 10)
            act.activation(tg[:], gate[:], ACT.Tanh).then_inc(tanh_done, 1)

            def put_maxima(tl):
                act.wait_ge(neg_out, tl.times(1, 1))
                for r in range(2):
                    for part in range(LESS):
                        row = 64 * r + PARTS + part
                        act.dma_start(qkT[tl.par][row:row + 1, 0].rearrange("o j c t -> o j (c t)"),
                                      negT[tl.par][part * BH + r:(part + 1) * BH:2].rearrange("j c t -> j (c t)")).then_inc(neg_in[tl.par], 16)

            def exponent(tl, h):
                act.wait_ge(score_k, tl.times(BH, h + 1))
                if h >= NPROB or tl.after(1):
                    act.wait_ge(pv_done, tl.times(BH, h - NPROB + 1))
                act.activation(prob[h % NPROB][:], sc[h % 2][:], ACT.Exp, scale=float(HD0) ** -0.5).then_inc(exp_done, 1)

            def sums(tl, g):
                act.wait_ge(pv_done, tl.times(BH, 4 * g + 4))
                if g >= 2 or tl.after(1):
                    act.wait_ge(u_turned, tl.times(4, g - 1))
                act.copy(u[g % 2][:].rearrange("p c n -> p (c n)"), pv[g % 2][:, 0, :]).then_inc(u_out, 1)

            def turned_heads(tl):
                act.wait_ge(att_turned, tl.times(1, 1))
                if tl.after(1):
                    act.wait_ge(out_done, tl.times(1, 0))
                act.copy(attT[:], pv[1][:, 0, :]).then_inc(attT_out, 1)

            def store(tl):
                act.wait_ge(x1_done, tl.times(1, 1))
                act.dma_start(x1_out[bass.ds(tl.t * P, P), :],
                              x1_all[:, bass.ds(tl.t, 1), :].rearrange("p o d -> p (o d)")).then_inc(stored[tl.par], 16)

            def step(tl):
                if tl.after(1):
                    sums(tl.plus(-1), 3)
                put_maxima(tl)
                for h in range(BH):
                    exponent(tl, h)
                    if h >= 6 and h % 4 == 2:
                        sums(tl, (h - 6) // 4)
                    if h == 2 and tl.after(1):
                        turned_heads(tl.plus(-1))
                    if h == 4 and tl.after(2):
                        store(tl.plus(-2))

            tile_steps(act, step, 0, NT - 1)
            sums(Tile(NT // 2 - 1, 1), 3)
            turned_heads(Tile(NT // 2 - 1, 1))
            store(Tile(NT // 2 - 1, 0))
            store(Tile(NT // 2 - 1, 1))
            for i in range(2):
                act.wait_ge(stored[i], 16 * (NT // 2))

        @block.vector
        def _(dve):
            for i in range(2):
                dve.memset(parts[i][:, 0, :, PARTS:64], 0.0).then_inc(ready, 1)
                dve.memset(parts[i][:, 1, :, PARTS:PARTS + LESS], 1.0).then_inc(ready, 1)
                dve.memset(parts[i][:, 1, :, PARTS + LESS:64], 0.0).then_inc(ready, 1)
                dve.memset(va[i][:, :, :, HD0:HD0 + 1], 1.0).then_inc(ready, 1)
                dve.memset(va[i][:, :, :, HD0 + 1:VW], 0.0).then_inc(ready, 1)
            dve.wait_ge(tanh_done, 1)
            dve.wait_ge(ready, 10)

            def projections(tl):
                for c in range(2):
                    dve.wait_ge(proj, tl.times(2, c + 1))
                    if c == 0 and tl.after(2):
                        dve.wait_ge(split, tl.times(1, -1))
                        dve.wait_ge(v_staged, tl.times(1, -1))
                    dve.tensor_tensor(qkv[tl.par][:, :, c, :], ma[c][:, 0:3 * P].rearrange("p (a n) -> p a n", a=3),
                                      bias[:].rearrange("p (a n) -> p a n", a=3), ALU.add).then_inc(proj_out, 1)

            def turned_pairs(tl, f):
                dve.wait_ge(turned, tl.times(4, f + 1))
                dve.tensor_copy(qkT[tl.par][:, f // 2, :, f % 2, :], ma[f % 2][:].bitcast(BF16)
                                .rearrange("p (j t) -> p j t", t=P)).then_inc(turned_out, 1)

            def maxima(tl, h):
                dve.wait_ge(score_q, tl.times(BH, h + 1))
                if h == 0 and tl.after(2):
                    dve.wait_ge(neg, tl.times(2, -2))
                dve.tensor_reduce(top[tl.par][:, h // 2, h % 2, :], mx[h % 2][:], AX.X, ALU.max).then_inc(max_done, 1)

            def negate(tl):
                dve.wait_ge(max_done, tl.times(BH, BH))
                if tl.after(1):
                    dve.wait_ge(neg_turned, tl.times(1, 0))
                m = top[tl.par][:].rearrange("p a r c -> p c (a r)")
                high, low = negm[:, :, 0, :], negm[:, :, 1, :]
                dve.tensor_scalar(high, m, -1.0, None, ALU.mult).then_inc(neg, 1)
                dve.wait_ge(neg, tl.times(2, 1))
                dve.scalar_tensor_tensor(low, m, -1.0, high, ALU.mult, ALU.subtract).then_inc(neg, 1)

            def negated(tl):
                dve.wait_ge(neg_turned, tl.times(1, 1))
                if tl.after(2):
                    dve.wait_ge(neg_in[tl.par], tl.half * 64)
                dve.tensor_copy(negT[tl.par][:].rearrange("p c t -> p (c t)"), ma[0][0:2 * BH, 0:P].bitcast(BF16)
                                ).then_inc(neg_out, 1)

            def divide(tl, g):
                dve.wait_ge(u_turned, tl.times(4, g + 1))
                heads = pv[g % 2][:, 1, :].rearrange("p (c h w) -> p c h w", c=2, w=VW)
                dve.reciprocal(rden[g % 2][:], heads[:, :, :, HD0]).then_inc(rden_done, 1)
                dve.wait_ge(rden_done, tl.times(4, g + 1))
                if g == 0 and tl.after(1):
                    dve.wait_ge(att_turned, tl.times(1, 0))
                dve.tensor_tensor(att[:, :, g * 32:(g + 1) * 32].rearrange("p c (h d) -> p c h d", d=HD0),
                                  heads[:, :, :, 0:HD0], rden[g % 2][:].unsqueeze(3).to_broadcast([P, 2, 4, HD0]), ALU.mult
                                  ).then_inc(att_done, 1)

            def gated(tl):
                dve.wait_ge(out_done, tl.times(1, 1))
                if tl.after(1):
                    dve.wait_ge(x1_done, tl.times(1, 0))
                dve.tensor_scalar(res[:], pv[1][:, 1, :], bo[:, 0:1], tg[:, 0:1], ALU.add, ALU.mult
                                  ).then_inc(res_done, 1)

            def step(tl, a=True, b=True, c=True):
                last, nxt, next2 = tl.plus(-1), tl.plus(1), tl.plus(2)
                for s in range(BH + 7):
                    if b and s < 4:
                        turned_pairs(nxt, s)
                    if tl.after(1) and s == 2:
                        divide(last, 3)
                    if b and 4 <= s < BH + 4:
                        maxima(nxt, s - 4)
                    if a and s == 5:
                        projections(next2)
                    if tl.after(1) and s == 7:
                        gated(last)
                    if c and s >= 14 and s % 4 == 2 and s < 26:
                        divide(tl, (s - 14) // 4)
                    if b and s == BH + 4:
                        negate(nxt)
                if b:
                    negated(nxt)

            projections(Tile(0, 0))
            step(Tile(-1, 1), c=False)
            step(Tile(0, 0))
            step(Tile(0, 1))
            with dve.Fori(1, NT // 2 - 1) as half:
                step(Tile(half, 0))
                step(Tile(half, 1))
            step(Tile(NT // 2 - 1, 0), a=False)
            step(Tile(NT // 2 - 1, 1), a=False, b=False)
            divide(Tile(NT // 2 - 1, 1), 3)
            gated(Tile(NT // 2 - 1, 1))


class Normalise:

    def __init__(self, ctx, nc, gs, tag, x_all, xn_all):
        def sb(name, shape):
            return ctx.enter_context(nc.sbuf_tensor(tag + name, shape, F32))

        self.x_all, self.xn_all = x_all, xn_all
        self.eps, self.stats, self.mv = sb("_eps", [P, 1]), sb("_stats", [P, NT, 6]), sb("_mv", [P, NT, 2])
        self.std, self.rstd = sb("_std", [P, NT]), sb("_rstd", [P, NT])
        self.eps_set, self.stats_done, self.mv_done = gs(tag + "_eps_set"), gs(tag + "_stats_done"), gs(tag + "_mv_done")
        self.std_done, self.rstd_done = gs(tag + "_std_done"), gs(tag + "_rstd_done")
        self.done = gs(tag + "_xn")

    def on_act(self, act):
        act.wait_ge(self.eps_set, 1)
        act.wait_ge(self.mv_done, NT)
        act.activation(self.std[:], self.mv[:, :, 1], ACT.Sqrt, bias=self.eps[:, 0:1]).then_inc(self.std_done, 1)

    def on_dve(self, dve):
        dve.memset(self.eps[:], EPS).then_inc(self.eps_set, 1)
        for t in range(NT):
            dve.bn_stats(self.stats[:, t, :], self.x_all[:, t, :]).then_inc(self.stats_done, 1)
        for t in range(NT):
            dve.wait_ge(self.stats_done, t + 1)
            dve.bn_aggr(self.mv[:, t, :], self.stats[:, t, :]).then_inc(self.mv_done, 1)
        dve.wait_ge(self.std_done, 1)
        dve.reciprocal(self.rstd[:], self.std[:]).then_inc(self.rstd_done, 1)
        dve.wait_ge(self.rstd_done, 1)
        for t in range(NT):
            dve.tensor_scalar(self.xn_all[:, t, :], self.x_all[:, t, :], self.mv[:, t, 0:1],
                              self.rstd[:, t:t + 1], ALU.subtract, ALU.mult).then_inc(self.done, 1)


E0, K0, I0 = 64, 8, 88
G0, GTOP = 8, 4
CAP = 128
SCALE0 = 2.5
NONE = E0 * CAP
KC = D // P


def turned_tiles(bank, gs, tag, src, dst):
    turned, out = gs(tag + "_turned"), gs(tag + "_turned_out")
    fills = NT * KC // 4

    def on_pe(pe, ident, ready=None):
        for f in range(fills):
            if ready is not None:
                pe.wait_ge(ready, 2 * f + 2)
            if f >= 2:
                pe.wait_ge(out, f - 1)
            for j in range(4):
                t, c = f * 2 + j // KC, j % KC
                mm = pe.transpose(bank[f % 2][:, j, :], src[:, t, c * P:(c + 1) * P], ident)
            mm.then_inc(turned, 1)

    def on_act(act):
        for f in range(fills):
            act.wait_ge(turned, f + 1)
            act.copy(dst[:, :, f * 2 * P:(f * 2 + 2) * P].rearrange("p c (t n) -> p t c n", t=2),
                     bank[f % 2][:].rearrange("p (t c) n -> p t c n", c=KC)).then_inc(out, 1)

    return on_pe, on_act, out, fills


ROUTING = {
    "rw": ([P, KC, E0], F32, "rw"), "ebias": ([P, E0], F32, "ebias"), "shg": ([P, KC, I0], F32, "shg"),
    "shu": ([P, KC, I0], F32, "shu"), "shd": ([I0, D], F32, "shd"), "earlier": ([P, P], BF16, "earlier"),
    "onesb": ([P, P], BF16, "onesb"), "below": ([P, G0, G0], F32, "below"), "slot1": ([P, E0], F32, "slot1"),
    "iota": ([P, CAP], F32, "iota"), "tok": ([P, NT], F32, "tok")}


def routing(nc, gs, x1_all, xn2, c0, c1, ck, w, shared_out, idx_out, y_zero, slot_ids, slot_w, keysT, keysN,
            aw, bp):
    ctx = ExitStack()
    with ctx:
        def sb(name, shape, dt=F32):
            return ctx.enter_context(nc.sbuf_tensor("r_" + name, shape, dt))

        def ps(name, shape, dt):
            return ctx.enter_context(nc.psum_tensor("r_" + name, shape, dt))

        NE = NT * E0
        ident = c0["ident"]
        rw, ebias, shg, shu, shd, earlier, onesb, below, slot1, iota, tok = (c1[n] for n in ROUTING)
        xn_all = x1_all
        norm = Normalise(ctx, nc, gs, "r", x1_all, xn_all)
        xT = sb("xT", [P, KC, T])
        gate_h = [sb(f"gate_h{i}", [I0, 512]) for i in range(2)]
        up_h = [sb(f"up_h{i}", [I0, 512]) for i in range(2)]
        turned_place = sb("turned_place", [P, T])
        hT = turned_place[0:I0, :]
        sh = sb("sh", [P, 2, D])
        zero = sb("zero", [1, D])
        score = sb("score", [P, NT, E0])
        sc = sb("sc", [P, NT, E0])
        hi = [sb(f"hi{n}", [P, NT * G0, 4 >> n]) for n in range(3)]
        lo = [sb(f"lo{n}", [P, NT * G0, 4 >> n]) for n in range(3)]
        tmp = sb("tmp", [P, NT * G0, 2])
        group = sb("group", [P, NT, G0])
        gt = sb("gt", [P, NT, G0, G0])
        eq = sb("eq", [P, NT, G0, G0])
        rank = sb("rank", [P, NT, G0])
        best = sb("best", [P, NT, K0])
        gone = sb("gone", [P, NT, E0])
        sel = sb("sel", [P, NT, E0])
        selb = sb("selb", [P, NT, E0], BF16)
        before = sb("before", [P, NT, E0], BF16)
        wsum = sb("wsum", [P, NT])
        wt = sb("wt", [P, NT, E0])
        slot = sb("slot", [P, NT, E0])
        mine = sb("mine", [P, NT, K0])
        empty = sb("empty", [P, NT, K0])
        idx = sb("idx", [P, NT, K0], U32)
        cidx = sb("cidx", [P, NT, K0], U32)
        cpos = sb("cpos", [P, NT, K0])
        val = sb("val", [P, NT, 3, E0], F16)
        onec = [sb(f"onec{i}", [P, K0, CAP], F16) for i in range(2)]
        onee = [sb(f"onee{i}", [P, K0, E0], F16) for i in range(2)]
        ev = [sb(f"ev{i}", [P, K0, 3, E0], F16) for i in range(2)]
        stage = sb("stage", [P, 3, E0])

        logits_done = gs("r_logits")
        score_done = gs("r_score")
        up_done = gs("r_up")
        silu_done = gs("r_silu")
        h_done = gs("r_h")
        down_done = gs("r_down")
        sh_out = gs("r_sh_out")
        sh_stored = [gs(f"r_sh_stored{i}") for i in range(2)]
        chain = gs("r_steps")
        sel_done = gs("r_sel")
        pos_done = gs("r_pos")
        val_done = gs("r_val")
        onec_done = gs("r_onec")
        ev_high_done = gs("r_ev_high")
        onee_done = gs("r_onee")
        ev_done = gs("r_ev")
        spread_done = gs("r_spread")
        idx_done = gs("r_idx")
        stored = gs("r_stored")
        zeroed = gs("r_zeroed")

        block = ctx.enter_context(nc.Block())
        turn = [ps(f"turn{i}", [P, 4, P], F32) for i in range(2)]
        turn_pe, turn_act, xT_out, xT_fills = turned_tiles(turn, gs, "r", xn_all, xT)
        lg = ps("lg", [P, NT, E0], F32)
        up = ps("up", [P, 2, 512], F32)
        down = [ps(f"down{i}", [P, 2, D], F32) for i in range(2)]
        flat = [d[:].rearrange("p a n -> p (a n)") for d in down]
        keys = Layer1Keys(nc, ctx, gs, ck, turned_place, ident, turn, flat, keysT, keysN, aw, bp)

        @block.sync
        def _(sp):
            sp.wait_ge(norm.done, NT)
            sp.dma_start(xn2.rearrange("(t p) d -> p t d", p=P), xn_all[:]).then_inc(stored, 16)
            sp.wait_ge(zeroed, 1)
            sp.dma_start(y_zero, zero[:]).then_inc(stored, 16)
            for p in range(NT // 2):
                sp.wait_ge(sh_out, p + 1)
                sp.dma_start(shared_out.rearrange("(t p) d -> p t d", p=P)[:, 2 * p:2 * p + 2, :], sh[:]
                             ).then_inc(sh_stored[0], 16)
            keys.store(sp)
            sp.wait_ge(idx_done, 1)
            sp.dma_start(idx_out.rearrange("(t p) k -> p t k", p=P), idx[:]).then_inc(stored, 16)
            sp.wait_ge(stored, 48)
            sp.wait_ge(sh_stored[0], 16 * (NT // 2))
            sp.wait_ge(keys.stored, 48)

        @block.tensor
        def _(pe):
            keys.turn_context(pe)
            turn_pe(pe, ident[:], norm.done)
            pe.wait_ge(xT_out, xT_fills)
            for t in range(NT):
                for c in range(KC):
                    mm = pe.matmul(lg[:, t, :], xT[:, c, t * P:(t + 1) * P], rw[:, c, :], start=(c == 0),
                                   stop=(c == KC - 1))
            mm.then_inc(logits_done, 1)
            for b in range(4):
                if b:
                    pe.wait_ge(silu_done, 2 * b)
                for n, wt_ in enumerate((shg, shu)):
                    for c in range(KC):
                        mm = pe.matmul(up[0:I0, n, :], wt_[:, c, :], xT[:, c, b * 512:(b + 1) * 512],
                                       start=(c == 0), stop=(c == KC - 1))
                mm.then_inc(up_done, 1)
            pe.wait_ge(h_done, 4)
            for p in range(NT // 2):
                if p >= 2:
                    pe.wait_ge(sh_out, p - 1)
                for j in range(2):
                    t = 2 * p + j
                    mm = pe.matmul(down[p % 2][:, j, :], hT[:, t * P:(t + 1) * P], shd[:], start=True, stop=True)
                mm.then_inc(down_done, 1)
            pe.wait_ge(sel_done, 1)
            for n in range(2):
                tiles = slice(n * NT // 2, (n + 1) * NT // 2)
                pe.matmul(lg[:, tiles, :], earlier[:], selb[:, tiles, :], start=True, stop=False)
                mm = pe.matmul(lg[:, tiles, :], onesb[:], before[:, tiles, :], start=False, stop=True)
            mm.then_inc(pos_done, 1)

            pe.wait_ge(sh_out, NT // 2)
            keys.latent_keys(pe)

            def spread(tl):
                pe.wait_ge(onec_done, tl.times(1, 1))
                pe.wait_ge(ev_done, tl.times(1, 1))
                pe.wait_ge(ev_high_done, tl.times(1, 1))
                first, last = tl.t == 0, isinstance(tl.t, int) and tl.t == NT - 1
                for k in range(K0):
                    mm = pe.matmul(up[:, 0, 0:3 * E0], onec[tl.par][:, k, :],
                                   ev[tl.par][:, k].rearrange("p v e -> p (v e)"),
                                   start=bool(isinstance(tl.t, int) and first and k == 0),
                                   stop=(last and k == K0 - 1), skip_group_check=True)
                mm.then_inc(spread_done, 1)

            pieces = (keys.rotated_keys, keys.key_products, keys.query_products, keys.output_products)
            for n, piece in enumerate(pieces):
                spread(Tile(n, 0))
                spread(Tile(n, 1))
                piece(pe)
            with pe.Fori(len(pieces), NT // 2 - 1) as half:
                spread(Tile(half, 0))
                spread(Tile(half, 1))
            spread(Tile(NT // 2 - 1, 0))
            spread(Tile(NT // 2 - 1, 1))

        @block.scalar
        def _(act):
            keys.turn_act(act)
            norm.on_act(act)
            turn_act(act)
            act.wait_ge(logits_done, 1)
            act.activation(score[:], lg[:], ACT.Sigmoid).then_inc(score_done, 1)
            for b in range(4):
                act.wait_ge(up_done, b + 1)
                if b >= 2:
                    act.wait_ge(h_done, b - 1)
                act.activation(gate_h[b % 2][:], up[0:I0, 0, :], ACT.Silu).then_inc(silu_done, 1)
                act.copy(up_h[b % 2][:], up[0:I0, 1, :]).then_inc(silu_done, 1)
            for p in range(NT // 2):
                act.wait_ge(down_done, p + 1)
                if p:
                    act.wait_ge(sh_stored[0], 16 * p)
                act.copy(sh[:], down[p % 2][:]).then_inc(sh_out, 1)
            keys.copies(act)

        @block.gpsimd
        def _(pool):
            held = Held(pool, gs("r_pool_passed"))
            for b in range(4):
                pool.wait_ge(silu_done, 2 * b + 2)
                pool.tensor_tensor(hT[:, b * 512:(b + 1) * 512], gate_h[b % 2][:], up_h[b % 2][:], ALU.mult
                                   ).then_inc(h_done, 1)

            def tokens_and_high(tl):
                held.wait_ge(onee_done, tl.times(1, 1))
                if tl.after(2):
                    held.wait_ge(spread_done, tl.times(1, -1))
                pool.tensor_tensor(ev[tl.par][:, :, 0:2, :], onee[tl.par][:].unsqueeze(2).to_broadcast([P, K0, 2, E0]),
                                   val[:, bass.ds(tl.t, 1), 0:2].rearrange("p o v e -> p (o v) e").unsqueeze(1)
                                   .to_broadcast([P, K0, 2, E0]), ALU.mult).then_inc(ev_high_done, 1)

            tokens_and_high(Tile(0, 0))
            tokens_and_high(Tile(0, 1))
            keys.rotate(pool, 0, 0)
            tokens_and_high(Tile(1, 0))
            tokens_and_high(Tile(1, 1))
            keys.rotate(pool, 0, 1)
            with pool.Fori(2, NT // 2) as half:
                tokens_and_high(Tile(half, 0))
                tokens_and_high(Tile(half, 1))

        @block.vector
        def _(dve):
            steps = [0]

            def link(ins):
                steps[0] += 1
                ins.then_inc(chain, 1)
                dve.wait_ge(chain, steps[0])

            norm.on_dve(dve)
            dve.memset(zero[:], 0.0).then_inc(zeroed, 1)
            dve.wait_ge(score_done, 1)
            link(dve.tensor_tensor(sc[:], score[:], ebias[:].unsqueeze(1).to_broadcast([P, NT, E0]), ALU.add))
            eight = sc[:].rearrange("p t (g m) -> p (t g) m", m=8)
            link(dve.tensor_tensor(hi[0][:], eight[:, :, 0:4], eight[:, :, 4:8], ALU.max))
            link(dve.tensor_tensor(lo[0][:], eight[:, :, 0:4], eight[:, :, 4:8], ALU.min))
            for n in range(2):
                m = 2 >> n
                h1, h2 = hi[n][:, :, 0:m], hi[n][:, :, m:2 * m]
                link(dve.tensor_tensor(hi[n + 1][:], h1, h2, ALU.max))
                link(dve.tensor_tensor(lo[n + 1][:], h1, h2, ALU.min))
                link(dve.tensor_tensor(tmp[:, :, 0:m], lo[n][:, :, 0:m], lo[n][:, :, m:2 * m], ALU.max))
                link(dve.tensor_tensor(lo[n + 1][:], lo[n + 1][:], tmp[:, :, 0:m], ALU.max))
            link(dve.tensor_tensor(group[:].rearrange("p t g -> p (t g)"), hi[2][:, :, 0], lo[2][:, :, 0], ALU.add))
            full = [P, NT, G0, G0]
            other, own = group[:].unsqueeze(2).to_broadcast(full), group[:].unsqueeze(3).to_broadcast(full)
            link(dve.tensor_tensor(gt[:], other, own, ALU.is_gt))
            link(dve.tensor_tensor(eq[:], other, own, ALU.is_equal))
            link(dve.tensor_tensor(eq[:], eq[:], below[:].unsqueeze(1).to_broadcast(full), ALU.mult))
            link(dve.tensor_tensor(gt[:], gt[:], eq[:], ALU.add))
            link(dve.tensor_reduce(rank[:], gt[:], AX.X, ALU.add))
            link(dve.tensor_scalar(rank[:], rank[:], float(GTOP) - 0.5, None, ALU.is_lt))
            link(dve.tensor_tensor(sc[:].rearrange("p t (g m) -> p (t g) m", m=8), eight,
                                   rank[:].rearrange("p t g -> p (t g)").unsqueeze(2).to_broadcast([P, NT * G0, 8]),
                                   ALU.mult))
            for t in range(NT):
                ins = dve.max(best[:, t, :], sc[:, t, :])
                if t == NT - 1:
                    link(ins)
            link(dve.memset(before[:, 0, :], 0.0))
            for t in range(NT):
                ins = dve.match_replace(gone[:, t, :], best[:, t, :], sc[:, t, :], -1e30)
                if t == NT - 1:
                    link(ins)
            link(dve.tensor_tensor(sel[:], gone[:], sc[:], ALU.is_lt))
            link(dve.tensor_copy(selb[:], sel[:]))
            for t in range(1, NT):
                link(dve.tensor_tensor(before[:, t, :], before[:, t - 1, :], selb[:, t - 1, :], ALU.add))
            dve.tensor_tensor(wt[:], score[:], sel[:], ALU.mult).then_inc(sel_done, 1)
            dve.wait_ge(sel_done, 1)
            link(dve.tensor_reduce(wsum[:], wt[:], AX.X, ALU.add))
            link(dve.tensor_scalar(wsum[:], wsum[:], 1e-20, None, ALU.add))
            link(dve.reciprocal(wsum[:], wsum[:]))
            link(dve.tensor_tensor(wt[:], wt[:], wsum[:].unsqueeze(2).to_broadcast([P, NT, E0]), ALU.mult))
            link(dve.tensor_scalar(wt[:], wt[:], SCALE0, None, ALU.mult))
            link(dve.tensor_copy(val[:, :, 1, :], wt[:]))
            link(dve.tensor_tensor(val[:, :, 2, :], wt[:], val[:, :, 1, :], ALU.subtract))
            link(dve.tensor_copy(val[:, :, 0, :], tok[:].unsqueeze(2).to_broadcast([P, NT, E0])))
            dve.wait_ge(pos_done, 1)
            link(dve.tensor_scalar(slot[:], lg[:], float(CAP) - 0.5, None, ALU.is_lt))
            link(dve.tensor_tensor(sel[:], sel[:], slot[:], ALU.mult))
            link(dve.tensor_tensor(slot[:], lg[:], slot1[:].unsqueeze(1).to_broadcast([P, NT, E0]), ALU.add))
            link(dve.tensor_tensor(slot[:], slot[:], sel[:], ALU.mult))
            for t in range(NT):
                ins = dve.max(mine[:, t, :], slot[:, t, :])
                if t == NT - 1:
                    link(ins)
            link(dve.tensor_scalar(empty[:], mine[:], 0.0, float(NONE + 1), ALU.is_equal, ALU.mult))
            link(dve.tensor_tensor(cpos[:], mine[:], empty[:], ALU.add))
            dve.tensor_scalar(idx[:], cpos[:], -1.0, None, ALU.add).then_inc(idx_done, 1)
            dve.wait_ge(idx_done, 1)
            link(dve.tensor_scalar(cidx[:], idx[:], CAP - 1, None, ALU.bitwise_and))
            link(dve.tensor_copy(cpos[:], cidx[:]))
            link(dve.tensor_tensor(cpos[:], cpos[:], empty[:], ALU.add))

            def one_hots(tl):
                if tl.after(2):
                    dve.wait_ge(spread_done, tl.times(1, -1))
                here = bass.ds(tl.t, 1)

                def of(a):
                    return a[:, here].rearrange("p o k -> p (o k)")

                if tl.after(2):
                    dve.wait_ge(ev_high_done, tl.times(1, -1))
                dve.tensor_tensor(onee[tl.par][:], of(slot).unsqueeze(1).to_broadcast([P, K0, E0]),
                                  of(mine).unsqueeze(2).to_broadcast([P, K0, E0]), ALU.is_equal
                                  ).then_inc(onee_done, 1)
                dve.tensor_tensor(onec[tl.par][:], iota[:].unsqueeze(1).to_broadcast([P, K0, CAP]),
                                  of(cpos).unsqueeze(2).to_broadcast([P, K0, CAP]), ALU.is_equal
                                  ).then_inc(onec_done, 1)
                dve.wait_ge(onee_done, tl.times(1, 1))
                dve.tensor_tensor(ev[tl.par][:, :, 2, :], onee[tl.par][:],
                                  val[:, here, 2].rearrange("p o e -> p (o e)").unsqueeze(1)
                                  .to_broadcast([P, K0, E0]), ALU.mult).then_inc(ev_done, 1)

            for t in range(4):
                one_hots(Tile(t // 2, t % 2))
            for q in range(2, 4):
                keys.rotate(dve, 1, q)
            with dve.Fori(2, NT // 2) as half:
                one_hots(Tile(half, 0))
                one_hots(Tile(half, 1))
            dve.wait_ge(spread_done, NT)
            link(dve.tensor_copy(stage[:].rearrange("p v e -> p (v e)"), up[:, 0, 0:3 * E0]))
            link(dve.tensor_copy(slot_ids[:], stage[:, 0, :]))
            link(dve.tensor_tensor(slot_w[:], stage[:, 1, :], stage[:, 2, :], ALU.add))


NX = 4


def expert(e):
    return Tile(e // NX, e % NX, NX, E0)


def expert_steps(eng, step):
    for e in range(NX):
        step(expert(e))
    with eng.Fori(1, E0 // NX - 1) as some:
        for par in range(NX):
            step(Tile(some, par, NX, E0))
    for e in range(E0 - NX, E0):
        step(expert(e))


def experts(nc, gs, xn2, w, c0, slot_ids, slot_w, y_out, early):
    ctx = ExitStack()
    with ctx:
        def sb(name, shape, dt=F32):
            return ctx.enter_context(nc.sbuf_tensor("e_" + name, shape, dt))

        def ps(name, shape):
            return ctx.enter_context(nc.psum_tensor("e_" + name, shape, F32))

        ident = c0["ident"]
        gu = [sb(f"gu{i}", [P, KC, 2, I0]) for i in range(NX)]
        dn = [sb(f"dn{i}", [I0, D]) for i in range(NX)]
        ids = [sb(f"ids{i}", [P, 1], U32) for i in range(NX)]
        x = [sb(f"x{i}", [P, D]) for i in range(NX)]
        xT = [sb(f"xT{i}", [P, KC, P]) for i in range(2)]
        sg = [sb(f"sg{i}", [I0, P]) for i in range(2)]
        h = [sb(f"h{i}", [I0, P]) for i in range(2)]
        y = [sb(f"y{i}", [P, D]) for i in range(NX)]
        pt = [ps(f"pt{i}", [P, KC, P]) for i in range(2)]
        pg = [ps(f"pg{i}", [P, 2, P]) for i in range(2)]
        py = [ps(f"py{i}", [P, D]) for i in range(2)]

        landed = gs("e_landed")
        gu_in = [gs(f"e_gu_in{i}") for i in range(NX)]
        dn_in = [gs(f"e_dn_in{i}") for i in range(NX)]
        ids_done = gs("e_ids")
        x_in = [gs(f"e_x_in{i}") for i in range(NX)]
        turned = gs("e_turned")
        xT_done = gs("e_xT")
        up_done = gs("e_up")
        silu_done = gs("e_silu")
        h_done = gs("e_h")
        down_done = gs("e_down")
        y_done = gs("e_y")
        stored = [gs(f"e_stored{i}") for i in range(NX)]
        passed = gs("e_pool_passed")
        block = ctx.enter_context(nc.Block())

        @block.sync
        def _(sp):
            def load(e):
                at = e.t if isinstance(e.t, int) else sp.snap(e.t)
                used = e.times(1, 1 - NX) if isinstance(e.t, int) else sp.snap(e.times(1, 1 - NX))
                if e.after(NX):
                    sp.wait_ge(up_done, used)
                sp.dma_start(gu[e.par][:], w["gu"][bass.ds(at, 1)].rearrange("o p c g i -> p (o c) g i")
                             ).then_inc(gu_in[e.par], 16)
                if e.after(NX):
                    sp.wait_ge(down_done, used)
                sp.dma_start(dn[e.par][:], w["dn"][bass.ds(at, 1)].rearrange("o i d -> i (o d)")
                             ).then_inc(dn_in[e.par], 16)

            expert_steps(sp, load)
            preload(sp, early, landed)
            sp.wait_ge(landed, 16 * len(early))

        @block.gpsimd
        def _(pool):
            held = Held(pool, passed)

            def fetch_ids(e):
                if e.after(NX):
                    held.wait_ge(x_in[e.par], e.half * 16)
                pool.tensor_copy(ids[e.par][:], slot_ids[:, bass.ds(e.t, 1)]).then_inc(ids_done, 1)

            def gather(e):
                if e.before(1):
                    fetch_ids(e.plus(1))
                held.wait_ge(ids_done, e.times(1, 1))
                if e.after(NX):
                    held.wait_ge(turned, e.times(1, 1 - NX))
                pool.indirect_dma_start(x[e.par][:], None, xn2, bass.IndirectOffsetOnAxis(ap=ids[e.par][:, 0:1], axis=0),
                                        bounds_check=T - 1, oob_is_err=False).then_inc(x_in[e.par], 16)

            fetch_ids(expert(0))
            expert_steps(pool, gather)

        @block.tensor
        def _(pe):
            def turn(e):
                pe.wait_ge(x_in[e.par], e.half * 16 + 16)
                if e.after(2):
                    pe.wait_ge(xT_done, e.times(1, -1))
                for c in range(KC):
                    mm = pe.transpose(pt[e.par % 2][:, c, :], x[e.par][:, c * P:(c + 1) * P], ident[:])
                mm.then_inc(turned, 1)

            def up(e):
                pe.wait_ge(gu_in[e.par], e.half * 16 + 16)
                pe.wait_ge(xT_done, e.times(1, 1))
                if e.after(2):
                    pe.wait_ge(h_done, e.times(1, -1))
                for g in range(2):
                    for c in range(KC):
                        mm = pe.matmul(pg[e.par % 2][0:I0, g, :], gu[e.par][:, c, g, :], xT[e.par % 2][:, c, :],
                                       start=(c == 0), stop=(c == KC - 1))
                mm.then_inc(up_done, 1)

            def down(e):
                pe.wait_ge(dn_in[e.par], e.half * 16 + 16)
                pe.wait_ge(h_done, e.times(1, 1))
                if e.after(2):
                    pe.wait_ge(y_done, e.times(1, -1))
                pe.matmul(py[e.par % 2][:], h[e.par % 2][:], dn[e.par][:], start=True, stop=True).then_inc(down_done, 1)

            def step(e):
                if e.before(1):
                    turn(e.plus(1))
                up(e)
                if e.after(1):
                    down(e.plus(-1))

            turn(expert(0))
            expert_steps(pe, step)
            down(expert(E0 - 1))

        @block.scalar
        def _(act):
            def rows(e):
                act.wait_ge(turned, e.times(1, 1))
                if e.after(2):
                    act.wait_ge(up_done, e.times(1, -1))
                act.copy(xT[e.par % 2][:], pt[e.par % 2][:]).then_inc(xT_done, 1)

            def silu(e):
                act.wait_ge(up_done, e.times(1, 1))
                if e.after(2):
                    act.wait_ge(h_done, e.times(1, -1))
                act.activation(sg[e.par % 2][:], pg[e.par % 2][0:I0, 0, :], ACT.Silu).then_inc(silu_done, 1)

            def store(e):
                act.wait_ge(y_done, e.times(1, 1))
                act.dma_start(y_out[bass.ds(e.t * CAP, CAP), :], y[e.par][:]).then_inc(stored[e.par], 16)

            def step(e):
                if e.before(1):
                    rows(e.plus(1))
                silu(e)
                if e.after(2):
                    store(e.plus(-2))

            rows(expert(0))
            expert_steps(act, step)
            store(expert(E0 - 2))
            store(expert(E0 - 1))
            for par in range(NX):
                act.wait_ge(stored[par], 16 * (E0 // NX))

        @block.vector
        def _(dve):
            def inner(e):
                dve.wait_ge(silu_done, e.times(1, 1))
                if e.after(2):
                    dve.wait_ge(down_done, e.times(1, -1))
                dve.tensor_tensor(h[e.par % 2][:], sg[e.par % 2][:], pg[e.par % 2][0:I0, 1, :], ALU.mult).then_inc(h_done, 1)

            def weigh(e):
                dve.wait_ge(down_done, e.times(1, 1))
                if e.after(NX):
                    dve.wait_ge(stored[e.par], e.half * 16)
                dve.tensor_scalar(y[e.par][:], py[e.par % 2][:], slot_w[:, bass.ds(e.t, 1)], None, ALU.mult
                                  ).then_inc(y_done, 1)

            def step(e):
                inner(e)
                if e.after(1):
                    weigh(e.plus(-1))

            expert_steps(dve, step)
            weigh(expert(E0 - 1))




H1, HD1, KVC, QC, R1, BACK = 16, 128, 64, 96, 64, 8
HP = H1 // 2
NEG = -1e30


LAYER1_KEYS = {
    "wkvc2": ([P, KC, 2 * KVC], F32, "wkvc2"),
    "wkr": ([KVC, 2, 2 * R1], F32, "wkr"),
    "kcos": ([P, S], F32, "kcos"), "ksin": ([P, S], F32, "ksin"),
    "wuqT": ([HD1, H1, QC], F32, "wuqT"), "wukT": ([HD1, H1, KVC], F32, "wukT"),
    "wuvT": ([HD1, H1, KVC], F32, "wuvT"), "wo": ([HD1, H1, D], F32, "wo1")}
LAYER1_ATTENTION = {
    "wdq": ([P, KC, QC], F32, "wdq"),
    "wqr": ([QC, H1, 2 * R1], F32, "wqr"),
    "qtab": ([P, S], F32, "qtab"),
    "keyno": ([P, S], F32, "keyno"),
    "seg": ([P, B], mybir.dt.int32, "seg"),
    "gate": ([P, 1], F32, "g10"), "gate_f": ([P, 1], F32, "g01")}


class Layer1Keys:

    def __init__(self, nc, ctx, gs, ck, kT, ident, turn, bank, keysT, keysN, aw, bp):
        def sb(name, shape, dt=F32):
            return ctx.enter_context(nc.sbuf_tensor("k_" + name, shape, dt))

        self.ident, self.bank = ident, bank
        self.keysT, self.keysN, self.aw, self.bp = keysT, keysN, aw, bp
        self.ctx_all = ck["ctx"]
        self.ctxT = sb("ctxT", [P, KC, T])
        self.wkvc2, self.wkr, self.kcos, self.ksin, self.wuqT, self.wukT, self.wuvT, self.wo = (
            ck[n] for n in LAYER1_KEYS)
        self.kT = kT
        place = self.ctx_all[:].rearrange("p t d -> p (t d)")
        RAW = T + NT * KVC
        self.rT = place[:, 0:T]
        self.kN = place[:, T:T + NT * KVC].rearrange("p (t l) -> p t l", l=KVC)
        self.raw = [self.ctxT[:, n, :] for n in range(2)]
        self.rs = [place[:, RAW + n * 512:RAW + (n + 1) * 512] for n in range(2)]
        self.kT_mm, self.kT_done = gs("k_kT_mm"), gs("k_kT")
        self.rope_mm = gs("k_rope_mm")
        self.raw_out = gs("k_raw_out")
        self.cos_done, self.sin_done, self.rope_done = ([gs(f"k_{n}{i}") for i in range(2)] for n in ("cos", "sin", "rope"))
        self.kN_mm, self.kN_done = gs("k_kN_mm"), gs("k_kN")
        self.aw_mm, self.aw_done = gs("k_aw_mm"), gs("k_aw")
        self.bp_mm, self.bp_done = gs("k_bp_mm"), gs("k_bp")
        self.stored = gs("k_stored")
        self.turn_pe, self.turn_act, self.ctxT_out, self.fills = turned_tiles(turn, gs, "k", self.ctx_all, self.ctxT)

    def store(self, sp):
        tiles = self.keysT.rearrange("(t p) c -> p t c", p=P)
        sp.wait_ge(self.kT_done, 4)
        sp.dma_start(tiles[:, :, 0:P], self.kT[:].rearrange("p (t c) -> p t c", c=P)).then_inc(self.stored, 16)
        for n in range(2):
            sp.wait_ge(self.rope_done[n], 2)
        sp.dma_start(tiles[:, :, P:2 * P], self.rT.rearrange("p (t c) -> p t c", c=P)).then_inc(self.stored, 16)
        sp.wait_ge(self.kN_done, 2)
        sp.dma_start(self.keysN.rearrange("(t p) c -> p t c", p=P), self.kN).then_inc(self.stored, 16)

    def turn_context(self, pe):
        self.turn_pe(pe, self.ident[:])
        pe.wait_ge(self.ctxT_out, self.fills)

    def latent_keys(self, pe):
        bank = self.bank
        for q in range(4):
            if q >= 2:
                pe.wait_ge(self.kT_done, q - 1)
            for c in range(KC):
                mm = pe.matmul(bank[q % 2], self.wkvc2[:, c, :], self.ctxT[:, c, q * 512:(q + 1) * 512],
                               start=(c == 0), stop=(c == KC - 1))
            mm.then_inc(self.kT_mm, 1)

    def rotated_keys(self, pe):
        bank = self.bank
        pe.wait_ge(self.kT_done, 4)
        for q in range(4):
            if q:
                pe.wait_ge(self.raw_out, 2 * q)
            for n in range(2):
                mm = pe.matmul(bank[n], self.wkr[:, n, :], self.kT[0:KVC, q * 512:(q + 1) * 512],
                               start=True, stop=True)
            mm.then_inc(self.rope_mm, 1)

    def key_products(self, pe):
        bank, kT, ident = self.bank, self.kT, self.ident
        pe.wait_ge(self.raw_out, 8)
        for n in range(2):
            for t in range(8 * n, 8 * n + 8):
                for b in range(2):
                    rows = slice(64 * b, 64 * b + 64)
                    mm = pe.matmul(bank[n][rows, (t % 8) * KVC:(t % 8 + 1) * KVC],
                                   kT[rows, (2 * t + b) * S:(2 * t + b + 1) * S],
                                   ident[rows, 64 * b:64 * b + KVC], start=True, stop=True)
            mm.then_inc(self.kN_mm, 1)

    def query_products(self, pe):
        bank = self.bank
        for n in range(2):
            pe.wait_ge(self.kN_done, 1 + n)
            for h in range(8 * n, 8 * n + 8):
                mm = pe.matmul(bank[n][0:QC, (h % 8) * KVC:(h % 8 + 1) * KVC], self.wuqT[:, h, :], self.wukT[:, h, :],
                               start=True, stop=True)
            mm.then_inc(self.aw_mm, 1)

    def output_products(self, pe):
        bank = self.bank
        for n in range(HP // 2):
            if n < 2:
                pe.wait_ge(self.aw_done, n + 1)
            else:
                pe.wait_ge(self.bp_done, n - 1)
            for hp in (2 * n, 2 * n + 1):
                for r in range(2):
                    mm = pe.matmul(bank[n % 2][64 * r:64 * r + 64, (hp % 2) * D:(hp % 2 + 1) * D],
                                   self.wuvT[:, 2 * hp + r, :], self.wo[:, 2 * hp + r, :], start=True, stop=True)
            mm.then_inc(self.bp_mm, 1)

    def copies(self, act):
        bank = self.bank
        for q in range(4):
            act.wait_ge(self.kT_mm, q + 1)
            act.copy(self.kT[:, q * 512:(q + 1) * 512], bank[q % 2]).then_inc(self.kT_done, 1)
        for q in range(4):
            act.wait_ge(self.rope_mm, q + 1)
            act.copy(self.raw[0][:, q * 512:(q + 1) * 512], bank[0]).then_inc(self.raw_out, 1)
            act.copy(self.raw[1][:, q * 512:(q + 1) * 512], bank[1]).then_inc(self.raw_out, 1)
        for n in range(2):
            act.wait_ge(self.kN_mm, n + 1)
            act.copy(self.kN[:, 8 * n:8 * n + 8, :].rearrange("p t l -> p (t l)"), bank[n]).then_inc(self.kN_done, 1)
        for n in range(2):
            act.wait_ge(self.aw_mm, n + 1)
            act.copy(self.aw[:, 4 * n:4 * n + 4, :].rearrange("p a b -> p (a b)"), bank[n][0:QC, :]
                     ).then_inc(self.aw_done, 1)
        for n in range(HP // 2):
            act.wait_ge(self.bp_mm, n + 1)
            act.copy(self.bp[:, 2 * n:2 * n + 2, :].rearrange("p a b -> p (a b)"), bank[n % 2]
                     ).then_inc(self.bp_done, 1)

    def rotate(self, eng, n, q):
        block, mine, rs = slice(q * 512, (q + 1) * 512), q % 2 + 1, self.rs[n]
        out = self.rT[:, block]

        def of(a):
            return a.rearrange("p (b s) -> p b s", s=S)

        def at_positions(table):
            return table[:].unsqueeze(1).to_broadcast([P, 8, S])

        eng.wait_ge(self.raw_out, 2 * q + 2)
        if mine == 2:
            eng.wait_ge(self.rope_done[n], 1)
        eng.tensor_tensor(of(out), of(self.raw[0][:, block]), at_positions(self.kcos), ALU.mult
                          ).then_inc(self.cos_done[n], 1)
        eng.tensor_tensor(of(rs), of(self.raw[1][:, block]), at_positions(self.ksin), ALU.mult
                          ).then_inc(self.sin_done[n], 1)
        eng.wait_ge(self.cos_done[n], mine)
        eng.wait_ge(self.sin_done[n], mine)
        eng.tensor_tensor(out, out, rs, ALU.add).then_inc(self.rope_done[n], 1)


def attention_steps(eng, step):
    for t in range(2):
        step(Tile(t // 2, t % 2))
    with eng.Fori(1, NT // 2 - 2) as half:
        step(Tile(half, 0))
        step(Tile(half, 1))
    for t in range(NT - 4, NT):
        step(Tile(t // 2, t % 2))


def layer1_attention(nc, gs, c0, c1, x1, shared, idx, y_in, keysT, keysN, aw, bp, x3_all, early):
    ctx = ExitStack()
    with ctx:
        def sb(name, shape, dt=F32):
            return ctx.enter_context(nc.sbuf_tensor("b_" + name, shape, dt))

        def ps(name, shape, dt=F32):
            return ctx.enter_context(nc.psum_tensor("b_" + name, shape, dt))

        ident = c0["ident"]
        wdq, wqr, qtab, keyno, seg_i, gate, gate_f = (c1[n] for n in LAYER1_ATTENTION)
        seg = sb("seg", [P, B])
        tg, tg_f = sb("tg", [P, 1]), sb("tg_f", [P, 1])
        eps = sb("eps", [P, 1])
        ix = [sb(f"ix{i}", [P, K0], U32) for i in range(2)]
        rows = [sb(f"rows{i}", [P, K0, D]) for i in range(2)]
        x_old = [sb(f"x_old{i}", [P, D]) for i in range(2)]
        sh = [sb(f"sh{i}", [P, D]) for i in range(2)]
        moe = sb("moe", [P, D])
        x_new = [sb(f"x_new{i}", [P, D]) for i in range(2)]
        stats = sb("stats", [P, 6])
        mv = [sb(f"mv{i}", [P, 2]) for i in range(2)]
        rstd = [sb(f"rstd{i}", [P, 1]) for i in range(2)]
        xn = [sb(f"xn{i}", [P, D]) for i in range(2)]
        x = [sb(f"x{i}", [P, D]) for i in range(2)]
        krT = [sb(f"krT{i}", [P, 2, P]) for i in range(2)]
        kN = [sb(f"kN{i}", [P, KVC]) for i in range(2)]
        xT = sb("xT", [P, KC, P])
        qc = sb("qc", [QC, P])
        qn = sb("qn", [P, HP, P])
        qr = sb("qr", [P, H1, P])
        mask = sb("mask", [P, 2, S])
        mask2 = sb("mask2", [P, 2, S])
        sT = sb("sT", [P, HP, 2, S])
        s = sb("s", [P, HP, 2, S])
        top = sb("top", [P, H1])
        e = sb("e", [P, HP, 2, S])
        total = sb("total", [P, H1])
        p = sb("p", [P, HP, 2, S])
        pT = sb("pT", [P, HP, P])
        u = sb("u", [P, HP, 2, S])
        x3 = [sb(f"x3{i}", [P, D]) for i in range(2)]
        pa = ps("pa", [P, 512])
        pb = [ps(f"pb{i}", [P, 4, P]) for i in range(2)]
        pc = [ps(f"pc{i}", [P, HP, S]) for i in range(2)]
        pd = [ps(f"pd{i}", [P, 4, P]) for i in range(2)]
        pu = ps("pu", [P, HP, S])

        landed = gs("b_landed")
        seg_done, tanh_done = gs("b_seg"), gs("b_tanh")
        eps_set = gs("b_eps")
        ix_in = [gs(f"b_ix_in{i}") for i in range(2)]
        x_in = [gs(f"b_x_in{i}") for i in range(2)]
        rows_in = [gs(f"b_rows_in{i}") for i in range(2)]
        summed, added = gs("b_summed"), gs("b_added")
        x2_done, stats_done, mv_done = gs("b_x2"), gs("b_stats"), gs("b_mv")
        std_done, rstd_done, xn_done = gs("b_std"), gs("b_rstd"), gs("b_xn")
        kept = gs("b_kept")
        k_in = [gs(f"b_k_in{i}") for i in range(2)]
        xT_mm, xT_done = gs("b_xT_mm"), gs("b_xT")
        qc_mm, qc_done = gs("b_qc_mm"), gs("b_qc")
        qn_mm, qn_done = gs("b_qn_mm"), gs("b_qn")
        qr_mm, qr_done = gs("b_qr_mm"), gs("b_qr")
        sT_mm, sT_done = gs("b_sT_mm"), gs("b_sT")
        s_mm, s_done = gs("b_s_mm"), gs("b_s")
        mask_steps, top_done, less_done = gs("b_mask"), gs("b_top"), gs("b_less")
        exp_done, total_steps, p_done = gs("b_exp"), gs("b_total"), gs("b_p")
        pT_mm, pT_done = gs("b_pT_mm"), gs("b_pT")
        u_mm, u_done = gs("b_u_mm"), gs("b_u")
        o_mm, x3_done = gs("b_o_mm"), gs("b_x3")
        x3_kept = gs("b_x3_kept")
        pe_passed, pool_passed = gs("b_pe_passed"), gs("b_pool_passed")
        block = ctx.enter_context(nc.Block())
        @block.sync
        def _(sp):
            def load(tl):
                fixed = isinstance(tl.t, int)
                row = tl.t * P if fixed else sp.snap(tl.t * P)
                used = tl.times(1, -1) if fixed else sp.snap(tl.times(1, -1))
                if tl.after(2):
                    sp.wait_ge(x2_done, used)
                sp.dma_start(ix[tl.par][:], idx[bass.ds(row, P), :]).then_inc(ix_in[tl.par], 16)
                sp.dma_start(x_old[tl.par][:], x1[bass.ds(row, P), :]).then_inc(x_in[tl.par], 16)
                sp.dma_start(sh[tl.par][:], shared[bass.ds(row, P), :]).then_inc(x_in[tl.par], 16)

            def load_keys(tl):
                fixed = isinstance(tl.t, int)
                row = tl.t * P if fixed else sp.snap(tl.t * P)
                weighed = tl.times(2, -2) if fixed else sp.snap(tl.times(2, -2))
                if tl.after(2):
                    sp.wait_ge(u_mm, weighed)
                sp.dma_start(krT[tl.par][:].rearrange("p a n -> p (a n)"), keysT[bass.ds(row, P), :]
                             ).then_inc(k_in[tl.par], 16)
                sp.dma_start(kN[tl.par][:], keysN[bass.ds(row, P), :]
                             ).then_inc(k_in[tl.par], 16)

            for t in range(4):
                load(Tile(t // 2, t % 2))
            load_keys(Tile(0, 0))
            load_keys(Tile(0, 1))

            def step(tl):
                if tl.before(4):
                    load(tl.plus(4))
                if tl.before(2):
                    load_keys(tl.plus(2))

            preload(sp, early, landed)
            attention_steps(sp, step)
            sp.wait_ge(landed, 16 * len(early))

        @block.tensor
        def _(pe):
            held = Held(pe, pe_passed)

            def turn_x(tl):
                pe.wait_ge(xn_done, tl.times(1, 1))
                if tl.after(1):
                    pe.wait_ge(qc_done, tl.times(1, 0))
                for c in range(KC):
                    mm = pe.transpose(pa[:, c * P:(c + 1) * P], xn[tl.par][:, c * P:(c + 1) * P], ident[:])
                mm.then_inc(xT_mm, 1)

            def latent(tl):
                pe.wait_ge(xT_done, tl.times(1, 1))
                for c in range(KC):
                    mm = pe.matmul(pa[0:QC, 2 * P:3 * P], wdq[:, c, :], xT[:, c, :], start=(c == 0), stop=(c == KC - 1))
                mm.then_inc(qc_mm, 1)

            def front(tl):
                pe.wait_ge(qc_done, tl.times(1, 1))
                for f in range(2):
                    if tl.after(1):
                        pe.wait_ge(s_done, tl.times(2, f - 1))
                    for j in range(4):
                        mm = pe.matmul(pb[f][:, j, :], aw[:, 4 * f + j, :], qc[:], start=True, stop=True)
                    mm.then_inc(qn_mm, 1)
                for f in range(4):
                    if f < 2:
                        pe.wait_ge(qn_done, tl.times(2, f + 1))
                    else:
                        pe.wait_ge(qr_done, tl.times(4, f - 1))
                    for j in range(4):
                        mm = pe.matmul(pb[f % 2][:, j, :], wqr[:, 4 * f + j, :], qc[:], start=True, stop=True)
                    mm.then_inc(qr_mm, 1)
                held.wait_ge(k_in[tl.par], tl.half * 32 + 32)
                if tl.after(1):
                    held.wait_ge(sT_done, tl.times(2, 0))
                for r in range(2):
                    rows = slice(64 * r, 64 * r + 64)
                    for b in range(2):
                        own = slice(64 * b, 64 * b + 64)
                        pe.matmul(pc[r][own], krT[tl.par][rows, 0, own], qn[rows, :, own], start=True, stop=False)
                for r in range(2):
                    for b in range(2):
                        own = slice(64 * b, 64 * b + 64)
                        if r == b == 0:
                            pe.wait_ge(qr_done, tl.times(4, 4))
                        mm = pe.matmul(pc[r][own], krT[tl.par][:, 1, own], qr[:, r:H1:2, own], start=False, stop=True)
                    mm.then_inc(sT_mm, 1)

            def turn_scores(tl):
                pe.wait_ge(sT_done, tl.times(2, 2))
                for f in range(2):
                    for j in range(4):
                        mm = pe.transpose(pb[f][:, j, :], sT[:, 4 * f + j].rearrange("p r q -> p (r q)"), ident[:])
                    mm.then_inc(s_mm, 1)

            def turn_probs(tl):
                pe.wait_ge(p_done, tl.times(2, 2))
                if tl.after(1):
                    pe.wait_ge(u_done, tl.times(2, 0))
                    pe.wait_ge(x3_done, tl.times(1, 0))
                for f in range(2):
                    for j in range(4):
                        mm = pe.transpose(pd[f][:, j, :], p[:, 4 * f + j].rearrange("p b k -> p (b k)"), ident[:])
                    mm.then_inc(pT_mm, 1)

            def weigh(tl):
                held.wait_ge(pT_done, tl.times(2, 2))
                for b in range(2):
                    rows = slice(64 * b, 64 * b + 64)
                    to = pu[:] if b == 0 else pd[0][:].rearrange("p a n -> p (a n)").rearrange("p (h q) -> p h q", q=S)
                    for r in range(2):
                        half = slice(64 * r, 64 * r + 64)
                        mm = pe.matmul(to[half], kN[tl.par][rows, :], pT[rows, :, half], start=True, stop=True)
                    mm.then_inc(u_mm, 1)

            def project_out(tl, pairs):
                if pairs[0] == 0:
                    pe.wait_ge(u_done, tl.times(2, 2))
                out = pd[1][:].rearrange("p a n -> p (a n)")[:, 0:D]
                for hp in pairs:
                    mm = pe.matmul(out, u[:, hp].rearrange("p b q -> p (b q)"), bp[:, hp, :],
                                   start=(hp == 0), stop=(hp == HP - 1))
                if pairs[-1] == HP - 1:
                    mm.then_inc(o_mm, 1)

            def step(tl):
                ahead, ahead2 = tl.before(1), tl.before(2)
                if ahead:
                    front(tl.plus(1))
                turn_probs(tl)
                if ahead:
                    turn_scores(tl.plus(1))
                weigh(tl)
                if ahead2:
                    turn_x(tl.plus(2))
                project_out(tl, range(0, HP // 2))
                if ahead2:
                    latent(tl.plus(2))
                project_out(tl, range(HP // 2, HP))

            turn_x(Tile(0, 0))
            latent(Tile(0, 0))
            front(Tile(0, 0))
            turn_scores(Tile(0, 0))
            turn_x(Tile(0, 1))
            latent(Tile(0, 1))
            attention_steps(pe, step)

        @block.scalar
        def _(act):
            act.wait_ge(eps_set, 1)
            act.activation(tg[:], gate[:], ACT.Tanh).then_inc(tanh_done, 1)
            act.activation(tg_f[:], gate_f[:], ACT.Tanh).then_inc(tanh_done, 1)

            def deviation(tl):
                act.wait_ge(mv_done, tl.times(1, 1))
                if tl.after(2):
                    act.wait_ge(xn_done, tl.times(1, -1))
                act.activation(rstd[tl.par][:], mv[tl.par][:, 1:2], ACT.Sqrt, bias=eps[:, 0:1]).then_inc(std_done, 1)

            def turned_x(tl):
                act.wait_ge(xT_mm, tl.times(1, 1))
                act.copy(xT[:].rearrange("p c t -> p (c t)"), pa[:, 0:2 * P]).then_inc(xT_done, 1)

            def latent(tl):
                act.wait_ge(qc_mm, tl.times(1, 1))
                if tl.after(1):
                    act.wait_ge(qr_mm, tl.times(4, 0))
                act.copy(qc[:], pa[0:QC, 2 * P:3 * P]).then_inc(qc_done, 1)

            def front(tl):
                for f in range(2):
                    act.wait_ge(qn_mm, tl.times(2, f + 1))
                    if f == 0 and tl.after(1):
                        act.wait_ge(sT_mm, tl.times(2, 0))
                    act.copy(qn[:, 4 * f:4 * f + 4, :], pb[f][:]).then_inc(qn_done, 1)
                for r in range(2):
                    act.wait_ge(sT_mm, tl.times(2, r + 1))
                    if r == 0 and tl.after(1):
                        act.wait_ge(s_mm, tl.times(2, 0))
                    act.copy(sT[:, :, r, :], pc[r][:]).then_inc(sT_done, 1)

            def exponent(tl):
                act.wait_ge(less_done, tl.times(1, 1))
                if tl.after(1):
                    act.wait_ge(p_done, tl.times(2, 0))
                act.activation(e[:], s[:], ACT.Exp, scale=float(HD1 + R1) ** -0.5).then_inc(exp_done, 1)

            def back(tl):
                for f in range(2):
                    act.wait_ge(pT_mm, tl.times(2, f + 1))
                    if f == 0 and tl.after(1):
                        act.wait_ge(u_mm, tl.times(2, 0))
                    act.copy(pT[:, 4 * f:4 * f + 4, :], pd[f][:]).then_inc(pT_done, 1)
                for b in range(2):
                    act.wait_ge(u_mm, tl.times(2, b + 1))
                    if b == 0 and tl.after(1):
                        act.wait_ge(o_mm, tl.times(1, 0))
                    src = pu[:] if b == 0 else pd[0][:].rearrange("p a n -> p (a n)").rearrange("p (h q) -> p h q", q=S)
                    act.copy(u[:, :, b, :], src).then_inc(u_done, 1)

            def step(tl):
                ahead, ahead2 = tl.before(1), tl.before(2)
                if ahead:
                    front(tl.plus(1))
                back(tl)
                if ahead2:
                    turned_x(tl.plus(2))
                if ahead:
                    exponent(tl.plus(1))
                if ahead2:
                    latent(tl.plus(2))
                if tl.before(3):
                    deviation(tl.plus(3))

            deviation(Tile(0, 0))
            turned_x(Tile(0, 0))
            latent(Tile(0, 0))
            front(Tile(0, 0))
            deviation(Tile(0, 1))
            turned_x(Tile(0, 1))
            exponent(Tile(0, 0))
            latent(Tile(0, 1))
            deviation(Tile(1, 0))
            attention_steps(act, step)

        @block.gpsimd
        def _(pool):
            held = Held(pool, pool_passed)

            def gather(tl):
                held.wait_ge(ix_in[tl.par], tl.half * 16 + 16)
                if tl.after(2):
                    held.wait_ge(summed, tl.times(1, -1))
                for k in range(K0):
                    pool.indirect_dma_start(rows[tl.par][:, k, :], None, y_in,
                                            bass.IndirectOffsetOnAxis(ap=ix[tl.par][:, k:k + 1], axis=0),
                                            bounds_check=NONE, oob_is_err=False).then_inc(rows_in[tl.par], 16)

            def keep(tl):
                held.wait_ge(x2_done, tl.times(1, 1))
                if tl.after(2):
                    held.wait_ge(x3_done, tl.times(1, -1))
                pool.tensor_copy(x[tl.par][:], x_new[tl.par][:]).then_inc(kept, 1)

            def keep3(tl):
                held.wait_ge(x3_done, tl.times(1, 1))
                pool.tensor_copy(x3_all[:, bass.ds(tl.t, 1), :].rearrange("p o d -> p (o d)"), x3[tl.par][:]
                                 ).then_inc(x3_kept, 1)

            def softmax(tl):
                held.wait_ge(top_done, tl.times(1, 1))
                heads = s[:].rearrange("p a b k -> p (a b) k")
                pool.tensor_tensor(heads, heads, top[:].unsqueeze(2).to_broadcast([P, H1, S]), ALU.subtract
                                   ).then_inc(less_done, 1)
                held.wait_ge(total_steps, tl.times(2, 2))
                if tl.after(1):
                    held.wait_ge(pT_mm, tl.times(2, 0))
                for f in range(2):
                    pairs = slice(4 * f, 4 * f + 4)
                    pool.tensor_tensor(p[:, pairs].rearrange("p a b k -> p (a b) k"),
                                       e[:, pairs].rearrange("p a b k -> p (a b) k"),
                                       total[:, 8 * f:8 * f + 8].unsqueeze(2).to_broadcast([P, 8, S]), ALU.mult
                                       ).then_inc(p_done, 1)

            def step(tl):
                if tl.after(1):
                    keep3(tl.plus(-1))
                if tl.before(1):
                    keep(tl.plus(1))
                if tl.before(4):
                    gather(tl.plus(4))
                if tl.before(1):
                    softmax(tl.plus(1))

            for t in range(3):
                gather(Tile(t // 2, t % 2))
            keep(Tile(0, 0))
            softmax(Tile(0, 0))
            gather(Tile(1, 1))
            attention_steps(pool, step)
            keep3(Tile(NT // 2 - 1, 1))

        @block.vector
        def _(dve):
            held = Held(dve, gs("b_dve_passed"))
            dve.memset(eps[:], EPS).then_inc(eps_set, 1)
            dve.wait_ge(tanh_done, 2)
            dve.tensor_copy(seg[:], seg_i[:]).then_inc(seg_done, 1)
            dve.wait_ge(seg_done, 1)

            def combine(tl):
                dve.wait_ge(rows_in[tl.par], tl.half * (16 * K0) + 16 * K0)
                if tl.after(1):
                    dve.wait_ge(x2_done, tl.times(1, 0))
                dve.tensor_reduce(moe[:], rows[tl.par][:].rearrange("p k d -> p d k"), AX.X, ALU.add
                                  ).then_inc(summed, 1)
                dve.wait_ge(summed, tl.times(1, 1))
                dve.wait_ge(x_in[tl.par], tl.half * 32 + 32)
                dve.tensor_tensor(moe[:], moe[:], sh[tl.par][:], ALU.add).then_inc(added, 1)
                dve.wait_ge(added, tl.times(1, 1))
                if tl.after(2):
                    dve.wait_ge(kept, tl.times(1, -1))
                    dve.wait_ge(xn_done, tl.times(1, -1))
                dve.scalar_tensor_tensor(x_new[tl.par][:], moe[:], tg_f[:, 0:1], x_old[tl.par][:], ALU.mult, ALU.add
                                         ).then_inc(x2_done, 1)
                held.wait_ge(x2_done, tl.times(1, 1))
                if tl.after(1):
                    held.wait_ge(mv_done, tl.times(1, 0))
                dve.bn_stats(stats[:], x_new[tl.par][:]).then_inc(stats_done, 1)
                held.wait_ge(stats_done, tl.times(1, 1))
                dve.bn_aggr(mv[tl.par][:], stats[:]).then_inc(mv_done, 1)

            def normalise(tl):
                dve.wait_ge(std_done, tl.times(1, 1))
                dve.reciprocal(rstd[tl.par][:], rstd[tl.par][:]).then_inc(rstd_done, 1)
                dve.wait_ge(rstd_done, tl.times(1, 1))
                if tl.after(2):
                    dve.wait_ge(xT_mm, tl.times(1, -1))
                dve.tensor_scalar(xn[tl.par][:], x_new[tl.par][:], mv[tl.par][:, 0:1], rstd[tl.par][:, 0:1],
                                  ALU.subtract, ALU.mult).then_inc(xn_done, 1)

            def front(tl):
                for f in range(4):
                    dve.wait_ge(qr_mm, tl.times(4, f + 1))
                    if f == 0 and tl.after(1):
                        dve.wait_ge(sT_mm, tl.times(2, 0))
                    dve.tensor_tensor(qr[:, 4 * f:4 * f + 4, :].rearrange("p h (b q) -> p (h b) q", q=S),
                                      pb[f % 2][:].rearrange("p h (b q) -> p (h b) q", q=S),
                                      qtab[:].unsqueeze(1).to_broadcast([P, 8, S]), ALU.mult).then_inc(qr_done, 1)
                if tl.after(1):
                    dve.wait_ge(s_done, tl.times(2, 0))
                step = Chain(dve, mask_steps, tl, 6)
                for b in range(2):
                    mine = seg[:, bass.ds(tl.t * 2 + b, 1)]
                    step(dve.tensor_scalar(mask[:, b], keyno[:], mine, 0.0, ALU.subtract, ALU.is_le))
                    step(dve.tensor_scalar(mask2[:, b], keyno[:], mine, float(-BACK), ALU.subtract, ALU.is_ge))
                step(dve.tensor_tensor(mask[:], mask[:], mask2[:], ALU.mult))
                step(dve.tensor_scalar(mask[:], mask[:], 1.0, -NEG, ALU.subtract, ALU.mult))
                step.close()

            def scores(tl):
                if tl.after(1):
                    dve.wait_ge(exp_done, tl.times(1, 0))
                for f in range(2):
                    dve.wait_ge(s_mm, tl.times(2, f + 1))
                    dve.tensor_tensor(s[:, 4 * f:4 * f + 4].rearrange("p a b k -> p a (b k)"), pb[f][:],
                                      mask[:].rearrange("p b k -> p (b k)").unsqueeze(1).to_broadcast([P, 4, P]),
                                      ALU.add).then_inc(s_done, 1)
                dve.wait_ge(s_done, tl.times(2, 2))
                dve.tensor_reduce(top[:], s[:].rearrange("p a b k -> p (a b) k"), AX.X, ALU.max).then_inc(top_done, 1)

            def sums(tl):
                dve.wait_ge(exp_done, tl.times(1, 1))
                if tl.after(1):
                    dve.wait_ge(p_done, tl.times(2, 0))
                dve.tensor_reduce(total[:], e[:].rearrange("p a b k -> p (a b) k"), AX.X, ALU.add
                                  ).then_inc(total_steps, 1)
                dve.wait_ge(total_steps, tl.times(2, 1))
                dve.reciprocal(total[:], total[:]).then_inc(total_steps, 1)

            def add(tl):
                dve.wait_ge(o_mm, tl.times(1, 1))
                dve.wait_ge(kept, tl.times(1, 1))
                if tl.after(2):
                    dve.wait_ge(x3_kept, tl.times(1, -1))
                dve.scalar_tensor_tensor(x3[tl.par][:], pd[1][:].rearrange("p a n -> p (a n)")[:, 0:D], tg[:, 0:1], x[tl.par][:], ALU.mult, ALU.add
                                         ).then_inc(x3_done, 1)

            def step(tl):
                if tl.before(1):
                    front(tl.plus(1))
                if tl.before(2):
                    normalise(tl.plus(2))
                if tl.before(3):
                    combine(tl.plus(3))
                if tl.before(1):
                    scores(tl.plus(1))
                    sums(tl.plus(1))
                add(tl)

            combine(Tile(0, 0))
            normalise(Tile(0, 0))
            front(Tile(0, 0))
            combine(Tile(0, 1))
            normalise(Tile(0, 1))
            scores(Tile(0, 0))
            combine(Tile(1, 0))
            sums(Tile(0, 0))
            attention_steps(dve, step)


E1, TOP1, I1 = 8, 2, 176
EW = E1 + 1
MT = -(-EW * I1 // P)


LAYER1_EXPERTS = {
    "gate": ([P, 1], F32, "g11"), "wr": ([P, KC, E1], F32, "wr1"), "below1": ([P, E1, E1], F32, "below"),
    "spread": ([32, MT, P], BF16, "spread1"), "w1": ([P, KC, MT * P], F32, "w1"), "w2": ([P, MT, D], F32, "w2")}


def layer1_experts(nc, gs, c0, c1, x3_all, out):
    ctx = ExitStack()
    with ctx:
        def sb(name, shape, dt=F32):
            return ctx.enter_context(nc.sbuf_tensor("f_" + name, shape, dt))

        def ps(name, shape, dt=F32):
            return ctx.enter_context(nc.psum_tensor("f_" + name, shape, dt))

        NB = 4
        TB = NT // NB
        ident, identb = c0["ident"], c0["identb"]
        gate, wr, below, spread, w1, w2 = (c1[n] for n in LAYER1_EXPERTS)
        tg = sb("tg", [P, 1])
        xn_all = sb("xn_all", [P, NT, D])
        norm = Normalise(ctx, nc, gs, "f", x3_all, xn_all)
        xT = sb("xT", [P, KC, T])
        logit = sb("logit", [P, NT, E1])
        top = sb("top", [P, NT])
        gt, eq = sb("gt", [P, NT, E1, E1]), sb("eq", [P, NT, E1, E1])
        rank = sb("rank", [P, NT, E1])
        share = sb("share", [P, NT, EW])
        left = sb("left", [P, NT, EW])
        parts = sb("parts", [P, NT, 32], BF16)
        shareT = sb("shareT", [32, T], BF16)
        hT = [sb(f"hT{i}", [P, MT, 512]) for i in range(2)]
        y = [sb(f"y{i}", [P, TB, D]) for i in range(2)]

        tanh_done, logit_mm, less_done, exp_done = gs("f_tanh"), gs("f_logit_mm"), gs("f_less"), gs("f_exp")
        chain, parts_done = gs("f_steps"), gs("f_parts")
        share_mm, share_done = gs("f_share_mm"), gs("f_share")
        up_mm, silu_done = gs("f_up_mm"), gs("f_silu")
        spread_mm, h_done = gs("f_spread_mm"), gs("f_h")
        down_mm, y_done = gs("f_down_mm"), gs("f_y")
        stored = [gs(f"f_stored{i}") for i in range(2)]
        block = ctx.enter_context(nc.Block())
        turn = [ps(f"turn{i}", [P, 4, P]) for i in range(2)]
        turn_pe, turn_act, xT_out, fills = turned_tiles(turn, gs, "f", xn_all, xT)
        ph = [ps(f"ph{i}", [P, 512]) for i in range(2)]
        pw = [ps(f"pw{i}", [P, 512]) for i in range(2)]
        po = [ps(f"po{i}", [P, D]) for i in range(2)]
        @block.tensor
        def _(pe):
            turn_pe(pe, ident[:], norm.done)
            pe.wait_ge(xT_out, fills)
            for t in range(NT):
                for c in range(KC):
                    mm = pe.matmul(po[0][:, t * E1:(t + 1) * E1], xT[:, c, t * P:(t + 1) * P], wr[:, c, :],
                                   start=(c == 0), stop=(c == KC - 1))
            mm.then_inc(logit_mm, 1)

            def up(b, m):
                tokens = bass.ds(b.t * 512, 512)
                if m >= 2 or b.after(1):
                    pe.wait_ge(silu_done, b.times(MT, m - 1))
                for c in range(KC):
                    mm = pe.matmul(ph[(b.par * MT + m) % 2][:], w1[:, c, m * P:(m + 1) * P], xT[:, c, tokens],
                                   start=(c == 0), stop=(c == KC - 1))
                mm.then_inc(up_mm, 1)

            def spread_shares(b, m):
                if m >= 2 or b.after(1):
                    pe.wait_ge(h_done, b.times(MT, m - 1))
                pe.matmul(pw[(b.par * MT + m) % 2][:], spread[:, m, :], shareT[:, bass.ds(b.t * 512, 512)],
                          start=True, stop=True).then_inc(spread_mm, 1)

            def down(b):
                for j in range(TB):
                    pe.wait_ge(h_done, b.times(MT, MT))
                    if j >= 2 or b.after(1):
                        pe.wait_ge(y_done, b.times(TB, j - 1))
                    for m in range(MT):
                        mm = pe.matmul(po[j % 2][:], hT[b.par][:, m, j * P:(j + 1) * P], w2[:, m, :],
                                       start=(m == 0), stop=(m == MT - 1))
                    mm.then_inc(down_mm, 1)

            def step(b, ahead=True):
                if ahead:
                    for m in range(MT):
                        up(b.plus(1), m)
                        spread_shares(b.plus(1), m)
                down(b)

            for m in range(MT):
                up(Tile(0, 0), m)
            pe.wait_ge(parts_done, 1)
            for n in range(2):
                for j in range(8):
                    mm = pe.transpose(pw[n][0:32, :].bitcast(BF16)[:, j * P:(j + 1) * P], parts[:, 8 * n + j, :],
                                      identb[:])
                mm.then_inc(share_mm, 1)
            pe.wait_ge(share_done, 2)
            for m in range(MT):
                spread_shares(Tile(0, 0), m)
            step(Tile(0, 0))
            step(Tile(0, 1))
            step(Tile(1, 0))
            step(Tile(1, 1), ahead=False)

        @block.scalar
        def _(act):
            act.activation(tg[:], gate[:], ACT.Tanh).then_inc(tanh_done, 1)
            norm.on_act(act)
            turn_act(act)
            def silu(b, rows):
                for m in rows:
                    act.wait_ge(up_mm, b.times(MT, m + 1))
                    if m == 0 and b.after(2):
                        act.wait_ge(down_mm, b.times(TB, -TB))
                    act.activation(hT[b.par][:, m, :], ph[(b.par * MT + m) % 2][:], ACT.Silu).then_inc(silu_done, 1)

            def store(b):
                act.wait_ge(y_done, b.times(TB, TB))
                act.dma_start(out[bass.ds(b.t * 512, 512), :].rearrange("(j p) d -> p j d", p=P), y[b.par][:]
                              ).then_inc(stored[b.par], 16)

            silu(Tile(0, 0), range(0, 6))
            act.wait_ge(less_done, 1)
            act.activation(logit[:], logit[:], ACT.Exp).then_inc(exp_done, 1)
            silu(Tile(0, 0), range(6, MT))
            for t in range(1, NB):
                silu(Tile(t // 2, t % 2), range(MT))
                store(Tile((t - 1) // 2, (t - 1) % 2))
            store(Tile((NB - 1) // 2, (NB - 1) % 2))
            for par in range(2):
                act.wait_ge(stored[par], 16 * (NB // 2))

        @block.vector
        def _(dve):
            steps = [0]

            def link(ins):
                steps[0] += 1
                ins.then_inc(chain, 1)
                dve.wait_ge(chain, steps[0])

            norm.on_dve(dve)
            dve.wait_ge(tanh_done, 1)
            dve.wait_ge(logit_mm, 1)
            link(dve.tensor_copy(logit[:].rearrange("p t e -> p (t e)"), po[0][:, 0:NT * E1]))
            full = [P, NT, E1, E1]
            other, own = logit[:].unsqueeze(2).to_broadcast(full), logit[:].unsqueeze(3).to_broadcast(full)
            link(dve.tensor_tensor(gt[:], other, own, ALU.is_gt))
            link(dve.tensor_tensor(eq[:], other, own, ALU.is_equal))
            link(dve.tensor_tensor(eq[:], eq[:], below[:].unsqueeze(1).to_broadcast(full), ALU.mult))
            link(dve.tensor_tensor(gt[:], gt[:], eq[:], ALU.add))
            link(dve.tensor_reduce(rank[:], gt[:], AX.X, ALU.add))
            link(dve.tensor_scalar(rank[:], rank[:], float(TOP1) - 0.5, None, ALU.is_lt))
            link(dve.tensor_reduce(top[:], logit[:], AX.X, ALU.max))
            dve.tensor_tensor(logit[:], logit[:], top[:].unsqueeze(2).to_broadcast([P, NT, E1]), ALU.subtract
                              ).then_inc(less_done, 1)
            dve.wait_ge(exp_done, 1)
            link(dve.tensor_tensor(rank[:], rank[:], logit[:], ALU.mult))
            link(dve.tensor_reduce(top[:], rank[:], AX.X, ALU.add))
            link(dve.reciprocal(top[:], top[:]))
            link(dve.tensor_tensor(share[:, :, 0:E1], rank[:], top[:].unsqueeze(2).to_broadcast([P, NT, E1]),
                                   ALU.mult))
            link(dve.memset(share[:, :, E1:EW], 1.0))
            link(dve.memset(parts[:, :, 3 * EW:32], 0.0))
            link(dve.tensor_copy(parts[:, :, 0:EW], share[:]))
            link(dve.tensor_tensor(left[:], share[:], parts[:, :, 0:EW], ALU.subtract))
            link(dve.tensor_copy(parts[:, :, EW:2 * EW], left[:]))
            dve.tensor_tensor(parts[:, :, 2 * EW:3 * EW], left[:], parts[:, :, EW:2 * EW], ALU.subtract
                              ).then_inc(parts_done, 1)
            for n in range(2):
                dve.wait_ge(share_mm, n + 1)
                dve.tensor_copy(shareT[:, n * 1024:(n + 1) * 1024], pw[n][0:32, :].bitcast(BF16)
                                ).then_inc(share_done, 1)

            def inner(b):
                for m in range(MT):
                    dve.wait_ge(silu_done, b.times(MT, m + 1))
                    dve.wait_ge(spread_mm, b.times(MT, m + 1))
                    dve.tensor_tensor(hT[b.par][:, m, :], hT[b.par][:, m, :], pw[(b.par * MT + m) % 2][:], ALU.mult
                                      ).then_inc(h_done, 1)

            def add(b):
                if b.after(2):
                    dve.wait_ge(stored[b.par], b.half * 16)
                for j in range(TB):
                    dve.wait_ge(down_mm, b.times(TB, j + 1))
                    dve.scalar_tensor_tensor(y[b.par][:, j, :], po[j % 2][:], tg[:, 0:1], x3_all[:, b.t * TB + j, :],
                                             ALU.mult, ALU.add).then_inc(y_done, 1)

            inner(Tile(0, 0))
            for t in range(1, NB):
                inner(Tile(t // 2, t % 2))
                add(Tile((t - 1) // 2, (t - 1) % 2))
            add(Tile((NB - 1) // 2, (NB - 1) % 2))


def program(nc, w, out):
    def scratch(name, shape, dt=F32):
        return nc.dram_tensor(name, shape, dt, kind="Internal").ap()

    rows = out.rearrange("b s d -> (b s) d")
    with ExitStack() as keep:
        def sb(name, shape, dt=F32):
            return keep.enter_context(nc.sbuf_tensor(name, shape, dt))

        x1, xn2 = scratch("d_x1", (T, D)), scratch("d_xn2", (T, D))
        shared, idx, y = scratch("d_shared", (T, D)), scratch("d_idx", (T, K0), U32), scratch("d_y", (NONE + 1, D))
        keysT, keysN = scratch("d_keysT", (T, 2 * P)), scratch("d_keysN", (T, KVC))
        x_all = sb("x_all", [P, NT, D])
        aw, bp = sb("aw", [QC, HP, P]), sb("bp", [P, HP, D])
        slot_ids, slot_w = sb("slot_ids", [P, E0], U32), sb("slot_w", [P, E0])
        c_id, load_id = constants(lambda name, shape, dt: sb("c_" + name, shape, dt), w, IDENTITIES)
        space = sb("constants", [P, 13616])

        first, second = Arena(space), Arena(space)
        c_route, load_route = constants(lambda name, shape, dt: first.take(shape, dt), w, ROUTING)
        c_keys, load_keys = constants(lambda name, shape, dt: first.take(shape, dt), w, LAYER1_KEYS)
        c_keys["ctx"] = first.take([P, NT, D], F32)
        load_keys.append((c_keys["ctx"], w["ctx"].rearrange("(t p) d -> p t d", p=P)))
        c_att1, load_att1 = constants(lambda name, shape, dt: second.take(shape, dt), w, LAYER1_ATTENTION)
        c_ffn1, load_ffn1 = constants(lambda name, shape, dt: second.take(shape, dt), w, LAYER1_EXPERTS)

        with ExitStack() as ctx:
            c_att0, load_att0 = constants(
                lambda name, shape, dt: ctx.enter_context(nc.sbuf_tensor("c_" + name, shape, dt)), w, LAYER0_ATTENTION)
            with stage_semaphores(nc) as gs:
                normalise_input(nc, gs, w["x"], x_all, load_id + load_att0)
            with stage_semaphores(nc) as gs:
                layer0_attention(nc, gs, w["x"], w["ctx"], x1, x_all, c_id, c_att0,
                                 load_route + load_keys)
        with stage_semaphores(nc) as gs:
            routing(nc, gs, x_all, xn2, c_id, c_route, c_keys, w, shared, idx, y[NONE:NONE + 1, :],
                    slot_ids, slot_w, keysT, keysN, aw, bp)
        with stage_semaphores(nc) as gs:
            experts(nc, gs, xn2, w, c_id, slot_ids, slot_w, y, load_att1)
        with stage_semaphores(nc) as gs:
            layer1_attention(nc, gs, c_id, c_att1, x1, shared, idx, y, keysT, keysN, aw, bp, x_all,
                             load_ffn1)
        with stage_semaphores(nc) as gs:
            layer1_experts(nc, gs, c_id, c_ffn1, x_all, rows)


def shape_constants():
    import numpy as np

    f, bf = np.float32, mybir.dt.np(BF16)
    w = {"ident": np.eye(P, dtype=f), "identb": np.eye(P).astype(bf)}
    half = HD0 // 4
    theta = (f(1.0) / f(10000.0) ** (np.arange(0, HD0 // 2, 2, dtype=f) / f(HD0 // 2))).astype(f)
    ang = (np.arange(D, dtype=f)[:, None] * theta[None, :]).astype(f)
    cos = np.concatenate([np.cos(ang)] * 2, 1).reshape(2, P, 1, 2 * half).transpose(1, 0, 2, 3)
    sin = np.concatenate([-np.sin(ang), np.sin(ang)], 1).reshape(2, P, 1, 2 * half).transpose(1, 0, 2, 3)
    for name, a in (("cos4", cos), ("sin4", sin)):
        a = np.broadcast_to(a[:, None], (P, 2, 2, BH, 2 * half))
        w[name] = np.ascontiguousarray(a.reshape(P, 4 * BH, 2 * half), dtype=f)
    j = np.arange(R1 // 2, dtype=f)
    inv = (f(1.0) / f(10000.0) ** (j / f(R1 // 2))).astype(f)
    ang = (np.arange(S, dtype=f)[:, None] * inv).astype(f)
    c, s_ = np.cos(ang).T, np.sin(ang).T
    w["qtab"] = np.concatenate([c, c, -s_, s_]).astype(f)
    w["kcos"] = np.concatenate([c] * 4).astype(f)
    w["ksin"] = np.concatenate([-s_, s_] * 2).astype(f)
    w["keyno"] = np.broadcast_to(np.arange(S, dtype=f), (P, S))
    spread = np.zeros((32, MT * P), bf)
    for e in range(EW):
        for part in range(3):
            spread[part * EW + e, e * I1:(e + 1) * I1] = 1
    w["spread1"] = spread.reshape(32, MT, P)
    w["earlier"] = np.triu(np.ones((P, P)), 1).astype(bf)
    w["onesb"] = np.ones((P, P), bf)
    w["below"] = np.broadcast_to(np.tril(np.ones((G0, G0), f), -1), (P, G0, G0))
    w["slot1"] = np.broadcast_to(np.arange(E0, dtype=f) * CAP + 1, (P, E0))
    w["iota"] = np.broadcast_to(np.arange(CAP, dtype=f), (P, CAP))
    w["tok"] = np.arange(T, dtype=f).reshape(NT, P).T
    return w


def laid_out(i):
    import numpy as np
    f = np.float32

    def twice(a):
        out = np.zeros((P, P), f)
        out[:S, :S] = out[S:, S:] = a
        return out

    w = shape_constants()
    w["x"] = i["x"].reshape(T, D)
    w["ctx"] = i["ctx_2048"].reshape(T, D)
    w["wq0"] = twice(i["L0_xattn_Wq"].T)
    w["wkv0"] = np.concatenate([twice(i["L0_xattn_Wk"].T), twice(i["L0_xattn_Wv"].T)], 1)
    w["wo0"] = twice(i["L0_xattn_Wo"].T)
    w["bias0"] = np.broadcast_to(np.concatenate([i["L0_xattn_" + n] for n in ("bq", "bq", "bk", "bk", "bv", "bv")]),
                                 (P, 3 * P))
    w["bo0"] = np.tile(i["L0_xattn_bo"], 2)[:, None]
    def chunks(a):
        return a.reshape(KC, P, a.shape[-1]).transpose(1, 0, 2)

    w["rw"] = chunks(i["L0_ffn_router_weight"].T)
    w["ebias"] = np.broadcast_to(i["L0_ffn_e_bias"], (P, E0))
    w["shg"], w["shu"], w["shd"] = chunks(i["L0_ffn_sh_gate"]), chunks(i["L0_ffn_sh_up"]), i["L0_ffn_sh_down"]
    gu = np.stack([i["L0_ffn_w_gate"], i["L0_ffn_w_up"]], 2)
    w["gu"] = gu.reshape(E0, KC, P, 2, I0).transpose(0, 2, 1, 3, 4)
    w["dn"] = i["L0_ffn_w_down"]

    wkvc, wkr = i["L1_xattn_W_kvc"], i["L1_xattn_W_kr"]

    def swapped(a):
        return np.concatenate([a[..., R1 // 2:], a[..., :R1 // 2]], -1)

    w["wkvc2"] = chunks(np.concatenate([wkvc, wkvc], 1))
    w["wkr"] = np.stack([np.concatenate([a, a], 1) for a in (wkr, swapped(wkr))], 1)
    for name, key in (("wuqT", "W_uq"), ("wukT", "W_uk"), ("wuvT", "W_uv")):
        a = i["L1_xattn_" + key]
        w[name] = a.reshape(a.shape[0], H1, HD1).transpose(2, 1, 0)
    w["wo1"] = i["L1_xattn_W_o"].reshape(H1, HD1, D).transpose(1, 0, 2)
    w["wdq"] = chunks(i["L1_xattn_W_dq"])
    wqr = i["L1_xattn_W_qr"].reshape(QC, H1, R1)
    w["wqr"] = np.concatenate([wqr, swapped(wqr)], 2)
    w["seg"] = np.tile(i["itok_BxS_0_1023"].reshape(B, S).T, (2, 1))
    w["wr1"] = chunks(i["L1_ffn_w_router"])
    w1 = np.zeros((D, MT * P), f)
    w2 = np.zeros((MT * P, D), f)
    w1[:, :EW * I1] = np.concatenate([*i["L1_ffn_w1"], i["L1_ffn_w_shared1"]], 1)
    w2[:EW * I1] = np.concatenate([*i["L1_ffn_w2"], i["L1_ffn_w_shared2"]], 0)
    w["w1"], w["w2"] = chunks(w1), w2.reshape(MT, P, D).transpose(1, 0, 2)
    for l in range(2):
        for n, g in (("0", "g_xattn"), ("1", "g_ffn")):
            w[f"g{l}{n}"] = np.broadcast_to(i[g][l:l + 1, None], (P, 1))
    return {k: np.ascontiguousarray(a) for k, a in w.items()}


def kernel(**inputs):
    import numpy as np
    import concourse.bacc as bacc
    from concourse.bass_utils import run_bass_kernel_spmd as run

    nc = bacc.Bacc("TRN2", target_bir_lowering=False, num_devices=1)
    arrays = laid_out({k: np.asarray(v) for k, v in inputs.items()})
    w = {k: nc.dram_tensor("in_" + k, a.shape, mybir.dt.from_np(a.dtype), kind="ExternalInput").ap()
         for k, a in arrays.items()}
    out = nc.dram_tensor("out", (B, S, D), F32, kind="ExternalOutput").ap()
    program(nc, w, out)
    r = run(nc, [{"in_" + k: a for k, a in arrays.items()}], core_ids=[0])
    return r.results[0]["out"]
```
